# Optimizing a Trainium2 kernel written in Bass

```python
import numpy as np
import jax
import jax.numpy as jnp

def _softmax(x, axis=-1):
    return jax.nn.softmax(x, axis=axis)
def _gelu(x):
    return jax.nn.gelu(x, approximate=True)
def _silu(x):
    return jax.nn.silu(x)
def _sigmoid(x):
    return jax.nn.sigmoid(x)
def _layernorm(x, axis=-1, eps=1e-5):
    m = jnp.mean(x, axis=axis, keepdims=True)
    v = jnp.var(x, axis=axis, keepdims=True)
    return (x - m) / jnp.sqrt(v + eps)
def _scatter_add(tgt, idx, src, axis=0):
    return tgt.at[idx].add(src)
def _segment_sum(src, seg, n):
    return jax.ops.segment_sum(src, seg, n)

kernel_name = 'mk_conv_preact_d4_conv_nhwc128_7b5b6c'

def setup_inputs(seed: int = 0):
    np.random.seed(seed)
    _w = jnp.asarray
    def _rec_inputs():
        import jax
        import jax.numpy as jnp
        _gk = jax.random.key(seed)
        x = -0.000929 + 1 * jax.random.normal(jax.random.fold_in(_gk, 1), (2, 32, 128, 128), jnp.float32)
        return x
    x = _rec_inputs()
    def _L0_conv_setup():
        import jax, jax.numpy as jnp
        import numpy as np
        EPS = 1e-05
        N_HEADS = 32
        TEMPERATURE = 1.0

        def _inorm(x, g, b):
            m = jnp.mean(x, axis=(-2, -1), keepdims=True)
            v = jnp.var(x, axis=(-2, -1), keepdims=True)
            return (x - m) * jax.lax.rsqrt(v + EPS) * g + b

        def _resample(x, out_hw):
            H, W = x.shape[-2:]
            Ho, Wo = out_hw
            if (H, W) == (Ho, Wo):
                return x
            xf = jnp.fft.rfft2(x, norm='forward')
            kh = min(H, Ho) // 2
            kw = min(W // 2 + 1, Wo // 2 + 1)
            of = jnp.zeros(x.shape[:-2] + (Ho, Wo // 2 + 1), dtype=xf.dtype)
            of = of.at[..., :kh, :kw].set(xf[..., :kh, :kw])
            of = of.at[..., -kh:, :kw].set(xf[..., -kh:, :kw])
            return jnp.fft.irfft2(of, s=(Ho, Wo), norm='forward')

        def _spec_conv(x, w, out_hw):
            m1, m2 = (w.shape[3], w.shape[4])
            Ho, Wo = out_hw
            wc = w[..., 0] + 1j * w[..., 1]
            xf = jnp.fft.rfft2(x, norm='forward')
            top = jnp.einsum('bimn,iomn->bomn', xf[:, :, :m1, :m2], wc[0])
            bot = jnp.einsum('bimn,iomn->bomn', xf[:, :, -m1:, :m2], wc[1])
            of = jnp.zeros((x.shape[0], w.shape[2], Ho, Wo // 2 + 1), dtype=xf.dtype)
            of = of.at[:, :, :m1, :m2].set(top)
            of = of.at[:, :, -m1:, :m2].set(bot)
            return jnp.fft.irfft2(of, s=(Ho, Wo), norm='forward')

        def _fno_layer(x, w, ws, bs, out_hw, norm_gb=None, act=False):
            skip = jnp.einsum('bchw,oc->bohw', x, ws) + bs[None, :, None, None]
            skip = _resample(skip, out_hw)
            fno = _spec_conv(x, w, out_hw)
            if norm_gb is not None:
                fno = _inorm(fno, norm_gb[0], norm_gb[1])
            y = fno + skip
            if act:
                y = jax.nn.gelu(y, approximate=False)
            return y

        def _forward(x, wK, wKs, bKs, wQ, wQs, bQs, wV, wVs, bVs, wP, wPs, bPs, wM0, wM0s, bM0s, wM1, wM1s, bM1s, norm_g, norm_b):
            B, T, H, W = x.shape
            xa = x.reshape(B * T, 1, H, W)
            xa_n = _inorm(xa, norm_g[0], norm_b[0])
            k = _fno_layer(xa_n, wK, wKs, bKs, (H // 2, W // 2))
            q = _fno_layer(xa_n, wQ, wQs, bQs, (H // 2, W // 2))
            v = _fno_layer(xa_n, wV, wVs, bVs, (H, W))

            def to_seq(z):
                h, w = z.shape[-2:]
                z = z.reshape(B, T, N_HEADS, 1, h, w).transpose(0, 2, 1, 3, 4, 5)
                return z.reshape(B, N_HEADS, T, h * w)
            qs, ks, vs = (to_seq(q), to_seq(k), to_seq(v))
            scores = jnp.einsum('bhtd,bhsd->bhts', qs, ks) / (np.sqrt(ks.shape[-1]).astype(np.float32) * TEMPERATURE)
            attn_w = jax.nn.softmax(scores, axis=-1)
            out = jnp.einsum('bhts,bhsd->bhtd', attn_w, vs)
            out = out.reshape(B, N_HEADS, T, 1, H, W).transpose(0, 2, 1, 3, 4, 5)
            out = out.reshape(B * T, N_HEADS, H, W)
            projd = _fno_layer(out, wP, wPs, bPs, (H, W))
            attention = _inorm(projd + xa, norm_g[1], norm_b[1])
            an = _inorm(attention, norm_g[2], norm_b[2])
            m = _fno_layer(an, wM0, wM0s, bM0s, (H, W), (norm_g[3], norm_b[3]), act=True)
            m = _fno_layer(m, wM1, wM1s, bM1s, (H, W), (norm_g[4], norm_b[4]), act=False)
            output = _inorm(m, norm_g[5], norm_b[5]) + attention
            return output.reshape(B, T, H, W)
        key = jax.random.key(seed)
        ks = jax.random.split(key, 16)
        B, T, H, W, heads = (2, 32, 128, 128, 32)

        def rn(k, shape, s=1.0):
            return jax.random.normal(k, shape, jnp.float32) * s
        inp = {'x': rn(ks[0], (B, T, H, W))}
        for i, nm in enumerate(['K', 'Q', 'V']):
            inp['w' + nm] = rn(ks[1 + 3 * i], (2, 1, heads, 16, 16, 2), 1.0 / heads)
            inp['w' + nm + 's'] = rn(ks[2 + 3 * i], (heads, 1), 1.0)
            inp['b' + nm + 's'] = jnp.zeros((heads,), jnp.float32)
        inp['wP'] = rn(ks[10], (2, heads, 1, 32, 32, 2), 1.0 / heads)
        inp['wPs'] = rn(ks[11], (1, heads), 1.0 / heads)
        inp['bPs'] = jnp.zeros((1,), jnp.float32)
        inp['wM0'] = rn(ks[12], (2, 1, 1, 32, 32, 2), 1.0)
        inp['wM0s'] = rn(ks[13], (1, 1), 1.0)
        inp['bM0s'] = jnp.zeros((1,), jnp.float32)
        inp['wM1'] = rn(ks[14], (2, 1, 1, 32, 32, 2), 1.0)
        inp['wM1s'] = rn(ks[15], (1, 1), 1.0)
        inp['bM1s'] = jnp.zeros((1,), jnp.float32)
        inp['norm_g'] = jnp.ones((6,), jnp.float32)
        inp['norm_b'] = jnp.zeros((6,), jnp.float32)
        return inp
    _L0_conv_all = _L0_conv_setup()
    _L0_conv_in = {k: v for k, v in _L0_conv_all.items() if k in ('wK', 'wKs', 'bKs', 'wQ', 'wQs', 'bQs', 'wV', 'wVs', 'bVs', 'wP', 'wPs', 'bPs', 'wM0', 'wM0s', 'bM0s', 'wM1', 'wM1s', 'bM1s', 'norm_g', 'norm_b', )}
    del _L0_conv_all

    def _L1_conv_setup():
        import jax, jax.numpy as jnp
        import numpy as np
        N_HEADS = 32
        EPS = 1e-05

        def _inorm(x, w=None, b=None):
            mu = jnp.mean(x, axis=(-2, -1), keepdims=True)
            var = jnp.var(x, axis=(-2, -1), keepdims=True)
            y = (x - mu) * jax.lax.rsqrt(var + EPS)
            if w is not None:
                y = y * w[None, :, None, None] + b[None, :, None, None]
            return y

        def _fourier_resize(x, oh, ow):
            B, C, H, W = x.shape
            if (oh, ow) == (H, W):
                return x
            X = jnp.fft.rfft2(x, norm='forward')
            kh = min(H, oh) // 2
            kw = min(W // 2 + 1, ow // 2 + 1)
            out = jnp.zeros((B, C, oh, ow // 2 + 1), dtype=X.dtype)
            out = out.at[:, :, :kh, :kw].set(X[:, :, :kh, :kw])
            out = out.at[:, :, -kh:, :kw].set(X[:, :, -kh:, :kw])
            return jnp.fft.irfft2(out, s=(oh, ow), norm='forward')

        def _spectral_conv(x, w2, oh, ow):
            w = w2[..., 0] + 1j * w2[..., 1]
            mh = w.shape[2] // 2
            mw = w.shape[3]
            X = jnp.fft.rfft2(x, norm='forward')
            Xk = jnp.concatenate([X[:, :, :mh, :mw], X[:, :, -mh:, :mw]], axis=2)
            Yk = jnp.einsum('bixy,ioxy->boxy', Xk, w)
            B = x.shape[0]
            O = w.shape[1]
            out = jnp.zeros((B, O, oh, ow // 2 + 1), dtype=Yk.dtype)
            out = out.at[:, :, :mh, :mw].set(Yk[:, :, :mh])
            out = out.at[:, :, -mh:, :mw].set(Yk[:, :, mh:])
            return jnp.fft.irfft2(out, s=(oh, ow), norm='forward')

        def _fno_layer(x, conv_w, skip_w, oh, ow, inner_norm=False, act=False):
            skip = jnp.einsum('bixy,oi->boxy', x, skip_w)
            skip = _fourier_resize(skip, oh, ow)
            xf = _spectral_conv(x, conv_w, oh, ow)
            if inner_norm:
                xf = _inorm(xf)
            y = xf + skip
            if act:
                y = jax.nn.gelu(y, approximate=False)
            return y
        key = jax.random.key(seed)
        ks = jax.random.split(key, 16)
        B, T, H, W = (4, 32, 128, 128)

        def cw(k, ci, co, mh2, mw):
            scale = 1.0 / (ci * co)
            return scale * jax.random.normal(k, (ci, co, mh2, mw, 2), jnp.float32)

        def sw(k, co, ci):
            return jax.random.normal(k, (co, ci), jnp.float32) / np.float32(np.sqrt(ci))
        one = jnp.ones((1,), jnp.float32)
        zero = jnp.zeros((1,), jnp.float32)
        return dict(x=jax.random.normal(ks[0], (B, T, H, W), jnp.float32), norm1_w=one, norm1_b=zero, Kcw=cw(ks[1], 1, N_HEADS, 32, 17), Ksw=sw(ks[2], N_HEADS, 1), Qcw=cw(ks[3], 1, N_HEADS, 32, 17), Qsw=sw(ks[4], N_HEADS, 1), Vcw=cw(ks[5], 1, N_HEADS, 32, 17), Vsw=sw(ks[6], N_HEADS, 1), Pcw=cw(ks[7], N_HEADS, 1, 64, 33), Psw=sw(ks[8], 1, N_HEADS), attn_w=one, attn_b=zero, norm2_w=one, norm2_b=zero, m0cw=cw(ks[9], 1, 1, 64, 33), m0sw=sw(ks[10], 1, 1), m1cw=cw(ks[11], 1, 1, 64, 33), m1sw=sw(ks[12], 1, 1), mon_w=one, mon_b=zero)
    _L1_conv_all = _L1_conv_setup()
    _L1_conv_in = {k: v for k, v in _L1_conv_all.items() if k in ('norm1_w', 'norm1_b', 'Kcw', 'Ksw', 'Qcw', 'Qsw', 'Vcw', 'Vsw', 'Pcw', 'Psw', 'attn_w', 'attn_b', 'norm2_w', 'norm2_b', 'm0cw', 'm0sw', 'm1cw', 'm1sw', 'mon_w', 'mon_b', )}
    del _L1_conv_all

    def _L2_conv_setup():
        import jax, jax.numpy as jnp
        import numpy as np
        IN_SIZE = 128
        OUT_SIZE = 128
        FILTER_SIZE = 6
        UP_FACTOR = 2
        DN_FACTOR = 2
        SLOPE = 0.2
        GAIN = float(np.sqrt(2.0))

        def _firwin_kaiser(numtaps, cutoff, width, fs):
            nyq = 0.5 * fs
            atten = 2.285 * (numtaps - 1) * np.pi * (width / nyq) + 7.95
            if atten > 50:
                beta = 0.1102 * (atten - 8.7)
            elif atten > 21:
                beta = 0.5842 * (atten - 21) ** 0.4 + 0.07886 * (atten - 21)
            else:
                beta = 0.0
            c = cutoff / nyq
            alpha = 0.5 * (numtaps - 1)
            m = np.arange(numtaps) - alpha
            h = c * np.sinc(c * m)
            h *= np.kaiser(numtaps, beta)
            h /= h.sum()
            return h.astype(np.float32)

        def _make_filter(size, factor):
            taps = FILTER_SIZE * factor
            f1d = _firwin_kaiser(taps, size / 2.0001, size, size)
            f2d = np.outer(f1d, f1d)[None, None]
            return jnp.asarray(f2d, dtype=jnp.float32)

        def _conv_same(x, f):
            k = f.shape[-1]
            pl = (k - 1) // 2
            pr = k - 1 - pl
            return jax.lax.conv_general_dilated(x, f, (1, 1), [(pl, pr), (pl, pr)])
        key = jax.random.key(seed)
        x = jax.random.normal(key, (16, 32, IN_SIZE, IN_SIZE), dtype=jnp.float32)
        bias = jnp.zeros((1, 32, 1, 1), dtype=jnp.float32)
        up_filter = _make_filter(IN_SIZE, UP_FACTOR)
        dn_filter = _make_filter(OUT_SIZE, DN_FACTOR)
        return {'x': x, 'bias': bias, 'up_filter': up_filter, 'dn_filter': dn_filter}
    _L2_conv_all = _L2_conv_setup()
    _L2_conv_in = {k: v for k, v in _L2_conv_all.items() if k in ('bias', 'up_filter', 'dn_filter', )}
    del _L2_conv_all

    def _L3_conv_setup():
        import jax, jax.numpy as jnp
        import numpy as np
        B, CIN, COUT, H, W = (8, 32, 32, 128, 128)

        def rfftshift(x):
            return jnp.conj(jnp.flip(jnp.fft.fftshift(x, axes=-2), axis=-1))

        def irfftshift(x):
            return jnp.conj(jnp.flip(jnp.fft.ifftshift(x, axes=-2), axis=-1))

        def symmetric_padding(xf_old, im_shape_old, im_shape_new):
            Ho, Wo = im_shape_old
            Hn, Wn = im_shape_new
            ft_h_old = Ho + (1 - Ho % 2)
            ft_w_old = Wo // 2 + 1
            ft_h_new = Hn + (1 - Hn % 2)
            ft_w_new = Wn // 2 + 1
            nlead = xf_old.ndim - 2
            xf = jnp.pad(xf_old, [(0, 0)] * nlead + [(0, ft_h_old - Ho), (0, 0)])
            if Ho % 2 == 0:
                xf = xf.at[..., 0, :].multiply(0.5)
                xf = xf.at[..., -1, :].set(xf[..., 0, :])
            if Wo % 2 == 0:
                xf = xf.at[..., :, 0].multiply(0.5)
            ph = (ft_h_new - ft_h_old) // 2
            pw = ft_w_new - ft_w_old
            xf = jnp.pad(xf, [(0, 0)] * nlead + [(ph, ph), (pw, 0)])
            if Hn % 2 == 0:
                xf = xf.at[..., 0, :].multiply(2.0)
            if Wn % 2 == 0:
                xf = xf.at[..., :, 0].multiply(2.0)
            return xf[..., :Hn, :]
        key = jax.random.key(seed)
        k1, k2, k3 = jax.random.split(key, 3)
        x = jax.random.normal(k1, (B, CIN, H, W), dtype=jnp.float32)
        weight_real = jax.random.uniform(k2, (CIN, COUT, H, W // 2 + 1), dtype=jnp.float32)
        weight_imag = jax.random.uniform(k3, (CIN, COUT, H, W // 2 + 1), dtype=jnp.float32)
        weight_imag = weight_imag.at[:, :, 0, 0].set(0.0)
        return {'x': x, 'weight_real': weight_real, 'weight_imag': weight_imag}
    _L3_conv_all = _L3_conv_setup()
    _L3_conv_in = {k: v for k, v in _L3_conv_all.items() if k in ('weight_real', 'weight_imag', )}
    del _L3_conv_all

    return {
        "x": x,
        "L0_conv_wK": _L0_conv_in["wK"],
        "L0_conv_wKs": _L0_conv_in["wKs"],
        "L0_conv_bKs": _L0_conv_in["bKs"],
        "L0_conv_wQ": _L0_conv_in["wQ"],
        "L0_conv_wQs": _L0_conv_in["wQs"],
        "L0_conv_bQs": _L0_conv_in["bQs"],
        "L0_conv_wV": _L0_conv_in["wV"],
        "L0_conv_wVs": _L0_conv_in["wVs"],
        "L0_conv_bVs": _L0_conv_in["bVs"],
        "L0_conv_wP": _L0_conv_in["wP"],
        "L0_conv_wPs": _L0_conv_in["wPs"],
        "L0_conv_bPs": _L0_conv_in["bPs"],
        "L0_conv_wM0": _L0_conv_in["wM0"],
        "L0_conv_wM0s": _L0_conv_in["wM0s"],
        "L0_conv_bM0s": _L0_conv_in["bM0s"],
        "L0_conv_wM1": _L0_conv_in["wM1"],
        "L0_conv_wM1s": _L0_conv_in["wM1s"],
        "L0_conv_bM1s": _L0_conv_in["bM1s"],
        "L0_conv_norm_g": _L0_conv_in["norm_g"],
        "L0_conv_norm_b": _L0_conv_in["norm_b"],
        "L1_conv_norm1_w": _L1_conv_in["norm1_w"],
        "L1_conv_norm1_b": _L1_conv_in["norm1_b"],
        "L1_conv_Kcw": _L1_conv_in["Kcw"],
        "L1_conv_Ksw": _L1_conv_in["Ksw"],
        "L1_conv_Qcw": _L1_conv_in["Qcw"],
        "L1_conv_Qsw": _L1_conv_in["Qsw"],
        "L1_conv_Vcw": _L1_conv_in["Vcw"],
        "L1_conv_Vsw": _L1_conv_in["Vsw"],
        "L1_conv_Pcw": _L1_conv_in["Pcw"],
        "L1_conv_Psw": _L1_conv_in["Psw"],
        "L1_conv_attn_w": _L1_conv_in["attn_w"],
        "L1_conv_attn_b": _L1_conv_in["attn_b"],
        "L1_conv_norm2_w": _L1_conv_in["norm2_w"],
        "L1_conv_norm2_b": _L1_conv_in["norm2_b"],
        "L1_conv_m0cw": _L1_conv_in["m0cw"],
        "L1_conv_m0sw": _L1_conv_in["m0sw"],
        "L1_conv_m1cw": _L1_conv_in["m1cw"],
        "L1_conv_m1sw": _L1_conv_in["m1sw"],
        "L1_conv_mon_w": _L1_conv_in["mon_w"],
        "L1_conv_mon_b": _L1_conv_in["mon_b"],
        "L2_conv_bias": _L2_conv_in["bias"],
        "L2_conv_up_filter": _L2_conv_in["up_filter"],
        "L2_conv_dn_filter": _L2_conv_in["dn_filter"],
        "L3_conv_weight_real": _L3_conv_in["weight_real"],
        "L3_conv_weight_imag": _L3_conv_in["weight_imag"],
    }

def reference(x, L0_conv_wK, L0_conv_wKs, L0_conv_bKs, L0_conv_wQ, L0_conv_wQs, L0_conv_bQs, L0_conv_wV, L0_conv_wVs, L0_conv_bVs, L0_conv_wP, L0_conv_wPs, L0_conv_bPs, L0_conv_wM0, L0_conv_wM0s, L0_conv_bM0s, L0_conv_wM1, L0_conv_wM1s, L0_conv_bM1s, L0_conv_norm_g, L0_conv_norm_b, L1_conv_norm1_w, L1_conv_norm1_b, L1_conv_Kcw, L1_conv_Ksw, L1_conv_Qcw, L1_conv_Qsw, L1_conv_Vcw, L1_conv_Vsw, L1_conv_Pcw, L1_conv_Psw, L1_conv_attn_w, L1_conv_attn_b, L1_conv_norm2_w, L1_conv_norm2_b, L1_conv_m0cw, L1_conv_m0sw, L1_conv_m1cw, L1_conv_m1sw, L1_conv_mon_w, L1_conv_mon_b, L2_conv_bias, L2_conv_up_filter, L2_conv_dn_filter, L3_conv_weight_real, L3_conv_weight_imag):
    import jax
    import jax.numpy as jnp
    def _L0_conv_ref(x, wK, wKs, bKs, wQ, wQs, bQs, wV, wVs, bVs, wP, wPs, bPs, wM0, wM0s, bM0s, wM1, wM1s, bM1s, norm_g, norm_b):
        import jax, jax.numpy as jnp
        import numpy as np
        EPS = 1e-05
        N_HEADS = 32
        TEMPERATURE = 1.0

        def _inorm(x, g, b):
            m = jnp.mean(x, axis=(-2, -1), keepdims=True)
            v = jnp.var(x, axis=(-2, -1), keepdims=True)
            return (x - m) * jax.lax.rsqrt(v + EPS) * g + b

        def _resample(x, out_hw):
            H, W = x.shape[-2:]
            Ho, Wo = out_hw
            if (H, W) == (Ho, Wo):
                return x
            xf = jnp.fft.rfft2(x, norm='forward')
            kh = min(H, Ho) // 2
            kw = min(W // 2 + 1, Wo // 2 + 1)
            of = jnp.zeros(x.shape[:-2] + (Ho, Wo // 2 + 1), dtype=xf.dtype)
            of = of.at[..., :kh, :kw].set(xf[..., :kh, :kw])
            of = of.at[..., -kh:, :kw].set(xf[..., -kh:, :kw])
            return jnp.fft.irfft2(of, s=(Ho, Wo), norm='forward')

        def _spec_conv(x, w, out_hw):
            m1, m2 = (w.shape[3], w.shape[4])
            Ho, Wo = out_hw
            wc = w[..., 0] + 1j * w[..., 1]
            xf = jnp.fft.rfft2(x, norm='forward')
            top = jnp.einsum('bimn,iomn->bomn', xf[:, :, :m1, :m2], wc[0])
            bot = jnp.einsum('bimn,iomn->bomn', xf[:, :, -m1:, :m2], wc[1])
            of = jnp.zeros((x.shape[0], w.shape[2], Ho, Wo // 2 + 1), dtype=xf.dtype)
            of = of.at[:, :, :m1, :m2].set(top)
            of = of.at[:, :, -m1:, :m2].set(bot)
            return jnp.fft.irfft2(of, s=(Ho, Wo), norm='forward')

        def _fno_layer(x, w, ws, bs, out_hw, norm_gb=None, act=False):
            skip = jnp.einsum('bchw,oc->bohw', x, ws) + bs[None, :, None, None]
            skip = _resample(skip, out_hw)
            fno = _spec_conv(x, w, out_hw)
            if norm_gb is not None:
                fno = _inorm(fno, norm_gb[0], norm_gb[1])
            y = fno + skip
            if act:
                y = jax.nn.gelu(y, approximate=False)
            return y

        def _forward(x, wK, wKs, bKs, wQ, wQs, bQs, wV, wVs, bVs, wP, wPs, bPs, wM0, wM0s, bM0s, wM1, wM1s, bM1s, norm_g, norm_b):
            B, T, H, W = x.shape
            xa = x.reshape(B * T, 1, H, W)
            xa_n = _inorm(xa, norm_g[0], norm_b[0])
            k = _fno_layer(xa_n, wK, wKs, bKs, (H // 2, W // 2))
            q = _fno_layer(xa_n, wQ, wQs, bQs, (H // 2, W // 2))
            v = _fno_layer(xa_n, wV, wVs, bVs, (H, W))

            def to_seq(z):
                h, w = z.shape[-2:]
                z = z.reshape(B, T, N_HEADS, 1, h, w).transpose(0, 2, 1, 3, 4, 5)
                return z.reshape(B, N_HEADS, T, h * w)
            qs, ks, vs = (to_seq(q), to_seq(k), to_seq(v))
            scores = jnp.einsum('bhtd,bhsd->bhts', qs, ks) / (np.sqrt(ks.shape[-1]).astype(np.float32) * TEMPERATURE)
            attn_w = jax.nn.softmax(scores, axis=-1)
            out = jnp.einsum('bhts,bhsd->bhtd', attn_w, vs)
            out = out.reshape(B, N_HEADS, T, 1, H, W).transpose(0, 2, 1, 3, 4, 5)
            out = out.reshape(B * T, N_HEADS, H, W)
            projd = _fno_layer(out, wP, wPs, bPs, (H, W))
            attention = _inorm(projd + xa, norm_g[1], norm_b[1])
            an = _inorm(attention, norm_g[2], norm_b[2])
            m = _fno_layer(an, wM0, wM0s, bM0s, (H, W), (norm_g[3], norm_b[3]), act=True)
            m = _fno_layer(m, wM1, wM1s, bM1s, (H, W), (norm_g[4], norm_b[4]), act=False)
            output = _inorm(m, norm_g[5], norm_b[5]) + attention
            return output.reshape(B, T, H, W)
        return _forward(x, wK, wKs, bKs, wQ, wQs, bQs, wV, wVs, bVs, wP, wPs, bPs, wM0, wM0s, bM0s, wM1, wM1s, bM1s, norm_g, norm_b)

    def _L1_conv_ref(x, norm1_w, norm1_b, Kcw, Ksw, Qcw, Qsw, Vcw, Vsw, Pcw, Psw, attn_w, attn_b, norm2_w, norm2_b, m0cw, m0sw, m1cw, m1sw, mon_w, mon_b):
        import jax, jax.numpy as jnp
        import numpy as np
        N_HEADS = 32
        EPS = 1e-05

        def _inorm(x, w=None, b=None):
            mu = jnp.mean(x, axis=(-2, -1), keepdims=True)
            var = jnp.var(x, axis=(-2, -1), keepdims=True)
            y = (x - mu) * jax.lax.rsqrt(var + EPS)
            if w is not None:
                y = y * w[None, :, None, None] + b[None, :, None, None]
            return y

        def _fourier_resize(x, oh, ow):
            B, C, H, W = x.shape
            if (oh, ow) == (H, W):
                return x
            X = jnp.fft.rfft2(x, norm='forward')
            kh = min(H, oh) // 2
            kw = min(W // 2 + 1, ow // 2 + 1)
            out = jnp.zeros((B, C, oh, ow // 2 + 1), dtype=X.dtype)
            out = out.at[:, :, :kh, :kw].set(X[:, :, :kh, :kw])
            out = out.at[:, :, -kh:, :kw].set(X[:, :, -kh:, :kw])
            return jnp.fft.irfft2(out, s=(oh, ow), norm='forward')

        def _spectral_conv(x, w2, oh, ow):
            w = w2[..., 0] + 1j * w2[..., 1]
            mh = w.shape[2] // 2
            mw = w.shape[3]
            X = jnp.fft.rfft2(x, norm='forward')
            Xk = jnp.concatenate([X[:, :, :mh, :mw], X[:, :, -mh:, :mw]], axis=2)
            Yk = jnp.einsum('bixy,ioxy->boxy', Xk, w)
            B = x.shape[0]
            O = w.shape[1]
            out = jnp.zeros((B, O, oh, ow // 2 + 1), dtype=Yk.dtype)
            out = out.at[:, :, :mh, :mw].set(Yk[:, :, :mh])
            out = out.at[:, :, -mh:, :mw].set(Yk[:, :, mh:])
            return jnp.fft.irfft2(out, s=(oh, ow), norm='forward')

        def _fno_layer(x, conv_w, skip_w, oh, ow, inner_norm=False, act=False):
            skip = jnp.einsum('bixy,oi->boxy', x, skip_w)
            skip = _fourier_resize(skip, oh, ow)
            xf = _spectral_conv(x, conv_w, oh, ow)
            if inner_norm:
                xf = _inorm(xf)
            y = xf + skip
            if act:
                y = jax.nn.gelu(y, approximate=False)
            return y
        B, T, H, W = x.shape
        Hs, Ws = (H // 2, W // 2)
        temperature = 1.0
        xa = x.reshape(B * T, 1, H, W)
        xn = _inorm(xa, norm1_w, norm1_b)
        k = _fno_layer(xn, Kcw, Ksw, Hs, Ws)
        q = _fno_layer(xn, Qcw, Qsw, Hs, Ws)
        v = _fno_layer(xn, Vcw, Vsw, H, W)
        nh = k.shape[1]
        kf = k.reshape(B, T, nh, Hs * Ws).transpose(0, 2, 1, 3)
        qf = q.reshape(B, T, nh, Hs * Ws).transpose(0, 2, 1, 3)
        vf = v.reshape(B, T, nh, H * W).transpose(0, 2, 1, 3)
        scores = jnp.einsum('bntk,bnsk->bnts', qf, kf) / (np.float32(np.sqrt(Hs * Ws)) * temperature)
        p_attn = jax.nn.softmax(scores, axis=-1)
        av = jnp.einsum('bnts,bnsk->bntk', p_attn, vf)
        av = av.reshape(B, nh, T, H, W).transpose(0, 2, 1, 3, 4).reshape(B * T, nh, H, W)
        p = _fno_layer(av, Pcw, Psw, H, W)
        a = _inorm(p + xa, attn_w, attn_b)
        an = _inorm(a, norm2_w, norm2_b)
        m = _fno_layer(an, m0cw, m0sw, H, W, inner_norm=True, act=True)
        m = _fno_layer(m, m1cw, m1sw, H, W, inner_norm=True, act=False)
        out = _inorm(m, mon_w, mon_b) + a
        return out.reshape(B, T, H, W)

    def _L2_conv_ref(x, bias, up_filter, dn_filter):
        import jax, jax.numpy as jnp
        import numpy as np
        IN_SIZE = 128
        OUT_SIZE = 128
        FILTER_SIZE = 6
        UP_FACTOR = 2
        DN_FACTOR = 2
        SLOPE = 0.2
        GAIN = float(np.sqrt(2.0))

        def _firwin_kaiser(numtaps, cutoff, width, fs):
            nyq = 0.5 * fs
            atten = 2.285 * (numtaps - 1) * np.pi * (width / nyq) + 7.95
            if atten > 50:
                beta = 0.1102 * (atten - 8.7)
            elif atten > 21:
                beta = 0.5842 * (atten - 21) ** 0.4 + 0.07886 * (atten - 21)
            else:
                beta = 0.0
            c = cutoff / nyq
            alpha = 0.5 * (numtaps - 1)
            m = np.arange(numtaps) - alpha
            h = c * np.sinc(c * m)
            h *= np.kaiser(numtaps, beta)
            h /= h.sum()
            return h.astype(np.float32)

        def _make_filter(size, factor):
            taps = FILTER_SIZE * factor
            f1d = _firwin_kaiser(taps, size / 2.0001, size, size)
            f2d = np.outer(f1d, f1d)[None, None]
            return jnp.asarray(f2d, dtype=jnp.float32)

        def _conv_same(x, f):
            k = f.shape[-1]
            pl = (k - 1) // 2
            pr = k - 1 - pl
            return jax.lax.conv_general_dilated(x, f, (1, 1), [(pl, pr), (pl, pr)])
        B, C, H, W = x.shape
        x = x + bias
        x = x.reshape(B * C, 1, H, W)
        x = jnp.repeat(jnp.repeat(x, UP_FACTOR, axis=2), UP_FACTOR, axis=3)
        x = _conv_same(x, up_filter)
        x = jax.nn.leaky_relu(x, negative_slope=SLOPE) * GAIN
        x = _conv_same(x, dn_filter)
        x = x[:, :, ::DN_FACTOR, ::DN_FACTOR]
        return x.reshape(B, C, OUT_SIZE, OUT_SIZE)

    def _L3_conv_ref(x, weight_real, weight_imag):
        import jax, jax.numpy as jnp
        import numpy as np
        B, CIN, COUT, H, W = (8, 32, 32, 128, 128)

        def rfftshift(x):
            return jnp.conj(jnp.flip(jnp.fft.fftshift(x, axes=-2), axis=-1))

        def irfftshift(x):
            return jnp.conj(jnp.flip(jnp.fft.ifftshift(x, axes=-2), axis=-1))

        def symmetric_padding(xf_old, im_shape_old, im_shape_new):
            Ho, Wo = im_shape_old
            Hn, Wn = im_shape_new
            ft_h_old = Ho + (1 - Ho % 2)
            ft_w_old = Wo // 2 + 1
            ft_h_new = Hn + (1 - Hn % 2)
            ft_w_new = Wn // 2 + 1
            nlead = xf_old.ndim - 2
            xf = jnp.pad(xf_old, [(0, 0)] * nlead + [(0, ft_h_old - Ho), (0, 0)])
            if Ho % 2 == 0:
                xf = xf.at[..., 0, :].multiply(0.5)
                xf = xf.at[..., -1, :].set(xf[..., 0, :])
            if Wo % 2 == 0:
                xf = xf.at[..., :, 0].multiply(0.5)
            ph = (ft_h_new - ft_h_old) // 2
            pw = ft_w_new - ft_w_old
            xf = jnp.pad(xf, [(0, 0)] * nlead + [(ph, ph), (pw, 0)])
            if Hn % 2 == 0:
                xf = xf.at[..., 0, :].multiply(2.0)
            if Wn % 2 == 0:
                xf = xf.at[..., :, 0].multiply(2.0)
            return xf[..., :Hn, :]
        weight = jax.lax.complex(weight_real, weight_imag)
        im_shape = (H, W)
        multiplier = symmetric_padding(weight, im_shape, im_shape)
        x_ft = symmetric_padding(rfftshift(jnp.fft.rfft2(x, norm='forward')), im_shape, im_shape)
        out_ft = jnp.einsum('bixy,ioxy->boxy', x_ft, multiplier)
        out = jnp.fft.irfft2(irfftshift(out_ft), s=im_shape, norm='forward')
        return out

    def _gn(v, G=32, eps=1e-5):
        B_, H_, W_, C_ = v.shape
        g = v.reshape(B_, H_, W_, G, C_ // G)
        m = jnp.mean(g, axis=(1, 2, 4), keepdims=True)
        s = jnp.var(g, axis=(1, 2, 4), keepdims=True)
        return ((g - m) / jnp.sqrt(s + eps)).reshape(v.shape)

    def _ln_c(v, eps=1e-6):
        m = jnp.mean(v, axis=-1, keepdims=True)
        s = jnp.var(v, axis=-1, keepdims=True)
        return (v - m) / jnp.sqrt(s + eps)

    def _ln_t(v, eps=1e-5):
        m = jnp.mean(v, axis=-1, keepdims=True)
        s = jnp.var(v, axis=-1, keepdims=True)
        return (v - m) / jnp.sqrt(s + eps)

    def _to_tokens(v):
        B_, H_, W_, C_ = v.shape
        return v.reshape(B_, H_ * W_, C_)
    def _from_tokens(t, like):
        return t.reshape(like.shape)

    x = x + _L0_conv_ref(_gn(x), L0_conv_wK, L0_conv_wKs, L0_conv_bKs, L0_conv_wQ, L0_conv_wQs, L0_conv_bQs, L0_conv_wV, L0_conv_wVs, L0_conv_bVs, L0_conv_wP, L0_conv_wPs, L0_conv_bPs, L0_conv_wM0, L0_conv_wM0s, L0_conv_bM0s, L0_conv_wM1, L0_conv_wM1s, L0_conv_bM1s, L0_conv_norm_g, L0_conv_norm_b)
    x = x + _L1_conv_ref(_gn(x), L1_conv_norm1_w, L1_conv_norm1_b, L1_conv_Kcw, L1_conv_Ksw, L1_conv_Qcw, L1_conv_Qsw, L1_conv_Vcw, L1_conv_Vsw, L1_conv_Pcw, L1_conv_Psw, L1_conv_attn_w, L1_conv_attn_b, L1_conv_norm2_w, L1_conv_norm2_b, L1_conv_m0cw, L1_conv_m0sw, L1_conv_m1cw, L1_conv_m1sw, L1_conv_mon_w, L1_conv_mon_b)
    x = x + _L2_conv_ref(_gn(x), L2_conv_bias, L2_conv_up_filter, L2_conv_dn_filter)
    x = x + _L3_conv_ref(_gn(x), L3_conv_weight_real, L3_conv_weight_imag)
    return x


_drawn_inputs = setup_inputs


def setup_inputs(seed=0):
    import zlib

    import numpy as np

    out = dict(_drawn_inputs(seed))
    spreads = {'L0_conv_bKs': (0.0, 2.0),
     'L0_conv_bQs': (0.0, 2.0),
     'L0_conv_bVs': (0.0, 2.0),
     'L0_conv_norm_g': (1.0, 0.2),
     'L0_conv_norm_b': (0.0, 0.1),
     'L2_conv_bias': (0.0, 0.692)}
    factors = {'L0_conv_wK': 64.0,
     'L0_conv_wQ': 64.0,
     'L0_conv_wV': 23.515,
     'L1_conv_Kcw': 64.0,
     'L1_conv_Qcw': 55.018,
     'L1_conv_Vcw': 8.0}
    for name, (base, spread) in spreads.items():
        noise = np.random.default_rng([zlib.crc32(name.encode()), seed]).standard_normal(out[name].shape)
        drawn = base * np.exp(spread * noise) if base else spread * noise
        out[name] = jnp.asarray(drawn.astype(out[name].dtype))
    for name, factor in factors.items():
        out[name] = (out[name] * factor).astype(out[name].dtype)
    return out
```

```python
import numpy as np
import concourse.bass as bass
from concourse import mybir
from contextlib import ExitStack

NIMG, B, T, H, W = 64, 2, 32, 128, 128
NH = 32
KY, KX, KC = 64, 33, 17
KQ = -(-KX // 4)
EPS = 1e-5
SLOPE, GAIN = 0.2, float(np.sqrt(2.0))
TAPS = 12

P_G, P_B, P_M0S, P_M1S, P_BM0, P_BM1, P_BP = 0, 6, 12, 13, 14, 15, 16
P_BQ, P_BK, P_QS, P_KS, P_PS, P_BV, P_VS, P_Q00, P_K00, P_P00 = range(32, 352, 32)
PROW = 352

C_FA, C_FB1, C_FB2, C_XB1, C_XB2 = 0, 128, 194, 260, 359
C_X21, C_X22, C_E, C_D, C_ID, C_ONE = 458, 558, 658, 786, 914, 1042
C_SR, C_SI, C_MASK = 1170, 1298, 1426
NCONST = 1428
K_FA, K_FB, K_E, K_DC, K_DS, K_ID, K_ROW, K_FLIP = 0, 256, 451, 963, 1091, 1219, 1347, 1351
NCONST3 = 1479


def shape_constants():
    pix = np.arange(128)
    ky = np.r_[0:32, -32:0]
    kx = np.arange(KX)
    ay = 2 * np.pi * np.outer(pix, ky) / 128
    ax = 2 * np.pi * np.outer(pix, kx) / 128
    t = np.zeros((128, NCONST))
    t[:, C_FA:C_FA + 64], t[:, C_FA + 64:C_FA + 128] = np.cos(ay) / 128, -np.sin(ay) / 128
    c, s = np.cos(ax) / 128, np.sin(ax) / 128
    t[:, C_FB1:C_FB1 + 66] = np.c_[c, -s]
    t[:, C_FB2:C_FB2 + 66] = np.c_[s, c]
    re, im = (c, s), (-s, c)
    for n, at in ((0, C_XB1), (1, C_XB2)):
        t[:, at:at + 99] = np.c_[re[n], im[n] - re[n], re[n] + im[n]]
    for n, at in ((0, C_X21), (1, C_X22)):
        r, i = re[n], im[n]
        t[:, at:at + 100] = np.c_[r[:, :KC], (i - r)[:, :KC], (r + i)[:, :KC], i[:, :KC], r[:, KC:], i[:, KC:]]
    t[:, C_E:C_E + 128] = np.r_[np.cos(ay).T, -np.sin(ay).T]
    twice = np.where(kx == 0, 1, 2)[:, None]
    t[:66, C_D:C_D + 128] = np.r_[twice * np.cos(ax).T, -twice * np.sin(ax).T]
    t[:, C_ID:C_ID + 128] = np.eye(128)
    t[:, C_ONE:C_ONE + 128] = 1 / 256
    flip = np.zeros((64, 64))
    flip[np.arange(64), -np.arange(64) % 64] = 1
    for at, sign in ((C_SR, 1), (C_SI, -1)):
        half = (np.eye(64) + sign * flip) / 2
        t[:64, at:at + 64] = half
        t[64:, at + 64:at + 128] = half
    t[:, C_MASK] = np.arange(128) % 64 != 0
    t[:, C_MASK + 1] = np.arange(128) % 64 != 32
    ky, kx = np.arange(128) - 64, 64 - np.arange(65)
    ay, ax = 2 * np.pi * np.outer(pix, ky) / 128, 2 * np.pi * np.outer(pix, kx) / 128
    t3 = np.zeros((128, NCONST3))
    t3[:, K_FA:K_FA + 256] = np.c_[np.cos(ay), -np.sin(ay)] / 128
    t3[:, K_FB:K_FB + 195] = np.c_[np.sin(ax), np.cos(ax), -np.sin(ax)] / 128
    back = np.stack([np.c_[np.cos(ay).T, np.sin(ay).T], np.c_[-np.sin(ay).T, np.cos(ay).T]])
    back = back.reshape(2, 2, 16, 2, 2, 256)
    t3[:, K_E:K_E + 512] = back.transpose(3, 2, 1, 0, 4, 5).reshape(128, 512)
    t3[:, K_ID:K_ID + 128] = np.eye(128)
    t3[:, K_ROW:K_ROW + 4] = np.arange(128)[:, None] % 4 == np.arange(4)
    t3[:, K_FLIP:K_FLIP + 128] = np.eye(128)[::-1]
    twice = np.where(kx % 64 == 0, 1, 2)[:, None]
    t3[:65, K_DC:K_DC + 128], t3[:65, K_DS:K_DS + 128] = twice * np.cos(ax).T, -twice * np.sin(ax).T
    sel = np.zeros((3, 32, 8, 4, 32))
    for h in range(32):
        sel[:, h, h // 4, h % 4, :] = 1
    return t.astype(np.float32), t3.astype(np.float32), sel.reshape(96, 1024).astype(np.float32)


def build(nc, io):
    f32, bf16 = mybir.dt.float32, mybir.dt.bfloat16
    ALU, ACT, AX = mybir.AluOpType, mybir.ActivationFunctionType, mybir.AxisListType
    mult, add, sub, amax = ALU.mult, ALU.add, ALU.subtract, ALU.max
    NL = 2
    NLINE = 52
    ctx = ExitStack()
    with ctx:
        SB = 53200
        sb = ctx.enter_context(nc.sbuf_tensor("sb", [128, SB], f32))
        bank = [ctx.enter_context(nc.psum_tensor(f"bank{i}", [128, 512], f32)) for i in range(8)]
        scratch_xn = nc.dram_tensor("scratch_xn", [NIMG, H, W], f32)
        scratch_ln = nc.dram_tensor("scratch_ln", [NLINE * 256], f32)
        scratch_x = nc.dram_tensor("scratch_x", [NIMG, H, W], f32)
        scratch_xb = nc.dram_tensor("scratch_xb", [NIMG, 3, KX, KY], f32)

        def sem(name):
            return ctx.enter_context(nc.semaphore(name))

        def at(off, dims, lo=0, hi=128, of=sb):
            pitch = SB if of is sb else 512
            return bass.AP(tensor=of, offset=off + lo * pitch, ap=[[pitch, hi - lo]] + [list(d) for d in dims])

        def pat(bk, off, dims, lo=0, hi=128):
            return at(off, dims, lo, hi, bank[bk])

        XR, XA, FF, CST = 0, 8192, 16384, 24576
        SEL = CST + NCONST
        SM = SEL + 512
        PR = SM
        ST = PR + 2 * PROW
        MS, DV, SQ, QQ, VS = ST + 384, ST + 448, ST + 576, ST + 704, ST + 832
        S0, C0, S1, C1, S2, C2 = (ST + 896 + 64 * i for i in range(6))
        S3, C3, S5, C5 = (S2 + 128 + 16 * i for i in range(4))
        RW = C5 + 16
        R_GO, R_CT, R_SS, R_Q0, R_K0, R_TMP = (RW + 32 * i for i in range(6))
        D0 = RW + 192
        EPSC = D0 + 1
        VP = D0 + 2
        WM = VP + 4
        WI = WM + 2 * 2 * 66
        U = WI + 2 * 66
        AF, BP = U, U + 1632
        AT = AF
        MB, MT = BP + 3168, BP + 3232
        V0 = MT + 64
        assert V0 + 17728 <= SB, V0
        NQ = KQ * KY
        PW, VW, VF = V0, V0 + 2 * NQ, V0 + 4 * NQ
        BF = VF + 128
        PARTS = [BF + 3 * NQ + i * (3 * NQ // 2) for i in range(3)]
        QK, QKF, QT = V0 + 12864, V0 + 15040, V0 + 15168
        assert QT + 1088 + 64 <= V0 + 17728 and PARTS[2] + 3 * NQ // 2 <= QK
        GG, XB, X2 = V0, V0 + 8192, V0 + 14528
        TX, TG, ZZ = V0, V0 + 3264, V0 + 8192
        SC, TP = ZZ + 512, ZZ + 1536
        XT = V0
        XC, BX, SY, ZC = V0, V0 + 1536, V0 + 4608, V0 + 8832
        YR = ZC + 1024
        assert YR + KX * 192 <= SB
        HH = U
        GR, SP, T1, T2, ZM = HH + 8192, HH + 10496, HH + 11024, HH + 11552, HH + 12080

        NP_ = W + 6
        XP, MAT, YY = XA, XA + NIMG * NP_, U
        LN = XA
        BI, TP2, CS = WM, LN + NLINE * 256, LN + NLINE * 256 + 288
        Y_N, Y_B, Y_A = NP_, 4 * NP_, 8 * NP_
        G3 = SEL
        XM = (2 * 8320, G3 + 3 * 4096)
        CK = XM[1] + 64 * 130
        XQ = CK + NCONST3
        TT = XQ + 2 * 2080
        WB = (0, 8320)
        YM, YT = G3, 0
        Z3, XO, OO = G3 + 8320, G3, G3 + 2048
        assert TT + 640 <= SB and Z3 + 2048 <= XM[1] and XM[0] + 8320 <= G3

        def cst(col, n, lo=0, hi=128):
            return sb[lo:hi, CST + col:CST + col + n]

        def par(L, col, lo=0, hi=128):
            return sb[lo:hi, PR + L * PROW + col:PR + L * PROW + col + 1]

        names = """x_loaded consts_loaded weights_loaded sel_cast
            stat_sums mean_ready var_in var_ready std_ready dve_order pool_order act_order
            gn_ready xn_ready a_form b_form hi_ready r1_ready mid_ready r2_ready lo_ready parts_moved a_psum
            g_psum g_ready x2_psum x2_ready xb_psum xb_ready sym_psum xb_stored xn_stored
            zero_t t_ready z_ready z_used gout_psum exp_in exp_ready
            mix_ready mixT_psum mixT_ready attn_ready attnT_psum attnT_ready xt_loaded
            skip_psum skip_used skip_done xc_loaded0 xc_loaded1 rep_psum bx_ready comb_ready bx_used acc_used sy_psum sy_ready
            zi_psum zi_ready p_psum p_used 
            an_ready ga_psum ga_ready gb_psum gb_used sp_ready zc_psum zc_ready h_psum h_ready
            att_var att_std pre_gelu gelu_ready x_done 
            taps_loaded lines_made lines_stored mats_loaded bias_loaded flip_psum mats_ready xp2_ready pads_ready
            up_psum up_copied y_ready dn_psum x2_done x2_stored
            k_loaded g3_psum g3_ready g3_neg xm_psum xm_ready w_loaded0 w_loaded1
            xq_zero xq_ready y3_psum t_part t_sum y3_kept ty_psum ty_ready z3_psum z3_ready o_psum o_ready xo_loaded0 xo_loaded1 xo_loaded2 xo_loaded3 o_stored0 o_stored1""".split()
        S = {n: sem(n) for n in names}

        class Rounds:
            def __init__(self):
                self.n = 0

        dve_r, pe_r, act_r = Rounds(), Rounds(), Rounds()
        order = {"dve": 0, "pool": 0, "act": 0}

        def link(ins, eng, who):
            order[who] += 1
            ins.then_inc(S[who + "_order"], 1)
            eng.wait_ge(S[who + "_order"], order[who])

        block = ctx.enter_context(nc.Block())

        def pe_mean(pe, C):
            pe.wait_ge(S["stat_sums"], pe_r.n + 1)
            nc.tensor.matmul(bank[7][:, 0:C], cst(C_ONE, 128), sb[:, MS:MS + C], start=True, stop=True).then_inc(S["mean_ready"], 1)

        def pe_var(pe, C):
            pe.wait_ge(S["var_in"], pe_r.n + 1)
            nc.tensor.matmul(bank[7][:, 64:64 + C], cst(C_ONE, 128), sb[:, VS:VS + C], start=True, stop=True).then_inc(S["var_ready"], 1)
            pe_r.n += 1

        def act_std(act, C):
            act.wait_ge(S["var_ready"], act_r.n + 1)
            nc.scalar.activation(bank[7][:, 128:128 + C], bank[7][:, 64:64 + C], ACT.Sqrt, bias=sb[:, EPSC:EPSC + 1]).then_inc(S["std_ready"], 1)
            act_r.n += 1

        def dve_sums(dve, C, st=ST):
            nc.vector.tensor_tensor(sb[:, MS:MS + C], at(st + 1, [[6, C]]), at(st + 4, [[6, C]]), add).then_inc(S["stat_sums"], 1)

        def dve_var_in(dve, C, st=ST):
            dve.wait_ge(S["mean_ready"], dve_r.n + 1)
            two = [[2, C], [1, 2]]
            link(nc.vector.tensor_tensor(at(DV, two), at(st + 1, [[6, C], [3, 2]]), pat(7, 0, [[1, C], [0, 2]]), sub), dve, "dve")
            link(nc.vector.tensor_tensor(at(SQ, two), at(DV, two), at(DV, two), mult), dve, "dve")
            link(nc.vector.scalar_tensor_tensor(at(QQ, two), at(st + 2, [[6, C], [3, 2]]), 1 / 64, at(SQ, two), mult, add), dve, "dve")
            nc.vector.tensor_tensor(sb[:, VS:VS + C], at(QQ, [[2, C]]), at(QQ + 1, [[2, C]]), add).then_inc(S["var_in"], 1)

        def dve_rstd(dve, C):
            dve.wait_ge(S["std_ready"], dve_r.n + 1)
            link(nc.vector.reciprocal(bank[7][:, 128:128 + C], bank[7][:, 128:128 + C]), dve, "dve")
            dve_r.n += 1

        def whole_round(eng, who, C):
            if who == "dve":
                dve_sums(eng, C); dve_var_in(eng, C); dve_rstd(eng, C)
            elif who == "pe":
                pe_mean(eng, C); pe_var(eng, C)
            else:
                act_std(eng, C)

        MEAN, VAR, RSTD = 0, 64, 128

        def affine(dve, L, g, b, C, s_at, c_at, extra=None):
            link(nc.vector.tensor_scalar(sb[:, s_at:s_at + C], bank[7][:, RSTD:RSTD + C], par(L, g), None, mult), dve, "dve")
            link(nc.vector.tensor_tensor(sb[:, c_at:c_at + C], bank[7][:, MEAN:MEAN + C], sb[:, s_at:s_at + C], mult), dve, "dve")
            link(nc.vector.tensor_scalar(sb[:, c_at:c_at + C], sb[:, c_at:c_at + C], -1.0, par(L, b), mult, add), dve, "dve")
            if extra is not None:
                link(nc.vector.tensor_scalar(sb[:, c_at:c_at + C], sb[:, c_at:c_at + C], extra, None, add), dve, "dve")

        def group_norm(dve, k):
            if k == 3:
                dve.wait_ge(S["x2_done"], 16)
            elif k >= 1:
                dve.wait_ge(S["x_done"], 4 * k)
            for b in range(B):
                for g in range(32):
                    last = nc.vector.bn_stats(sb[:, ST + (b * 32 + g) * 6:ST + (b * 32 + g) * 6 + 6],
                                              at(XR + b * 4096 + 4 * g, [[128, 32], [1, 4]]))
            link(last, dve, "dve")
            whole_round(dve, "dve", 64)
            if k == 0:
                dve.wait_ge(S["lines_stored"], 16)
            if k == 2:
                dve.wait_ge(S["bias_loaded"], 16)
                link(nc.vector.tensor_copy(bank[7][:, 192:256], sb[:, BI:BI + 64]), dve, "dve")
                for b in range(B):
                    img, pad = [[128, 32], [4, 32], [1, 4]], [[NP_, 32], [4, 32], [1, 4]]
                    grp, o = [[0, 32], [1, 32], [0, 4]], XP + 32 * NP_ * b + 3
                    link(nc.vector.tensor_tensor(at(o, pad), at(XR + b * 4096, img), pat(7, MEAN + b * 32, grp), sub), dve, "dve")
                    link(nc.vector.tensor_tensor(at(o, pad), at(o, pad), pat(7, RSTD + b * 32, grp), mult), dve, "dve")
                    row = [[NP_, 32], [1, 128]]
                    last = nc.vector.tensor_tensor(at(o, row), at(o, row), pat(7, 192 + b * 32, [[1, 32], [0, 128]]), add)
                last.then_inc(S["xp2_ready"], 1)
                return
            for b in range(B):
                img = [[128, 32], [4, 32], [1, 4]]
                grp = [[0, 32], [1, 32], [0, 4]]
                link(nc.vector.tensor_tensor(at(XA + b * 4096, img), at(XR + b * 4096, img), pat(7, MEAN + b * 32, grp), sub), dve, "dve")
                last = nc.vector.tensor_tensor(at(XA + b * 4096, img), at(XA + b * 4096, img), pat(7, RSTD + b * 32, grp), mult)
                if b == 0:
                    link(last, dve, "dve")
            last.then_inc(S["gn_ready"], 1)
            dve.wait_ge(S["gn_ready"], min(k + 1, 3))

        def image_stats(dve, src, n0, n1, st=ST):
            for j, n in enumerate(range(n0, n1)):
                last = nc.vector.bn_stats(sb[:, st + 6 * j:st + 6 * j + 6], sb[:, src + n * 128:src + n * 128 + 128])
            link(last, dve, "dve")

        def scale_images(src, dst, n0, n1, s_at, c_at):
            for n in range(n0, n1):
                last = nc.vector.tensor_scalar(sb[:, dst + n * 128:dst + n * 128 + 128], sb[:, src + n * 128:src + n * 128 + 128],
                                               sb[:, s_at + n - n0:s_at + n - n0 + 1], sb[:, c_at + n - n0:c_at + n - n0 + 1], mult, add)
            return last

        NKP = 17
        NU = NIMG // 4
        UPS = [(a, b) for a in range(2) for b in range(2)]

        @block.sync
        def _(sp):
            sp.dma_start(sb[0:1, TP2:TP2 + 288], io["taps"]).then_inc(S["taps_loaded"], 16)
            for q in range(4):
                sp.dma_start(at(XR + q * 2048, [[128, 16], [1, 128]]), io["x"][16 * q:16 * q + 16].rearrange("n h w -> h n w")).then_inc(S["x_loaded"], 16)
            sp.dma_start(cst(0, NCONST), io["cst"]).then_inc(S["consts_loaded"], 16)
            sp.dma_start(sb[:, PR:PR + 2 * PROW], bass.AP(tensor=io["prow"].tensor, offset=io["prow"].offset, ap=[[0, 128], [1, 2 * PROW]])).then_inc(S["consts_loaded"], 16)
            sp.dma_start(sb[:, VP:VP + 4], io["vsps"]).then_inc(S["consts_loaded"], 16)
            sp.dma_start(at(WM, [[132, 2], [66, 2], [1, 66]]), io["wm"].rearrange("l j p c -> p l j c")).then_inc(S["consts_loaded"], 16)
            sp.dma_start(sb[0:96, V0 + 16384:V0 + 16384 + 1024], io["sel"]).then_inc(S["consts_loaded"], 16)
            sp.wait_ge(S["lines_made"], 1)
            sp.dma_start(scratch_ln.ap().rearrange("(p n) -> p n", p=1), sb[0:1, LN:LN + NLINE * 256]).then_inc(S["lines_stored"], 16)
            for L in range(NL):
                if L:
                    sp.wait_ge(S["x_done"], 4 * L)
                sp.dma_start(sb[:, QK:QK + 2176], io["qk"][L]).then_inc(S["weights_loaded"], 16)
                sp.dma_start(sb[:, QKF:QKF + 128], io["qkf"][L]).then_inc(S["weights_loaded"], 16)
                sp.dma_start(sb[:, PW:PW + 2 * NQ], io["pw"][L]).then_inc(S["weights_loaded"], 16)
                sp.dma_start(sb[:, VW:VW + 2 * NQ], io["vw"][L]).then_inc(S["weights_loaded"], 16)
                sp.dma_start(sb[0:32, VF:VF + 128], io["vf"][L]).then_inc(S["weights_loaded"], 16)
                for i, ready in enumerate(("hi_ready", "mid_ready", "lo_ready")):
                    sp.wait_ge(S[ready], L + 1)
                    for g in range(4):
                        w = min(KQ, KX - KQ * g) * KY // 2
                        sp.dma_start(at(BP + g * (NQ // 2), [[KX * KY // 2, 3], [1, w]], 32 * i, 32 * i + 32),
                                     at(PARTS[i], [[NQ // 2, 3], [1, w]], 32 * g, 32 * g + 32)).then_inc(S["parts_moved"], 16)
                sp.wait_ge(S["xn_ready"], L + 1)
                sp.dma_start(scratch_xn.ap().rearrange("n h w -> h n w"), at(FF, [[128, 64], [1, 128]])).then_inc(S["xn_stored"], 16)
                sp.wait_ge(S["xb_ready"], 13 * (L + 1))
                sp.dma_start(scratch_xb.ap().rearrange("n f x y -> n (f x y)"), sb[0:64, XB:XB + 6336]).then_inc(S["xb_stored"], 16)
                sp.wait_ge(S["attnT_ready"], L + 1)
                sp.wait_ge(S["xn_stored"], 16 * (L + 1))
                sp.dma_start(sb[0:64, XT:XT + 16384], scratch_xn.ap().rearrange("n h w -> n (h w)")).then_inc(S["xt_loaded"], 16)
                sp.wait_ge(S["xb_stored"], 16 * (L + 1))
                for kp in range(NKP):
                    k = L * NKP + kp
                    if kp == 0:
                        sp.wait_ge(S["skip_done"], L + 1)
                    if k >= 2:
                        sp.wait_ge(S["bx_ready"], 8 * (k - 1))
                    nk = 2 if kp < NKP - 1 else 1
                    for b in range(B):
                        src = bass.AP(tensor=scratch_xb, offset=b * 32 * 6336 + kp * 2 * KY,
                                      ap=[[0, 4], [6336, 32], [KX * KY, 3], [1, nk * KY]])
                        sp.dma_start(at(XC + 768 * (k % 2) + 384 * b, [[nk * KY, 3], [1, nk * KY]]), src).then_inc(S[f"xc_loaded{k % 2}"], 16)
            sp.wait_ge(S["x_done"], 8)
            sp.wait_ge(S["lines_stored"], 16)
            sp.dma_start(at(MAT, [[128, NLINE], [1, 128]]), bass.AP(tensor=scratch_ln, offset=0, ap=[[1, 128], [256, NLINE], [1, 128]])).then_inc(S["mats_loaded"], 16)
            sp.dma_start(sb[:, BI:BI + 64], bass.AP(tensor=io["bias"].tensor, offset=0, ap=[[0, 128], [1, 64]])).then_inc(S["bias_loaded"], 16)
            w = (io["w3r"], io["w3i"])

            def load_chunk(c, k):
                for part in range(2):
                    for a in range(2):
                        src = bass.AP(tensor=w[part].tensor, offset=a * 64 * 65 + c * 260, ap=[[32 * 8320, 32], [8320, 32], [1, 260]])
                        lo = 64 * part + 32 * a
                        sp.dma_start(at(WB[k], [[260, 32], [1, 260]], lo, lo + 32), src).then_inc(S[f"w_loaded{k}"], 16)

            sp.dma_start(sb[:, CK:CK + NCONST3], io["cst3"]).then_inc(S["k_loaded"], 16)
            sp.wait_ge(S["x2_done"], 16)
            sp.dma_start(scratch_x.ap().rearrange("n h w -> h n w"), at(XR, [[128, 64], [1, 128]])).then_inc(S["x2_stored"], 16)
            sp.wait_ge(S["x2_stored"], 16)
            sp.wait_ge(S["gn_ready"], 3)
            sp.wait_ge(S["g3_psum"], 1)
            load_chunk(0, 0)
            sp.wait_ge(S["g3_psum"], 32)
            load_chunk(1, 1)
            with sp.Fori(1, 8) as it:
                for k in range(2):
                    sp.wait_ge(S["y3_psum"], 10 * it + 5 * k - 5)
                    load_chunk(2 * it + k, k)
            for u in range(NU):
                if u == 0:
                    sp.wait_ge(S["ty_psum"], 33)
                if u >= 4:
                    sp.wait_ge(S["o_ready"], u - 3)
                sp.dma_start(at(XO + 512 * (u % 4), [[128, 4], [1, 128]]), scratch_x.ap()[4 * u:4 * u + 4].rearrange("n h w -> h n w")).then_inc(S[f"xo_loaded{u % 4}"], 16)
                if u >= 2:
                    sp.wait_ge(S["o_ready"], u - 1)
                    sp.dma_start(io["out"][4 * u - 8:4 * u - 4].rearrange("n h w -> h n w"), at(OO + 512 * (u % 2), [[128, 4], [1, 128]])).then_inc(S[f"o_stored{u % 2}"], 16)
            for u in (NU, NU + 1):
                sp.wait_ge(S["o_ready"], u - 1)
                sp.dma_start(io["out"][4 * u - 8:4 * u - 4].rearrange("n h w -> h n w"), at(OO + 512 * (u % 2), [[128, 4], [1, 128]])).then_inc(S[f"o_stored{u % 2}"], 16)
            for e in range(2):
                sp.wait_ge(S[f"o_stored{e}"], 16 * NU // 2)

        @block.gpsimd
        def _(gp):
            def tt(o, a, b_, op):
                link(nc.gpsimd.tensor_tensor(o, a, b_, op), gp, "pool")

            def ts(o, a, s1, s2, o1, o2=ALU.bypass):
                link(nc.gpsimd.tensor_scalar(o, a, s1, s2, o1, o2) if s2 is not None else nc.gpsimd.tensor_scalar(o, a, s1, None, o1), gp, "pool")

            gp.wait_ge(S["taps_loaded"], 16)
            one = lambda off, dims: at(off, dims, 0, 1)
            nc.gpsimd.memset(sb[0:1, CS:CS + 168], 0.0)
            link(nc.gpsimd.memset(sb[0:1, LN:LN + NLINE * 256], 0.0), gp, "pool")
            f, d = TP2, TP2 + 144
            nc.gpsimd.tensor_copy(one(CS, [[7, 12], [6, 2]]), one(f, [[12, 12], [11, 2]]))
            nc.gpsimd.tensor_tensor(one(CS + 1, [[7, 12], [1, 5]]), one(f + 1, [[12, 12], [2, 5]]), one(f + 2, [[12, 12], [2, 5]]), add)
            link(nc.gpsimd.tensor_tensor(one(CS + 84 + 1, [[7, 12], [1, 6]]), one(f, [[12, 12], [2, 6]]), one(f + 1, [[12, 12], [2, 6]]), add), gp, "pool")
            for b in range(2):
                ln, cs = LN + 7 * 256 * b, CS + 84 * b
                nc.gpsimd.tensor_copy(one(ln + 124, [[256, 7], [6, 2]]), one(cs + 77, [[1, 7], [-77, 2]]))
                nc.gpsimd.tensor_tensor(one(ln + 129, [[256, 7], [-1, 5]]), one(cs + 7, [[1, 7], [14, 5]]), one(cs + 14, [[1, 7], [14, 5]]), add)
                ln += 14 * 256
                nc.gpsimd.tensor_tensor(one(ln + 129, [[256, 7], [-1, 6]]), one(cs, [[1, 7], [14, 6]]), one(cs + 7, [[1, 7], [14, 6]]), add)
            ln = LN + 28 * 256
            nc.gpsimd.tensor_scalar(one(ln + 129, [[256, 12], [-1, 6]]), one(d + 12, [[1, 12], [24, 6]]), GAIN, None, mult)
            nc.gpsimd.tensor_scalar(one(ln + 12 * 256 + 130, [[256, 12], [-1, 6]]), one(d, [[1, 12], [24, 6]]), GAIN, None, mult).then_inc(S["lines_made"], 1)
            gp.wait_ge(S["consts_loaded"], 80)
            for L in range(NL):
                gp.wait_ge(S["weights_loaded"], 80 * (L + 1))
                q, k = QK, QK + 1088
                for j in range(4):
                    o = QK + 544 * j
                    tt(sb[:, o:o + 32], sb[:, o:o + 32], sb[:, QKF + 32 * j:QKF + 32 * j + 32], add if j % 2 == 0 else sub)
                    ts(sb[:, o:o + 32], sb[:, o:o + 32], 0.5, None, mult)
                for o, p in ((q, P_QS), (k, P_KS)):
                    kh = [[32, KC], [1, 32]]
                    tt(at(o, kh), at(o, kh), at(PR + L * PROW + p, [[0, KC], [1, 32]]), add)
                n = KC * 32
                fa = [[96, KC], [1, 32]]
                kh = [[32, KC], [1, 32]]
                qr, qi, kr, ki = q, q + n, k, k + n
                tt(sb[:, QT:QT + n], sb[:, qr:qr + n], sb[:, kr:kr + n], mult)
                tt(sb[:, QT + n:QT + 2 * n], sb[:, qi:qi + n], sb[:, ki:ki + n], mult)
                tt(at(AF + 32, fa), at(QT, kh), at(QT + n, kh), add)
                tt(sb[:, QT:QT + n], sb[:, qr:qr + n], sb[:, ki:ki + n], mult)
                tt(sb[:, QT + n:QT + 2 * n], sb[:, qi:qi + n], sb[:, kr:kr + n], mult)
                tt(at(AF + 64, fa), at(QT, kh), at(QT + n, kh), sub)
                ts(at(AF + 96 + 32, [[96, KC - 1], [1, 64]]), at(AF + 96 + 32, [[96, KC - 1], [1, 64]]), 128.0, None, mult)
                ts(sb[:, AF + 32:AF + 96], sb[:, AF + 32:AF + 96], cst(C_MASK, 1), 64.0, mult, mult)
                nc.gpsimd.tensor_tensor(at(AF, fa), at(AF + 32, fa), at(AF + 64, fa), add).then_inc(S["a_form"], 1)
                n = NQ
                w_v, w_p = sb[:, VP + 2 * L:VP + 2 * L + 1], sb[:, VP + 2 * L + 1:VP + 2 * L + 2]
                for j, op in ((0, add), (1, sub)):
                    o = VW + n * j
                    tt(sb[0:32, o:o + 64], sb[0:32, o:o + 64], sb[0:32, VF + 64 * j:VF + 64 * j + 64], op)
                    ts(sb[0:32, o:o + 64], sb[0:32, o:o + 64], 0.5, None, mult)
                vr, vi, pr, pi = VW, VW + n, PW, PW + n
                tmp, fr, fi = BF, BF + n, BF + 2 * n
                col = lambda o: sb[:, o:o + n]
                ts(col(fr), col(pr), w_v, None, mult)
                ts(col(fi), col(pi), w_v, None, mult)
                for o, a, c, op in ((fr, vr, pr, add), (fr, vi, pi, sub), (fi, vr, pi, add), (fi, vi, pr, add)):
                    tt(col(tmp), col(a), col(c), mult)
                    tt(col(o), col(o), col(tmp), op)
                for o, a in ((fr, vr), (fi, vi)):
                    ts(col(tmp), col(a), w_p, None, mult)
                    tt(col(o), col(o), col(tmp), add)
                nc.gpsimd.tensor_tensor(col(BF), col(fr), col(fi), add).then_inc(S["b_form"], 1)
                gp.wait_ge(S["b_form"], L + 1)
                f = sb[:, BF:BF + 3 * n]
                part = lambda i: sb[:, PARTS[i]:PARTS[i] + 3 * n // 2].bitcast(bf16)
                gp.wait_ge(S["hi_ready"], L + 1)
                nc.gpsimd.tensor_tensor(f, f, part(0), sub).then_inc(S["r1_ready"], 1)
                gp.wait_ge(S["mid_ready"], L + 1)
                nc.gpsimd.tensor_tensor(f, f, part(1), sub).then_inc(S["r2_ready"], 1)
                gp.wait_ge(S["xb_psum"], 13 * (L + 1))
                gp.wait_ge(S["x2_psum"], 8 * (L + 1))
                nc.gpsimd.memset(sb[:, TX:TX + 5312], 0.0)
                nc.gpsimd.memset(sb[0:64, MB:MB + 64], 0.0).then_inc(S["zero_t"], 1)
                for kp in range(NKP):
                    n = 128 if kp < NKP - 1 else 64
                    for c in range(8):
                        k = (L * NKP + kp) * 8 + c
                        form = lambda f: at(BX + 768 * (k % 4) + f * n, [[3 * n, 2], [1, n]])
                        gp.wait_ge(S["bx_ready"], k + 1)
                        if c % 2 == 0:
                            nc.gpsimd.tensor_tensor(form(2), form(0), form(2), sub)
                        nc.gpsimd.tensor_tensor(form(1), form(0), form(1), add).then_inc(S["comb_ready"], 1)
                for k in range(L * 32, L * 32 + 32):
                    b_ = k % 2
                    gp.wait_ge(S["gb_used"], k + 1)
                    if k >= 2:
                        gp.wait_ge(S["zc_psum"], k - 1)
                    nc.gpsimd.tensor_tensor(sb[:, SP + 264 * b_:SP + 264 * b_ + 264], sb[:, T1 + 264 * b_:T1 + 264 * b_ + 264],
                                            sb[:, T2 + 264 * b_:T2 + 264 * b_ + 264], add).then_inc(S["sp_ready"], 1)
            gp.wait_ge(S["x_done"], 8)
            nc.gpsimd.memset(at(XP, [[NP_, 64], [131, 2], [1, 3]]), 0.0)
            nc.gpsimd.memset(at(YY, [[NP_, 32], [131, 2], [1, 3]]), 0.0).then_inc(S["pads_ready"], 1)
            gp.wait_ge(S["k_loaded"], 16)
            nc.gpsimd.memset(sb[:, XQ:XQ + 4160], 0.0).then_inc(S["xq_zero"], 1)
            gp.wait_ge(S["xq_zero"], 1)
            gp.wait_ge(S["xm_ready"], 64)

            def spread(c, e, first=False):
                if not first:
                    gp.wait_ge(S["y3_psum"], 5 * c - 5)
                for lo in range(0, 128, 32):
                    a = lo // 32 % 2
                    last = nc.gpsimd.tensor_copy(at(XQ + 2080 * e + 2 * a, [[8, 260], [4, 2], [1, 2]], lo, lo + 32),
                                                 at(XM[0] + 520 * c, [[2, 260], [XM[1] - XM[0], 2], [1, 2]], lo, lo + 32))
                last.then_inc(S["xq_ready"], 1)

            spread(0, 0, True)
            spread(1, 1, True)
            with gp.Fori(1, 8) as it:
                spread(2 * it, 0)
                spread(2 * it + 1, 1)

        def round_at(i):
            out = []
            if (i - 7) % 4 == 0 and 0 <= (i - 7) // 4 < 8:
                out.append(("first", (i - 7) // 4))
            if (i - 8) % 4 == 0 and 4 <= (i - 8) // 4 < 8:
                out.append(("second", (i - 8) // 4))
            return out

        @block.scalar
        def _(act):
            act.wait_ge(S["consts_loaded"], 80)
            nc.scalar.activation(sb[0:96, SEL:SEL + 512].bitcast(bf16), sb[0:96, V0 + 16384:V0 + 16384 + 1024], ACT.Copy).then_inc(S["sel_cast"], 1)
            act.wait_ge(S["sel_cast"], 2)
            for L in range(NL):
                whole_round(act, "act", 64)
                whole_round(act, "act", 64)
                act.wait_ge(S["b_form"], L + 1)
                f = sb[:, BF:BF + 3 * NQ]
                part = lambda i: sb[:, PARTS[i]:PARTS[i] + 3 * NQ // 2].bitcast(bf16)
                nc.scalar.activation(part(0), f, ACT.Copy).then_inc(S["hi_ready"], 1)
                act.wait_ge(S["r1_ready"], L + 1)
                nc.scalar.activation(part(1), f, ACT.Copy).then_inc(S["mid_ready"], 1)
                act.wait_ge(S["r2_ready"], L + 1)
                nc.scalar.activation(part(2), f, ACT.Copy).then_inc(S["lo_ready"], 1)
                act.wait_ge(S["parts_moved"], 192 * (L + 1))
                for u in range(NU):
                    k = L * NU + u
                    act.wait_ge(S["g_psum"], k + 1)
                    nc.scalar.activation(sb[:, GG + u * 512:GG + u * 512 + 512], bank[u % 2][:, :], ACT.Copy).then_inc(S["g_ready"], 1)
                for u in range(8):
                    k = L * 8 + u
                    act.wait_ge(S["x2_psum"], k + 1)
                    nc.scalar.activation(sb[:, X2 + u * 400:X2 + u * 400 + 400], bank[2 + u % 2][:, 0:400], ACT.Copy).then_inc(S["x2_ready"], 1)
                for u in range(13):
                    k = L * 13 + u
                    ny = min(5, KY - 5 * u)
                    act.wait_ge(S["xb_psum"], k + 1)
                    nc.scalar.activation(at(XB + 5 * u, [[64, 99], [1, ny]], 0, 64), pat(4 + u % 2, 0, [[1, 99], [99, ny]], 0, 64),
                                         ACT.Copy).then_inc(S["xb_ready"], 1)
                act.wait_ge(S["a_form"], L + 1)
                for j in range(4):
                    n = 96 * min(5, KC - 5 * j)
                    last = nc.scalar.activation(bank[j][:, 0:n], sb[:, AF + 480 * j:AF + 480 * j + n], ACT.Copy)
                last.then_inc(S["a_psum"], 1)
                act.wait_ge(S["exp_in"], L + 1)
                nc.scalar.activation(sb[0:64, SC:SC + 1024], sb[0:64, SC:SC + 1024], ACT.Exp).then_inc(S["exp_ready"], 1)
                def rows_copy(kp):
                    kk = L * NKP + kp
                    act.wait_ge(S["sy_psum"], kk + 1)
                    cols = 2 if kp < NKP - 1 else 1
                    nc.scalar.activation(at(SY + 2 * kp, [[33, 2], [1, cols], [66, 64]]), pat(4 + kk % 2, 0, [[128, 2], [64, cols], [1, 64]]),
                                         ACT.Copy).then_inc(S["sy_ready"], 1)

                for kp in range(NKP):
                    kk = L * NKP + kp
                    cols = 2 if kp < NKP - 1 else 1
                    if kp:
                        rows_copy(kp - 1)
                    act.wait_ge(S["bx_used"], 8 * (kk + 1))
                    if kp == 0:
                        act.wait_ge(S["skip_done"], L + 1)
                    for f, part, scale in ((0, 1, 1.0), (1, 0, 1.0), (2, 1, -1.0)):
                        last = nc.scalar.activation(at(YR + 384 * kp + 64 * f, [[192, cols], [1, 64]], 0, 64),
                                                    pat(3 + 3 * (kk % 2), 64 * cols * part, [[64, cols], [1, 64]], 0, 64), ACT.Copy, scale=scale)
                    last.then_inc(S["acc_used"], 1)
                rows_copy(NKP - 1)
                for u in range(NU):
                    k = L * NU + u
                    act.wait_ge(S["zi_psum"], k + 1)
                    if u >= 2:
                        act.wait_ge(S["p_psum"], k - 1)
                    nc.scalar.activation(sb[0:66, ZC + 512 * (u % 2):ZC + 512 * (u % 2) + 512], bank[4][0:66, :], ACT.Copy).then_inc(S["zi_ready"], 1)
                whole_round(act, "act", 64)
                act.wait_ge(S["att_var"], L + 1)
                nc.scalar.activation(sb[:, DV:DV + 64], sb[:, QQ:QQ + 64], ACT.Sqrt, bias=sb[:, EPSC:EPSC + 1]).then_inc(S["att_std"], 1)
                for i in range(38):
                    k = L * 32 + i
                    if i < 32:
                        o = GR + 768 * (k % 3)
                        bk = (0, 4)[k % 2]
                        act.wait_ge(S["ga_psum"], k + 1)
                        if k >= 3:
                            act.wait_ge(S["gb_psum"], k - 2)
                        nc.scalar.activation(at(o, [[192, 4], [1, 128]]), pat(bk, 0, [[128, 4], [1, 128]]), ACT.Copy)
                        nc.scalar.activation(at(o + 128, [[192, 4], [1, 64]]), pat(bk, 0, [[128, 4], [1, 64]]), ACT.Copy, scale=-1.0).then_inc(S["ga_ready"], 1)
                    if round_at(i):
                        act_std(act, 16)
                    if 0 <= i - 2 < 32:
                        k = L * 32 + i - 2
                        act.wait_ge(S["zc_psum"], k + 1)
                        if k >= 2:
                            act.wait_ge(S["h_psum"], k - 1)
                        nc.scalar.activation(sb[0:66, ZM + 512 * (k % 2):ZM + 512 * (k % 2) + 512], bank[(2, 6)[k % 2]][0:66, :], ACT.Copy).then_inc(S["zc_ready"], 1)
                    if 0 <= i - 3 < 32:
                        k = L * 32 + i - 3
                        o = HH + 512 * ((i - 3) % 16)
                        act.wait_ge(S["h_psum"], k + 1)
                        nc.scalar.activation(sb[:, o:o + 512], bank[3][:, :], ACT.Copy).then_inc(S["h_ready"], 1)
                    gg = (i - 9) // 4
                    if (i - 9) % 4 == 0 and 0 <= gg < 4:
                        act.wait_ge(S["pre_gelu"], L * 4 + gg + 1)
                        nc.scalar.activation(sb[:, FF + 2048 * gg:FF + 2048 * gg + 2048], sb[:, HH + 2048 * gg:HH + 2048 * gg + 2048], ACT.Gelu).then_inc(S["gelu_ready"], 1)

            def copy_up(g, e, ab, first=False):
                act.wait_ge(S["up_psum"], 4 * g + ab + 1)
                if ab == 0 and not first:
                    act.wait_ge(S["dn_psum"], g - 1)
                a, b = UPS[ab]
                nc.scalar.activation(at(YY + e * 2 * Y_A + a * Y_A + b * Y_B + 3, [[Y_N, 4], [1, 128]]), bank[ab][:, :], ACT.Copy).then_inc(S["up_copied"], 1)

            for u in range(NLINE // 4):
                act.wait_ge(S["flip_psum"], u + 1)
                nc.scalar.activation(sb[:, MAT + 512 * u:MAT + 512 * u + 512], bank[u % 2][:, :], ACT.Copy).then_inc(S["mats_ready"], 1)
            whole_round(act, "act", 64)
            act.wait_ge(S["pads_ready"], 1)
            for e in range(2):
                for ab in range(4):
                    copy_up(e, e, ab, True)
            with act.Fori(1, 8) as it:
                for e in range(2):
                    for ab in range(4):
                        copy_up(2 * it + e, e, ab)
            whole_round(act, "act", 64)
            for b in range(B):
                for u in range(16):
                    act.wait_ge(S["g3_psum"], 16 * b + u + 1)
                    if u == 0 and b:
                        act.wait_ge(S["xm_psum"], 32)
                    for c in range(2):
                        last = nc.scalar.activation(at(G3 + 2 * u + 64 * c, [[1, 2], [32, 2], [192, 64]]), pat(u % 2, 128 * c, [[256, 2], [64, 2], [1, 64]]), ACT.Copy)
                    last.then_inc(S["g3_ready"], 1)
                for u in range(32):
                    act.wait_ge(S["xm_psum"], 32 * b + u + 1)
                    nc.scalar.activation(at(XM[b] + 520 * (u // 2) + 4 * (u % 2), [[8, 65], [2, 2], [1, 2]]),
                                         pat(2 + u % 2, 0, [[1, 65], [130, 2], [65, 2]]), ACT.Copy).then_inc(S["xm_ready"], 1)

            def keep(c, first=False):
                for g in range(5):
                    n = 16 if g < 4 else 1
                    act.wait_ge(S["t_sum"], 5 * c + g + 1)
                    nc.scalar.activation(at(YM + 16 * 64 * g + 4 * c, [[64, n], [4160, 2], [1, 4]]), at(TT + 128 * g, [[8, n], [4, 2], [1, 4]]),
                                         ACT.Copy).then_inc(S["y3_kept"], 1)

            with act.Fori(0, 16) as it:
                keep(it)
            for u in range(33):
                act.wait_ge(S["ty_psum"], u + 1)
                for j in range(2):
                    b, k0, n = (u // 16, 4 * (u % 16), 4) if u < 32 else (0, 64, 2)
                    step = 1 if u < 32 else 4160
                    last = nc.scalar.activation(at(YT + 4160 * b + k0, [[step, n], [130, 32], [65, 2]], 64 * j, 64 * j + 64),
                                                pat(u % 2, 2 * j, [[128, n], [4, 32], [1, 2]], 0, 64), ACT.Copy)
                last.then_inc(S["ty_ready"], 1)
            for u in range(32):
                act.wait_ge(S["z3_psum"], u + 1)
                if u >= 4:
                    act.wait_ge(S["o_psum"], (u - 4) // 2 + 1)
                nc.scalar.activation(sb[0:65, Z3 + 512 * (u % 4):Z3 + 512 * (u % 4) + 512], bank[u % 4][0:65, :], ACT.Copy).then_inc(S["z3_ready"], 1)

        @block.tensor
        def _(pe):
            mm = nc.tensor.matmul

            pe.wait_ge(S["consts_loaded"], 80)
            pe.wait_ge(S["sel_cast"], 2)
            for L in range(NL):
                whole_round(pe, "pe", 64)
                whole_round(pe, "pe", 64)
                pe.wait_ge(S["xn_ready"], L + 1)
                for u in range(NU):
                    k = L * NU + u
                    if u >= 2:
                        pe.wait_ge(S["g_ready"], k - 1)
                    for j in range(4):
                        n = 4 * u + j
                        last = mm(bank[u % 2][:, 128 * j:128 * j + 128], sb[:, FF + 128 * n:FF + 128 * n + 128], cst(C_FA, 128), start=True, stop=True)
                    last.then_inc(S["g_psum"], 1)
                pe.wait_ge(S["g_ready"], NU * (L + 1))
                for u in range(8):
                    k = L * 8 + u
                    if u >= 2:
                        pe.wait_ge(S["x2_ready"], k - 1)
                    for j in range(4):
                        for b in range(B):
                            for ri in range(2):
                                o = GG + (b * 32 + 4 * u + j) * 128 + 64 * ri
                                last = mm(bank[2 + u % 2][64 * b:64 * b + 64, 100 * j:100 * j + 100], sb[:, o:o + 64],
                                          cst((C_X21, C_X22)[ri], 100), start=ri == 0, stop=ri == 1)
                    last.then_inc(S["x2_psum"], 1)
                for u in range(13):
                    k = L * 13 + u
                    if u >= 2:
                        pe.wait_ge(S["xb_ready"], k - 1)
                    for j in range(min(5, KY - 5 * u)):
                        for ri in range(2):
                            last = mm(bank[4 + u % 2][0:64, 99 * j:99 * j + 99], at(GG + 5 * u + j + 64 * ri, [[128, 64]]),
                                      cst((C_XB1, C_XB2)[ri], 99), start=ri == 0, stop=ri == 1)
                    last.then_inc(S["xb_psum"], 1)
                pe.wait_ge(S["x2_ready"], 8 * (L + 1))
                mm(bank[6][:, 0:32], cst(C_SR, 128), at(X2 + 83, [[100, 32]]), start=True, stop=True)
                mm(bank[6][:, 32:64], cst(C_SI, 128), at(X2 + 99, [[100, 32]]), start=True, stop=True).then_inc(S["sym_psum"], 1)
                pe.wait_ge(S["t_ready"], L + 1)
                pe.wait_ge(S["xb_ready"], 13 * (L + 1))
                for j in range(16):
                    for ri in range(2):
                        last = mm(bank[5][0:64, 0:32], sb[:, TG + (2 * j + ri) * 64:TG + (2 * j + ri) * 64 + 64],
                                  at(X2 + 68 + 16 * ri + j, [[100, 32]]), start=j + ri == 0, stop=j + ri == 16)
                last.then_inc(S["gout_psum"], 1)
                for kx in range(KC):
                    k = L * KC + kx
                    pe.wait_ge(S["z_ready"], k + 1)
                    for f in range(3):
                        for j in range(2):
                            o = ZZ + 3072 * (k % 2) + 1024 * f + 512 * j
                            last = mm(bank[(4, 6)[j]][0:64, :], sb[:, TX + (3 * kx + f) * 64:TX + (3 * kx + f) * 64 + 64], sb[:, o:o + 512],
                                      start=kx + f == 0, stop=kx == KC - 1 and f == 2)
                    last.then_inc(S["z_used"], 1)
                pe.wait_ge(S["attn_ready"], L + 1)
                for c in range(8):
                    last = nc.tensor.transpose(bank[2][:, 64 * c:64 * c + 64], sb[0:64, SC + 128 * c:SC + 128 * c + 128], cst(C_ID, 64, 0, 64))
                last.then_inc(S["attnT_psum"], 1)
                pe.wait_ge(S["mix_ready"], L + 1)
                nc.tensor.transpose(bank[6][0:64, 0:64], sb[0:64, MB:MB + 64], cst(C_ID, 64, 0, 64)).then_inc(S["mixT_psum"], 1)
                pe.wait_ge(S["mixT_ready"], L + 1)
                pe.wait_ge(S["xt_loaded"], 16 * (L + 1))
                for u in range(16):
                    k = L * 16 + u
                    if u >= 2:
                        pe.wait_ge(S["skip_used"], k - 1)
                    for j in range(8):
                        last = mm(bank[4 + u % 2][:, 64 * j:64 * j + 64], at(XT + 8 * u + j, [[128, 128]], 0, 64), sb[0:64, MT:MT + 64], start=True, stop=True)
                    last.then_inc(S["skip_psum"], 1)
                pe.wait_ge(S["attnT_ready"], L + 1)
                pe.wait_ge(S["parts_moved"], 192 * (L + 1))
                seq = [(kp, c) for kp in range(NKP) for c in range(8)]

                def rep(i):
                    kp, c = seq[i]
                    n = 128 if kp < NKP - 1 else 64
                    k = L * len(seq) + i
                    if i >= 3:
                        pe.wait_ge(S["bx_ready"], k - 2)
                    moving = sb[0:96, BP:BP + 3168].bitcast(bf16)
                    moving = bass.AP(tensor=moving.tensor, offset=moving.offset + 128 * kp, ap=[list(moving.ap[0]), [2112, 3], [1, n]])
                    mm(bank[i % 3][:, 0:3 * n], sb[0:96, SEL:SEL + 512].bitcast(bf16)[:, 128 * c:128 * c + 128], moving, start=True, stop=True).then_inc(S["rep_psum"], 1)

                def to_rows(kp):
                    kk = L * NKP + kp
                    pe.wait_ge(S["acc_used"], kk + 1)
                    if kk >= 2:
                        pe.wait_ge(S["sy_ready"], kk - 1)
                    cols = 2 if kp < NKP - 1 else 1
                    for half in range(2):
                        for j in range(cols):
                            o = YR + 192 * (2 * kp + j) + 64 * half
                            last = nc.tensor.transpose(bank[4 + kk % 2][:, 64 * (2 * half + j):64 * (2 * half + j) + 64], sb[0:64, o:o + 128], cst(C_ID, 64, 0, 64))
                    last.then_inc(S["sy_psum"], 1)

                for i in range(3):
                    rep(i)
                for i, (kp, c) in enumerate(seq):
                    k = L * len(seq) + i
                    n = 128 if kp < NKP - 1 else 64
                    kk = L * NKP + kp
                    if c == 0 and kk >= 2:
                        pe.wait_ge(S["acc_used"], kk - 1)
                    if c == 4 and kp:
                        to_rows(kp - 1)
                    pe.wait_ge(S["comb_ready"], k + 1)
                    if i + 3 < len(seq):
                        rep(i + 3)
                    for b in range(B):
                        o = BX + 768 * (k % 4) + 3 * n * b
                        a = AT + 64 * (2 * c + b)
                        im, re = (bank[3 + 3 * (kk % 2)][32 * b:32 * b + 32, n * f:n * f + n] for f in range(2))
                        if c % 2 == 0:
                            both = bank[3 + 3 * (kk % 2)][32 * b:32 * b + 32, 0:2 * n]
                            last = mm(both, sb[:, a:a + 32], sb[:, o + n:o + 3 * n], start=c == 0, stop=False, skip_group_check=True)
                        else:
                            mm(im, sb[:, a:a + 32], sb[:, o + n:o + 2 * n], start=False, stop=c == 7, skip_group_check=True)
                            mm(re, sb[:, a:a + 32], sb[:, o:o + n], start=False, stop=False, skip_group_check=True)
                            last = mm(re, sb[:, a + 32:a + 64], sb[:, o + 2 * n:o + 3 * n], start=False, stop=c == 7, skip_group_check=True)
                    last.then_inc(S["bx_used"], 1)
                to_rows(NKP - 1)
                pe.wait_ge(S["sy_ready"], NKP * (L + 1))
                for u in range(NU + 1):
                    if u < NU:
                        k = L * NU + u
                        if u >= 1:
                            pe.wait_ge(S["zi_ready"], k)
                        for j in range(4):
                            o = SY + (4 * u + j) * 66
                            last = mm(bank[4][0:66, 128 * j:128 * j + 128], sb[:, o:o + 66], cst(C_E, 128), start=True, stop=True)
                        last.then_inc(S["zi_psum"], 1)
                    if u >= 1:
                        k = L * NU + u - 1
                        pe.wait_ge(S["zi_ready"], k + 1)
                        if u >= 2:
                            pe.wait_ge(S["p_used"], k)
                        for j in range(4):
                            o = ZC + 512 * ((u - 1) % 2) + 128 * j
                            last = mm(bank[5][:, 128 * j:128 * j + 128], sb[0:66, o:o + 128], cst(C_D, 128, 0, 66), start=True, stop=True)
                        last.then_inc(S["p_psum"], 1)
                whole_round(pe, "pe", 64)
                for i in range(38):
                    if i < 32:
                        k = L * 32 + i
                        if i % 4 == 0:
                            if i < 16:
                                pe.wait_ge(S["an_ready"], 4 * L + i // 4 + 1)
                            else:
                                pe.wait_ge(S["gelu_ready"], 4 * L + (i - 16) // 4 + 1)
                        if k >= 2:
                            pe.wait_ge(S["ga_ready"], k - 1)
                        for j in range(4):
                            o = FF + 512 * (i % 16) + 128 * j
                            last = mm(bank[(0, 4)[k % 2]][:, 128 * j:128 * j + 128], sb[:, o:o + 128], cst(C_FA, 128), start=True, stop=True)
                        last.then_inc(S["ga_psum"], 1)
                    for r in round_at(i):
                        pe_mean(pe, 16)
                    if 0 <= i - 1 < 32:
                        k = L * 32 + i - 1
                        pe.wait_ge(S["ga_ready"], k + 1)
                        if k >= 2:
                            pe.wait_ge(S["gb_used"], k - 1)
                        for j in range(4):
                            o = GR + 768 * (k % 3) + 192 * j
                            dst = bank[(1, 5)[k % 2]][:, 66 * j:66 * j + 66]
                            mm(dst, sb[:, o:o + 128], cst(C_FB1, 66), start=True, stop=False)
                            last = mm(dst, sb[:, o + 64:o + 192], cst(C_FB2, 66), start=False, stop=True)
                        last.then_inc(S["gb_psum"], 1)
                    for r in round_at(i):
                        pe_var(pe, 16)
                    if 0 <= i - 2 < 32:
                        k = L * 32 + i - 2
                        pe.wait_ge(S["sp_ready"], k + 1)
                        if k >= 2:
                            pe.wait_ge(S["zc_ready"], k - 1)
                        for j in range(4):
                            o = SP + 264 * (k % 2) + 66 * j
                            last = mm(bank[(2, 6)[k % 2]][0:66, 128 * j:128 * j + 128], sb[:, o:o + 66], cst(C_E, 128), start=True, stop=True)
                        last.then_inc(S["zc_psum"], 1)
                    if 0 <= i - 3 < 32:
                        k = L * 32 + i - 3
                        pe.wait_ge(S["zc_ready"], k + 1)
                        if k >= 1:
                            pe.wait_ge(S["h_ready"], k)
                        for j in range(4):
                            o = ZM + 512 * (k % 2) + 128 * j
                            last = mm(bank[3][:, 128 * j:128 * j + 128], sb[0:66, o:o + 128], cst(C_D, 128, 0, 66), start=True, stop=True)
                        last.then_inc(S["h_psum"], 1)
            def up(g, e, first=False):
                for ab, (a, b) in enumerate(UPS):
                    if not first:
                        pe.wait_ge(S["y_ready"], 4 * g + ab - 3)
                    shifts = range(-3 + b, 4)
                    for dq in shifts:
                        m = MAT + ((a * 2 + b) * 7 + dq + 3) * 128
                        last = mm(bank[ab][:, :], sb[:, m:m + 128], at(XP + 4 * NP_ * g + 3 + dq, [[NP_, 4], [1, 128]]), start=dq == shifts[0], stop=dq == 3)
                    last.then_inc(S["up_psum"], 1)

            def down(g, e, first=False):
                pe.wait_ge(S["y_ready"], 4 * g + 4)
                if not first:
                    pe.wait_ge(S["x2_done"], g - 1)
                for a in range(2):
                    for j in range(TAPS):
                        b = (j + 1) % 2
                        dq = (j - 5 - b) // 2
                        m = MAT + (28 + 12 * a + j) * 128
                        last = mm(bank[4 + e][:, :], sb[:, m:m + 128], at(YY + e * 2 * Y_A + a * Y_A + b * Y_B + 3 + dq, [[Y_N, 4], [1, 128]]),
                                  start=a + j == 0, stop=a == 1 and j == TAPS - 1)
                last.then_inc(S["dn_psum"], 1)

            pe.wait_ge(S["mats_loaded"], 16)
            pe.wait_ge(S["k_loaded"], 16)
            for u in range(NLINE // 4):
                if u >= 2:
                    pe.wait_ge(S["mats_ready"], u - 1)
                mm(bank[u % 2][:, :], sb[:, CK + K_FLIP:CK + K_FLIP + 128], sb[:, MAT + 512 * u:MAT + 512 * u + 512], start=True, stop=True).then_inc(S["flip_psum"], 1)
            whole_round(pe, "pe", 64)
            pe.wait_ge(S["mats_ready"], 13)
            pe.wait_ge(S["pads_ready"], 1)
            pe.wait_ge(S["xp2_ready"], 1)
            up(0, 0, True)
            up(1, 1)
            down(0, 0, True)
            up(2, 0)
            down(1, 1, True)
            with pe.Fori(1, 7) as it:
                up(2 * it + 1, 1)
                down(2 * it, 0)
                up(2 * it + 2, 0)
                down(2 * it + 1, 1)
            up(15, 1)
            down(14, 0)
            down(15, 1)
            ck = lambda col, n, hi=128: sb[0:hi, CK + col:CK + col + n]
            whole_round(pe, "pe", 64)
            pe.wait_ge(S["k_loaded"], 16)
            pe.wait_ge(S["gn_ready"], 3)
            for b in range(B):
                for u in range(16):
                    if 16 * b + u >= 2:
                        pe.wait_ge(S["g3_ready"], 16 * b + u - 1)
                    for j in range(2):
                        n = 32 * b + 2 * u + j
                        last = mm(bank[u % 2][:, 256 * j:256 * j + 256], sb[:, XA + 128 * n:XA + 128 * n + 128], ck(K_FA, 256), start=True, stop=True)
                    last.then_inc(S["g3_psum"], 1)
                pe.wait_ge(S["g3_neg"], b + 1)
                for u in range(32):
                    k = 32 * b + u
                    if k >= 2:
                        pe.wait_ge(S["xm_ready"], k - 1)
                    for j in range(2):
                        o = G3 + 192 * (2 * u + j)
                        for s in range(2):
                            last = mm(bank[2 + u % 2][:, 130 * j:130 * j + 130], sb[:, o + 64 * s:o + 64 * s + 128],
                                      ck(K_FB + (65, 0)[s], 130), start=s == 0, stop=s == 1)
                    last.then_inc(S["xm_psum"], 1)

            COPIES = 3

            def modes_chunk(c, k, first=False):
                pe.wait_ge(S["xq_ready"], c + 1)
                pe.wait_ge(S[f"w_loaded{k}"], 32 * (c - k) + 64)
                for g in range(5):
                    if not first:
                        pe.wait_ge(S["t_sum"], 5 * c + g - 4)
                    for j in range(16 if g < 4 else 1):
                        kx = 16 * g + j
                        n = min(COPIES, 16 - j)
                        last = mm(bank[g][:, 32 * j:32 * (j + n)], at(WB[k] + kx, [[65, 128]]), at(XQ + 2080 * k + 32 * kx, [[0, n], [1, 32]]), start=True, stop=True)
                    last.then_inc(S["y3_psum"], 1)

            pe.wait_ge(S["xm_ready"], 64)
            modes_chunk(0, 0, True)
            modes_chunk(1, 1)
            with pe.Fori(1, 8) as it:
                modes_chunk(2 * it, 0)
                modes_chunk(2 * it + 1, 1)
            pe.wait_ge(S["y3_kept"], 80)
            for u in range(33):
                if u >= 2:
                    pe.wait_ge(S["ty_ready"], u - 1)
                for j in range(4 if u < 32 else 2):
                    o = 4160 * (u // 16) + 64 * (4 * (u % 16) + j) if u < 32 else 4160 * j + 64 * 64
                    last = nc.tensor.transpose(bank[u % 2][0:64, 128 * j:128 * j + 128], sb[:, YM + o:YM + o + 64], ck(K_ID, 128))
                last.then_inc(S["ty_psum"], 1)
            pe.wait_ge(S["ty_ready"], 33)
            for u in range(NU + 1):
                for e in range(2):
                    if u < NU:
                        k = 2 * u + e
                        if k >= 4:
                            pe.wait_ge(S["z3_ready"], k - 3)
                        for j in range(2):
                            o = YT + 130 * (4 * u + 2 * e + j)
                            dst = bank[k % 4][0:65, 256 * j:256 * j + 256]
                            mm(dst, sb[:, o:o + 65], ck(K_E, 256), start=True, stop=False)
                            last = mm(dst, sb[:, o + 65:o + 130], ck(K_E + 256, 256), start=False, stop=True)
                        last.then_inc(S["z3_psum"], 1)
                if u >= 1:
                    pe.wait_ge(S["z3_ready"], 2 * u)
                    if u >= 3:
                        pe.wait_ge(S["o_ready"], u - 2)
                    for j in range(4):
                        o = Z3 + 512 * ((2 * u - 2 + j // 2) % 4) + 256 * (j % 2)
                        dst = bank[4 + u % 2][:, 128 * j:128 * j + 128]
                        mm(dst, sb[0:65, o:o + 128], ck(K_DC, 128, 65), start=True, stop=False)
                        last = mm(dst, sb[0:65, o + 128:o + 256], ck(K_DS, 128, 65), start=False, stop=True)
                    last.then_inc(S["o_psum"], 1)

        @block.vector
        def _(dve):
            v = nc.vector

            def L_(ins):
                link(ins, dve, "dve")

            v.memset(sb[:, EPSC:EPSC + 1], EPS).then_inc(S["sel_cast"], 1)
            dve.wait_ge(S["x_loaded"], 64)
            dve.wait_ge(S["consts_loaded"], 80)
            for L in range(NL):
                group_norm(dve, L)
                image_stats(dve, XA, 0, NIMG)
                whole_round(dve, "dve", 64)
                affine(dve, L, P_G, P_B, 64, S0, C0)
                scale_images(XA, FF, 0, NIMG, S0, C0).then_inc(S["xn_ready"], 1)
                row = lambda p: sb[:, PR + L * PROW + p:PR + L * PROW + p + 32]
                R = lambda r: sb[:, r:r + 32]
                L_(v.scalar_tensor_tensor(R(R_GO), row(P_QS), 64.0, row(P_KS), mult, mult))
                for r, w00, ws, bs in ((R_Q0, P_Q00, P_QS, P_BQ), (R_K0, P_K00, P_KS, P_BK)):
                    L_(v.tensor_tensor(R(r), row(w00), row(ws), add))
                    L_(v.scalar_tensor_tensor(R(r), R(r), par(L, P_B), row(bs), mult, add))
                L_(v.scalar_tensor_tensor(R(R_CT), R(R_Q0), 64.0, R(R_K0), mult, mult))
                L_(v.tensor_tensor(R(R_SS), row(P_PS), row(P_VS), mult))
                L_(v.tensor_tensor(R(R_TMP), row(P_P00), row(P_PS), add))
                L_(v.tensor_tensor(R(R_TMP), R(R_TMP), row(P_BV), mult))
                L_(v.tensor_reduce(sb[:, D0:D0 + 1], R(R_TMP), AX.X, add))
                L_(v.tensor_tensor(sb[:, D0:D0 + 1], sb[:, D0:D0 + 1], par(L, P_BP), add))
                dve.wait_ge(S["sym_psum"], L + 1)
                L_(v.tensor_copy(at(X2 + 83, [[100, 32], [16, 2]]), pat(6, 0, [[1, 32], [32, 2]])))
                L_(v.tensor_scalar(at(X2 + 51, [[100, 32]]), at(X2 + 51, [[100, 32]]), cst(C_MASK + 1, 1), None, mult))
                L_(v.tensor_tensor(at(X2 + 17, [[100, 32]]), at(X2 + 51, [[100, 32]]), at(X2, [[100, 32]]), sub))
                L_(v.tensor_tensor(at(X2 + 34, [[100, 32]]), at(X2 + 51, [[100, 32]]), at(X2, [[100, 32]]), add))
                dve.wait_ge(S["zero_t"], L + 1)
                for b in range(B):
                    p = dict(lo=64 * b, hi=64 * b + 64)
                    for f, src, scale in ((0, 34, 1.0), (1, 51, 1.0), (2, 0, -1.0)):
                        v.tensor_scalar(at(TX + 64 * f + 32 * b, [[192, KC], [1, 32]], **p), at(X2 + src, [[1, KC], [100, 32]], **p), scale, None, mult)
                    for ri in range(2):
                        v.tensor_scalar(at(TG + 64 * ri + 32 * b, [[128, 15], [1, 32]], **p), at(X2 + 68 + 16 * ri, [[1, 15], [100, 32]], **p), 2.0, None, mult)
                        last = v.tensor_copy(at(TG + 64 * ri + 32 * b + 15 * 128, [[1, 32]], **p), at(X2 + 83 + 16 * ri, [[100, 32]], **p))
                last.then_inc(S["t_ready"], 1)
                dve.wait_ge(S["a_psum"], L + 1)
                dve.wait_ge(S["xb_stored"], 16 * (L + 1))
                for kx in range(KC):
                    k = L * KC + kx
                    if kx >= 2:
                        dve.wait_ge(S["z_used"], k - 1)
                    for f in range(3):
                        last = v.tensor_tensor(at(ZZ + 3072 * (k % 2) + 1024 * f, [[32, 32], [1, 32]]), at(X2 + kx + 17 * f, [[0, 32], [100, 32]]),
                                               pat(kx // 5, 96 * (kx % 5) + 32 * f, [[1, 32], [0, 32]]), mult)
                    last.then_inc(S["z_ready"], 1)
                hs, h0, s0 = [[32, 32], [1, 32]], [[1, 32], [0, 32]], [[0, 32], [1, 32]]
                q = lambda off, dims: at(off, dims, 0, 64)
                dve.wait_ge(S["gout_psum"], L + 1)
                dve.wait_ge(S["z_used"], KC * (L + 1))
                L_(v.tensor_tensor(q(TP, hs), pat(5, 0, s0, 0, 64), q(R_GO, h0), mult))
                L_(v.tensor_tensor(q(TP, hs), q(TP, hs), q(R_CT, h0), add))
                for j in range(2):
                    last = v.tensor_tensor(sb[0:64, SC + 512 * j:SC + 512 * j + 512], bank[(4, 6)[j]][0:64, :], sb[0:64, TP + 512 * j:TP + 512 * j + 512], add)
                L_(last)
                L_(v.tensor_reduce(sb[0:64, DV:DV + 32], q(SC, hs), AX.X, amax))
                v.tensor_tensor(q(SC, hs), q(SC, hs), q(DV, h0), sub).then_inc(S["exp_in"], 1)
                dve.wait_ge(S["exp_ready"], L + 1)
                L_(v.tensor_reduce(sb[0:64, DV:DV + 32], q(SC, hs), AX.X, add))
                L_(v.reciprocal(sb[0:64, DV:DV + 32], sb[0:64, DV:DV + 32]))
                v.tensor_tensor(q(SC, hs), q(SC, hs), q(DV, h0), mult).then_inc(S["attn_ready"], 1)
                dve.wait_ge(S["attn_ready"], L + 1)
                L_(v.tensor_tensor(q(TP, hs), q(SC, hs), q(R_SS, h0), mult))
                for b in range(B):
                    last = v.tensor_reduce(sb[32 * b:32 * b + 32, MB + 32 * b:MB + 32 * b + 32], at(TP, [[1, 32], [32, 32]], 32 * b, 32 * b + 32), AX.X, add)
                last.then_inc(S["mix_ready"], 1)
                dve.wait_ge(S["attnT_psum"], L + 1)
                a2 = [[64, 16], [1, 32]]
                v.tensor_copy(at(AT, a2), pat(2, 0, [[32, 16], [1, 32]]))
                v.tensor_scalar(at(AT + 32, a2), pat(2, 0, [[32, 16], [1, 32]]), -1.0, None, mult).then_inc(S["attnT_ready"], 1)
                dve.wait_ge(S["mixT_psum"], L + 1)
                v.tensor_copy(sb[0:64, MT:MT + 64], bank[6][0:64, 0:64]).then_inc(S["mixT_ready"], 1)
                dve.wait_ge(S["xn_stored"], 16 * (L + 1))
                for u in range(16):
                    k = L * 16 + u
                    dve.wait_ge(S["skip_psum"], k + 1)
                    last = v.scalar_tensor_tensor(at(FF + 8 * u, [[1, 8], [128, 64]]), pat(4 + u % 2, 0, [[64, 8], [1, 64]]), sb[:, D0:D0 + 1],
                                                  at(XA + 8 * u, [[1, 8], [128, 64]]), add, add)
                    last.then_inc(S["skip_used"], 1)
                dve.wait_ge(S["skip_used"], 16 * (L + 1))
                v.memset(sb[0:1, R_TMP:R_TMP + 1], 0.0).then_inc(S["skip_done"], 1)
                for kp in range(NKP):
                    n = 128 if kp < NKP - 1 else 64
                    kk = L * NKP + kp
                    dve.wait_ge(S[f"xc_loaded{kk % 2}"], 32 * (kk // 2 + 1))
                    for c in range(8):
                        k = kk * 8 + c
                        dve.wait_ge(S["rep_psum"], k + 1)
                        if k >= 4:
                            dve.wait_ge(S["bx_used"], k - 3)
                        v.tensor_tensor(at(BX + 768 * (k % 4), [[3 * n, 2], [1, 3 * n]]), pat((kp * 8 + c) % 3, 0, [[0, 2], [1, 3 * n]]),
                                        at(XC + 768 * (kk % 2), [[384, 2], [1, 3 * n]]), mult).then_inc(S["bx_ready"], 1)
                for u in range(NU):
                    k = L * NU + u
                    dve.wait_ge(S["p_psum"], k + 1)
                    v.tensor_tensor(sb[:, XA + 512 * u:XA + 512 * u + 512], bank[5][:, :], sb[:, FF + 512 * u:FF + 512 * u + 512], add).then_inc(S["p_used"], 1)
                dve.wait_ge(S["p_used"], NU * (L + 1))
                image_stats(dve, XA, 0, NIMG)
                whole_round(dve, "dve", 64)
                affine(dve, L, P_G + 1, P_B + 1, 64, S1, C1)
                L_(v.tensor_tensor(sb[:, QQ:QQ + 64], bank[7][:, VAR:VAR + 64], sb[:, S1:S1 + 64], mult))
                v.tensor_tensor(sb[:, QQ:QQ + 64], sb[:, QQ:QQ + 64], sb[:, S1:S1 + 64], mult).then_inc(S["att_var"], 1)
                dve.wait_ge(S["att_std"], L + 1)
                L_(v.reciprocal(sb[:, DV:DV + 64], sb[:, DV:DV + 64]))
                L_(v.tensor_tensor(sb[:, S2:S2 + 64], sb[:, DV:DV + 64], sb[:, S1:S1 + 64], mult))
                L_(v.tensor_scalar(sb[:, S2:S2 + 64], sb[:, S2:S2 + 64], par(L, P_G + 2), None, mult))
                L_(v.tensor_tensor(sb[:, C2:C2 + 64], bank[7][:, MEAN:MEAN + 64], sb[:, S2:S2 + 64], mult))
                L_(v.tensor_scalar(sb[:, C2:C2 + 64], sb[:, C2:C2 + 64], -1.0, par(L, P_B + 2), mult, add))
                wm = lambda j, ri: WM + (2 * L + j) * 66 + 33 * ri
                for j in range(2):
                    v.tensor_scalar(sb[:, WI + 66 * j:WI + 66 * j + 33], sb[:, wm(j, 1):wm(j, 1) + 33], -1.0, None, mult)
                    L_(v.tensor_copy(sb[:, WI + 66 * j + 33:WI + 66 * j + 66], sb[:, wm(j, 1):wm(j, 1) + 33]))
                for g in range(4):
                    scale_images(XA, FF, 16 * g, 16 * g + 16, S2 + 16 * g, C2 + 16 * g).then_inc(S["an_ready"], 1)
                for i in range(38):
                    for kind, gg in round_at(i):
                        dve_var_in(dve, 16, ST + 96 * (gg % 2) if kind == "first" else ST + 192)
                    if 0 <= i - 1 < 32:
                        k = L * 32 + i - 1
                        j = (i - 1) // 16
                        bk = (1, 5)[k % 2]
                        dve.wait_ge(S["gb_psum"], k + 1)
                        if k >= 2:
                            dve.wait_ge(S["sp_ready"], k - 1)
                        out = [[66, 4], [33, 2], [1, 33]]
                        v.tensor_tensor(at(T1 + 264 * (k % 2), out), pat(bk, 0, out), at(wm(j, 0), [[0, 4], [0, 2], [1, 33]]), mult)
                        v.tensor_tensor(at(T2 + 264 * (k % 2), out), pat(bk, 33, [[66, 4], [-33, 2], [1, 33]]),
                                        at(WI + 66 * j, [[0, 4], [33, 2], [1, 33]]), mult).then_inc(S["gb_used"], 1)
                    for kind, gg in round_at(i):
                        dve_rstd(dve, 16)
                        j, g = gg // 4, gg % 4
                        h, f, a = HH + 2048 * g, FF + 2048 * g, XA + 2048 * g
                        if kind == "first":
                            affine(dve, L, P_G + 3 + j, P_B + 3 + j, 16, S3, C3, par(L, (P_BM0, P_BM1)[j]))
                            L_(scale_images(h, h, 0, 16, S3, C3))
                            last = v.scalar_tensor_tensor(sb[:, h:h + 2048], sb[:, f:f + 2048], par(L, (P_M0S, P_M1S)[j]), sb[:, h:h + 2048], mult, add)
                            if j == 0:
                                last.then_inc(S["pre_gelu"], 1)
                            else:
                                L_(last)
                                image_stats(dve, h, 0, 16, ST + 192)
                                dve_sums(dve, 16, ST + 192)
                        else:
                            affine(dve, L, P_G + 5, P_B + 5, 16, S5, C5)
                            L_(v.tensor_tensor(sb[:, C5:C5 + 16], sb[:, C5:C5 + 16], sb[:, C1 + 16 * g:C1 + 16 * g + 16], add))
                            L_(scale_images(h, h, 0, 16, S5, C5))
                            for n in range(16):
                                last = v.scalar_tensor_tensor(sb[:, h + 128 * n:h + 128 * n + 128], sb[:, a + 128 * n:a + 128 * n + 128],
                                                              sb[:, S1 + 16 * g + n:S1 + 16 * g + n + 1], sb[:, h + 128 * n:h + 128 * n + 128], mult, add)
                            L_(last)
                            x = XR + 2048 * g
                            v.tensor_tensor(sb[:, x:x + 2048], sb[:, x:x + 2048], sb[:, h:h + 2048], add).then_inc(S["x_done"], 1)
                    if 0 <= i - 3 < 32:
                        u = i - 3
                        dve.wait_ge(S["h_ready"], L * 32 + u + 1)
                        st = ST + 96 * (u // 4 % 2)
                        for n in range(4):
                            o = HH + 512 * (u % 16) + 128 * n
                            last = v.bn_stats(sb[:, st + 6 * (4 * (u % 4) + n):st + 6 * (4 * (u % 4) + n) + 6], sb[:, o:o + 128])
                        if u % 4 == 3:
                            L_(last)
                            dve_sums(dve, 16, st)

            def sloped(g, e, ab):
                dve.wait_ge(S["up_copied"], 4 * g + ab + 1)
                a, b = UPS[ab]
                y = at(YY + e * 2 * Y_A + a * Y_A + b * Y_B + 3, [[Y_N, 4], [1, 128]])
                v.scalar_tensor_tensor(y, pat(ab, 0, [[128, 4], [1, 128]]), SLOPE, y, mult, amax).then_inc(S["y_ready"], 1)

            def residual(g, e):
                dve.wait_ge(S["dn_psum"], g + 1)
                x = at(XR + 512 * g, [[1, 512]])
                v.tensor_tensor(x, bank[4 + e][:, :], x, add).then_inc(S["x2_done"], 1)

            group_norm(dve, 2)
            for ab in range(4):
                sloped(0, 0, ab)
            for ab in range(4):
                sloped(1, 1, ab)
            residual(0, 0)
            with dve.Fori(1, 8) as it:
                for ab in range(4):
                    sloped(2 * it, 0, ab)
                residual(2 * it - 1, 1)
                for ab in range(4):
                    sloped(2 * it + 1, 1, ab)
                residual(2 * it, 0)
            residual(15, 1)
            group_norm(dve, 3)
            for b in range(B):
                dve.wait_ge(S["g3_ready"], 16 * b + 16)
                v.tensor_scalar(at(G3 + 128, [[192, 64], [1, 64]]), at(G3, [[192, 64], [1, 64]]), -1.0, None, mult).then_inc(S["g3_neg"], 1)

            def own_rows(c, first=False):
                for g in range(5):
                    n = 16 if g < 4 else 1
                    dve.wait_ge(S["y3_psum"], 5 * c + g + 1)
                    if not first:
                        dve.wait_ge(S["y3_kept"], 5 * c + g - 4)
                    t = at(TT + 128 * g, [[8, n], [1, 8]])
                    row = lambda e: sb[:, CK + K_ROW + e:CK + K_ROW + e + 1]
                    col = lambda e: pat(g, 8 * e, [[32, n], [1, 8]])
                    v.tensor_scalar(t, col(0), row(0), None, mult).then_inc(S["t_part"], 1)
                    dve.wait_ge(S["t_part"], 15 * c + 3 * g + 1)
                    v.scalar_tensor_tensor(t, col(1), row(1), t, mult, add).then_inc(S["t_part"], 1)
                    dve.wait_ge(S["t_part"], 15 * c + 3 * g + 2)
                    v.scalar_tensor_tensor(t, col(2), row(2), t, mult, add).then_inc(S["t_part"], 1)
                    dve.wait_ge(S["t_part"], 15 * c + 3 * g + 3)
                    v.scalar_tensor_tensor(t, col(3), row(3), t, mult, add).then_inc(S["t_sum"], 1)

            own_rows(0, True)
            with dve.Fori(1, 16) as it:
                own_rows(it)
            for u in range(NU):
                dve.wait_ge(S["o_psum"], u + 1)
                dve.wait_ge(S[f"xo_loaded{u % 4}"], 16 * (u // 4 + 1))
                if u >= 2:
                    dve.wait_ge(S[f"o_stored{u % 2}"], 16 * (u // 2))
                v.tensor_tensor(sb[:, OO + 512 * (u % 2):OO + 512 * (u % 2) + 512], bank[4 + (u + 1) % 2][:, :], sb[:, XO + 512 * (u % 4):XO + 512 * (u % 4) + 512], add).then_inc(S["o_ready"], 1)


def kernel(**inputs):
    import concourse.bacc as _bacc
    from concourse.bass_utils import run_bass_kernel_spmd as _run

    a = {k: np.asarray(v) for k, v in inputs.items()}
    f32 = np.float32
    zero, one = np.zeros(32, f32), np.ones(1, f32)

    def modes(w, columns):
        out = np.zeros((w.shape[0], KY, columns, 2), f32)
        r = w.shape[1] // 2
        out[:, :r, :w.shape[2]], out[:, KY - r:, :w.shape[2]] = w[:, :r], w[:, r:]
        return out

    def flipped(w):
        return w[:, -np.arange(KY) % KY, 0]

    def quarters(w):
        out = np.zeros((NH, 2, 4 * KQ, KY), f32)
        out[:, :, :w.shape[2]] = w.transpose(0, 3, 2, 1)
        return out.reshape(NH, 2, 4, -1).transpose(2, 0, 1, 3).reshape(4 * NH, -1)

    l0 = lambda n: a["L0_conv_" + n]
    l1 = lambda n: a["L1_conv_" + n]
    join = lambda w: np.concatenate([w[0], w[1]], axis=-3)
    layers = [
        dict(q=join(l0("wQ"))[0], k=join(l0("wK"))[0], v=join(l0("wV"))[0], p=join(l0("wP"))[:, 0], m=(join(l0("wM0"))[0], join(l0("wM1"))[0]),
             g=l0("norm_g"), b=l0("norm_b"), one=(l0("wM0s")[0], l0("wM1s")[0], l0("bM0s"), l0("bM1s"), l0("bPs")),
             rows=(l0("bQs"), l0("bKs"), l0("wQs")[:, 0], l0("wKs")[:, 0], l0("wPs")[0], l0("bVs"), l0("wVs")[:, 0])),
        dict(q=l1("Qcw")[0], k=l1("Kcw")[0], v=l1("Vcw")[0], p=l1("Pcw")[:, 0], m=(l1("m0cw")[0], l1("m1cw")[0]),
             g=np.concatenate([l1("norm1_w"), l1("attn_w"), l1("norm2_w"), one, one, l1("mon_w")]),
             b=np.concatenate([l1("norm1_b"), l1("attn_b"), l1("norm2_b"), zero[:2], l1("mon_b")]),
             one=(l1("m0sw")[0], l1("m1sw")[0], zero[:1], zero[:1], zero[:1]),
             rows=(zero, zero, l1("Qsw")[:, 0], l1("Ksw")[:, 0], l1("Psw")[0], zero, l1("Vsw")[:, 0])),
    ]
    prow, vsps, qk, qkf, pw, vw, vf, wm = ([] for _ in range(8))
    for y in layers:
        q, k, v, p = modes(y["q"], KC), modes(y["k"], KC), modes(y["v"], KC), modes(y["p"], KX)
        prow.append(np.concatenate([y["g"], y["b"], *y["one"], zero[:15], *y["rows"], q[:, 0, 0, 0], k[:, 0, 0, 0], p[:, 0, 0, 0]]))
        vsps += [y["rows"][6], y["rows"][4]]
        both = lambda w: np.concatenate([w, w])
        qk.append(both(np.concatenate([w.transpose(1, 3, 2, 0).reshape(KY, -1) for w in (q, k)], axis=1)))
        qkf.append(both(np.concatenate([flipped(w).transpose(1, 2, 0).reshape(KY, -1) for w in (q, k)], axis=1)))
        pw.append(quarters(p))
        vw.append(quarters(v))
        vf.append(flipped(v).transpose(0, 2, 1).reshape(NH, -1))
        wm.append(np.stack([both(modes(w, KX)[0].transpose(0, 2, 1).reshape(KY, -1)) for w in y["m"]]))
    cst, cst3, sel = shape_constants()
    arrays = {"x": a["x"].reshape(NIMG, H, W), "cst": cst, "cst3": cst3, "w3r": a["L3_conv_weight_real"], "w3i": a["L3_conv_weight_imag"],
              "bias": np.tile(a["L2_conv_bias"].reshape(1, T), (1, B)), "taps": np.concatenate([a["L2_conv_up_filter"].reshape(1, -1), a["L2_conv_dn_filter"].reshape(1, -1)], axis=1),
              "sel": sel, "prow": np.stack(prow), "vsps": np.tile(np.stack(vsps, axis=1), (4, 1)), "qk": np.stack(qk),
              "qkf": np.stack(qkf), "pw": np.stack(pw), "vw": np.stack(vw), "vf": np.stack(vf), "wm": np.stack(wm)}
    arrays = {k: np.ascontiguousarray(v) for k, v in arrays.items()}
    nc = _bacc.Bacc("TRN2", target_bir_lowering=False, num_devices=1)
    io = {k: nc.dram_tensor("in_" + k, v.shape, mybir.dt.from_np(v.dtype), kind="ExternalInput").ap() for k, v in arrays.items()}
    io["out"] = nc.dram_tensor("out_0", (NIMG, H, W), mybir.dt.float32, kind="ExternalOutput").ap()
    build(nc, io)
    r = _run(nc, [{"in_" + k: v for k, v in arrays.items()}], core_ids=[0])
    return r.results[0]["out_0"].reshape(B, T, H, W)
```

```python
import numpy as np
import concourse.bass as bass
from concourse import mybir
from contextlib import ExitStack

NIMG, B, T, H, W = 64, 2, 32, 128, 128
NH = 32
KY, KX, KC = 64, 33, 17
KQ = -(-KX // 4)
EPS = 1e-5
SLOPE, GAIN = 0.2, float(np.sqrt(2.0))
TAPS = 12

P_G, P_B, P_M0S, P_M1S, P_BM0, P_BM1, P_BP = 0, 6, 12, 13, 14, 15, 16
P_BQ, P_BK, P_QS, P_KS, P_PS, P_BV, P_VS, P_Q00, P_K00, P_P00 = range(32, 352, 32)
PROW = 352

C_FA, C_FB1, C_FB2, C_XB1, C_XB2 = 0, 128, 194, 260, 359
C_X21, C_X22, C_E, C_D, C_ID, C_ONE = 458, 558, 658, 786, 914, 1042
C_SR, C_SI, C_MASK = 1170, 1298, 1426
NCONST = 1428
K_FA, K_FB, K_E, K_DC, K_DS, K_ID, K_ROW, K_FLIP = 0, 256, 451, 963, 1091, 1219, 1347, 1351
NCONST3 = 1479


def shape_constants():
    pix = np.arange(128)
    ky = np.r_[0:32, -32:0]
    kx = np.arange(KX)
    ay = 2 * np.pi * np.outer(pix, ky) / 128
    ax = 2 * np.pi * np.outer(pix, kx) / 128
    t = np.zeros((128, NCONST))
    t[:, C_FA:C_FA + 64], t[:, C_FA + 64:C_FA + 128] = np.cos(ay) / 128, -np.sin(ay) / 128
    c, s = np.cos(ax) / 128, np.sin(ax) / 128
    t[:, C_FB1:C_FB1 + 66] = np.c_[c, -s]
    t[:, C_FB2:C_FB2 + 66] = np.c_[s, c]
    re, im = (c, s), (-s, c)
    for n, at in ((0, C_XB1), (1, C_XB2)):
        t[:, at:at + 99] = np.c_[re[n], im[n] - re[n], re[n] + im[n]]
    for n, at in ((0, C_X21), (1, C_X22)):
        r, i = re[n], im[n]
        t[:, at:at + 100] = np.c_[r[:, :KC], (i - r)[:, :KC], (r + i)[:, :KC], i[:, :KC], r[:, KC:], i[:, KC:]]
    t[:, C_E:C_E + 128] = np.r_[np.cos(ay).T, -np.sin(ay).T]
    twice = np.where(kx == 0, 1, 2)[:, None]
    t[:66, C_D:C_D + 128] = np.r_[twice * np.cos(ax).T, -twice * np.sin(ax).T]
    t[:, C_ID:C_ID + 128] = np.eye(128)
    t[:, C_ONE:C_ONE + 128] = 1 / 256
    flip = np.zeros((64, 64))
    flip[np.arange(64), -np.arange(64) % 64] = 1
    for at, sign in ((C_SR, 1), (C_SI, -1)):
        half = (np.eye(64) + sign * flip) / 2
        t[:64, at:at + 64] = half
        t[64:, at + 64:at + 128] = half
    t[:, C_MASK] = np.arange(128) % 64 != 0
    t[:, C_MASK + 1] = np.arange(128) % 64 != 32
    ky, kx = np.arange(128) - 64, 64 - np.arange(65)
    ay, ax = 2 * np.pi * np.outer(pix, ky) / 128, 2 * np.pi * np.outer(pix, kx) / 128
    t3 = np.zeros((128, NCONST3))
    t3[:, K_FA:K_FA + 256] = np.c_[np.cos(ay), -np.sin(ay)] / 128
    t3[:, K_FB:K_FB + 195] = np.c_[np.sin(ax), np.cos(ax), -np.sin(ax)] / 128
    back = np.stack([np.c_[np.cos(ay).T, np.sin(ay).T], np.c_[-np.sin(ay).T, np.cos(ay).T]])
    back = back.reshape(2, 2, 16, 2, 2, 256)
    t3[:, K_E:K_E + 512] = back.transpose(3, 2, 1, 0, 4, 5).reshape(128, 512)
    t3[:, K_ID:K_ID + 128] = np.eye(128)
    t3[:, K_ROW:K_ROW + 4] = np.arange(128)[:, None] % 4 == np.arange(4)
    t3[:, K_FLIP:K_FLIP + 128] = np.eye(128)[::-1]
    twice = np.where(kx % 64 == 0, 1, 2)[:, None]
    t3[:65, K_DC:K_DC + 128], t3[:65, K_DS:K_DS + 128] = twice * np.cos(ax).T, -twice * np.sin(ax).T
    sel = np.zeros((3, 32, 8, 4, 32))
    for h in range(32):
        sel[:, h, h // 4, h % 4, :] = 1
    return t.astype(np.float32), t3.astype(np.float32), sel.reshape(96, 1024).astype(np.float32)


def build(nc, io):
    f32, bf16, f32r = mybir.dt.float32, mybir.dt.bfloat16, mybir.dt.float32r
    ALU, ACT, AX = mybir.AluOpType, mybir.ActivationFunctionType, mybir.AxisListType
    mult, add, sub, amax = ALU.mult, ALU.add, ALU.subtract, ALU.max
    NL = 2
    NLINE = 52
    ctx = ExitStack()
    with ctx:
        SB = 53200
        NX = 8320
        with nc.sbuf_tensor("x_columns", [128, NX], f32) as x_columns, nc.sbuf_tensor("columns", [128, SB - NX], f32) as columns:
            pass

        class Columns:
            def __getitem__(self, key):
                rows, cols = key
                if cols.start < NX:
                    return x_columns[rows, cols]
                return columns[rows, cols.start - NX:cols.stop - NX]

        sb = Columns()

        def alias(name, start, n, dtype):
            with nc.sbuf_tensor(name + "_before", [128, start], f32), nc.sbuf_tensor(name, [128, n], dtype) as t:
                return t

        def at_part(t, off, dims):
            return bass.AP(tensor=t, offset=off, ap=[[t.shape[1], 128]] + [list(d) for d in dims])

        bank = [ctx.enter_context(nc.psum_tensor(f"bank{i}", [128, 512], f32)) for i in range(8)]
        scratch_xn = nc.dram_tensor("scratch_xn", [NIMG, H, W], f32)
        scratch_ln = nc.dram_tensor("scratch_ln", [NLINE * 256], f32)
        scratch_x = nc.dram_tensor("scratch_x", [NIMG, H, W], f32)
        scratch_xb = nc.dram_tensor("scratch_xb", [NIMG, 3, KX, KY], f32)

        def sem(name):
            return ctx.enter_context(nc.semaphore(name))

        def at(off, dims, lo=0, hi=128, of=None):
            if of is None:
                of, off = (x_columns, off) if isinstance(off, int) and off < NX else (columns, off - NX)
            pitch = {id(x_columns): NX, id(columns): SB - NX}.get(id(of), 512)
            return bass.AP(tensor=of, offset=off + lo * pitch, ap=[[pitch, hi - lo]] + [list(d) for d in dims])

        def pat(bk, off, dims, lo=0, hi=128):
            return at(off, dims, lo, hi, bank[bk])

        XR, XA, FF, CST = 0, NX, NX + 8192, NX + 16384
        SEL = CST + NCONST
        SM = SEL + 512
        PR = SM
        ST = PR + 2 * PROW
        MS, DV, SQ, QQ, VS = ST + 384, ST + 448, ST + 576, ST + 704, ST + 832
        S0, C0, S1, C1, S2, C2 = (ST + 896 + 64 * i for i in range(6))
        S3, C3, S5, C5 = (S2 + 128 + 16 * i for i in range(4))
        RW = C5 + 16
        R_GO, R_CT, R_SS, R_Q0, R_K0, R_TMP = (RW + 32 * i for i in range(6))
        D0 = RW + 192
        EPSC = D0 + 1
        VP = D0 + 2
        WM = VP + 4
        WI = WM + 2 * 2 * 66
        U = WI + 2 * 66
        AF, BP = U, U + 1632
        AT = AF
        MB, MT = BP + 3168, BP + 3232
        V0 = MT + 128
        assert V0 + 17728 <= SB, V0
        NQ = KQ * KY
        PW, VW, VF = V0, V0 + 2 * NQ, V0 + 4 * NQ
        BF = VF + 128
        PARTS = [BF + 3 * NQ + i * (3 * NQ // 2) for i in range(3)]
        QK, QKF, QT = V0 + 12864, V0 + 15040, V0 + 15168
        assert QT + 1088 + 64 <= V0 + 17728 and PARTS[2] + 3 * NQ // 2 <= QK
        GG, XB, X2 = V0, V0 + 8192, V0 + 14528
        TX, TG, ZZ = V0, V0 + 3264, V0 + 8192
        SC, TP = ZZ + 512, ZZ + 1536
        XT = V0
        XC, BX, SY, ZC = V0 + 16192, V0 + 1536, V0 + 4608, V0 + 8832
        YR = ZC + 1024
        assert YR + KX * 192 <= XC and XC + 1536 <= SB
        HH = U
        GR, SP, T1, T2, ZM = HH + 8192, HH + 10496, HH + 11024, HH + 11552, HH + 12080

        NP_ = W + 6
        XP, MAT, YY = XA, XA + NIMG * NP_, -(-U // 8) * 8
        FLIP = MAT + NLINE * 128
        YL = YY + 16 * 2 * NP_
        XL = YL + 16 * 2 * NP_
        ML = XL + NIMG * NP_
        ZERO = FLIP + 128
        assert ZERO + 384 <= CST and ML + NLINE * 128 <= SB
        x_high, x_low, x_whole = (alias(n, o, NIMG * NP_, d) for n, o, d in (("x_high", XP, f32r), ("x_low", XL, f32r), ("x_whole", XL, f32)))
        m_high, m_low, m_whole = (alias(n, o, NLINE * 128, d) for n, o, d in (("m_high", MAT, f32r), ("m_low", ML, f32r), ("m_whole", ML, f32)))
        y_high, y_low, y_whole = (alias(n, o, 32 * NP_, d) for n, o, d in (("y_high", YY, f32r), ("y_low", YL, f32r), ("y_whole", YL, f32)))
        X_PARTS, M_PARTS, Y_PARTS = (x_whole, x_high, x_low), (m_whole, m_high, m_low), (y_whole, y_high, y_low)
        LN = XA
        BI, TP2, CS = WM, LN + NLINE * 256, LN + NLINE * 256 + 288
        Y_N, Y_B, Y_A = NP_, 4 * NP_, 8 * NP_
        G3 = SEL
        XM = (2 * 8320, G3 + 3 * 4096)
        CK = XM[1] + 64 * 130
        XQ = CK + NCONST3
        TT = XQ + 2 * 2080
        WB = (0, 8320)
        YM, YT = G3, 0
        Z3, XO, OO = G3 + 8320, G3, G3 + 2048
        assert TT + 640 <= SB and Z3 + 2048 <= XM[1] and XM[0] + 8320 <= G3

        def cst(col, n, lo=0, hi=128):
            return sb[lo:hi, CST + col:CST + col + n]

        def par(L, col, lo=0, hi=128):
            return sb[lo:hi, PR + L * PROW + col:PR + L * PROW + col + 1]

        names = """x_loaded consts_loaded weights_loaded sel_cast
            stat_sums mean_ready var_in var_ready std_ready dve_order pool_order act_order
            gn_ready xn_ready a_form b_form hi_ready r1_ready mid_ready r2_ready lo_ready parts_moved a_psum
            g_psum g_ready x2_psum x2_ready xb_psum xb_ready sym_psum xb_stored xn_stored
            zero_t t_ready z_ready z_used gout_psum exp_in exp_ready
            mix_ready mixT_psum mixT_ready attn_ready attnT_psum attnT_ready xt_loaded
            skip_psum skip_used skip_done xc_loaded0 xc_loaded1 rep_psum bx_ready comb_ready bx_used acc_used sy_psum sy_ready
            zi_psum zi_ready p_psum p_used
            an_ready ga_psum ga_ready gb_psum gb_used sp_ready zc_psum zc_ready h_psum h_ready
            att_var att_std pre_gelu gelu_ready stats_used out_ready x_done
            taps_loaded lines_made lines_stored mats_loaded bias_loaded flip_loaded flip_psum mats_high mats_ready xp2_raw xp2_high xp2_ready pads_ready
            up_psum up_copied y_max y_high y_ready dn_psum x2_done x2_stored
            k_loaded g3_psum g3_ready g3_neg xm_psum xm_ready w_loaded0 w_loaded1
            xq_zero xq_ready y3_psum t_part t_sum y3_kept ty_psum ty_ready z3_psum z3_ready o_psum o_ready xo_loaded0 xo_loaded1 xo_loaded2 xo_loaded3 o_stored0 o_stored1""".split()
        S = {n: sem(n) for n in names}

        class Rounds:
            def __init__(self):
                self.n = 0

        dve_r, pe_r, act_r = Rounds(), Rounds(), Rounds()
        order = {"dve": 0, "pool": 0, "act": 0}

        def link(ins, eng, who):
            order[who] += 1
            ins.then_inc(S[who + "_order"], 1)
            eng.wait_ge(S[who + "_order"], order[who])

        block = ctx.enter_context(nc.Block())

        def pe_mean(pe, C, ms=MS):
            pe.wait_ge(S["stat_sums"], pe_r.n + 1)
            nc.tensor.matmul(bank[7][:, 0:C], cst(C_ONE, 128), sb[:, ms:ms + C], start=True, stop=True).then_inc(S["mean_ready"], 1)

        def pe_var(pe, C):
            pe.wait_ge(S["var_in"], pe_r.n + 1)
            nc.tensor.matmul(bank[7][:, 64:64 + C], cst(C_ONE, 128), sb[:, VS:VS + C], start=True, stop=True).then_inc(S["var_ready"], 1)
            pe_r.n += 1

        def act_std(act, C):
            act.wait_ge(S["var_ready"], act_r.n + 1)
            nc.scalar.activation(bank[7][:, 128:128 + C], bank[7][:, 64:64 + C], ACT.Sqrt, bias=sb[:, EPSC:EPSC + 1]).then_inc(S["std_ready"], 1)
            act_r.n += 1

        def dve_sums(dve, C, st=ST, ms=MS):
            nc.vector.tensor_tensor(sb[:, ms:ms + C], at(st + 1, [[6, C]]), at(st + 4, [[6, C]]), add).then_inc(S["stat_sums"], 1)

        def dve_var_in(dve, C, st=ST):
            dve.wait_ge(S["mean_ready"], dve_r.n + 1)
            two = [[2, C], [1, 2]]
            link(nc.vector.tensor_tensor(at(DV, two), at(st + 1, [[6, C], [3, 2]]), pat(7, 0, [[1, C], [0, 2]]), sub), dve, "dve")
            link(nc.vector.tensor_tensor(at(SQ, two), at(DV, two), at(DV, two), mult), dve, "dve")
            link(nc.vector.scalar_tensor_tensor(at(QQ, two), at(st + 2, [[6, C], [3, 2]]), 1 / 64, at(SQ, two), mult, add), dve, "dve")
            nc.vector.tensor_tensor(sb[:, VS:VS + C], at(QQ, [[2, C]]), at(QQ + 1, [[2, C]]), add).then_inc(S["var_in"], 1)

        def dve_rstd(dve, C):
            dve.wait_ge(S["std_ready"], dve_r.n + 1)
            link(nc.vector.reciprocal(bank[7][:, 128:128 + C], bank[7][:, 128:128 + C]), dve, "dve")
            dve_r.n += 1

        def whole_round(eng, who, C):
            if who == "dve":
                dve_sums(eng, C); dve_var_in(eng, C); dve_rstd(eng, C)
            elif who == "pe":
                pe_mean(eng, C); pe_var(eng, C)
            else:
                act_std(eng, C)

        MEAN, VAR, RSTD = 0, 64, 128

        def affine(dve, L, g, b, C, s_at, c_at, extra=None):
            link(nc.vector.tensor_scalar(sb[:, s_at:s_at + C], bank[7][:, RSTD:RSTD + C], par(L, g), None, mult), dve, "dve")
            link(nc.vector.tensor_tensor(sb[:, c_at:c_at + C], bank[7][:, MEAN:MEAN + C], sb[:, s_at:s_at + C], mult), dve, "dve")
            link(nc.vector.tensor_scalar(sb[:, c_at:c_at + C], sb[:, c_at:c_at + C], -1.0, par(L, b), mult, add), dve, "dve")
            if extra is not None:
                link(nc.vector.tensor_scalar(sb[:, c_at:c_at + C], sb[:, c_at:c_at + C], extra, None, add), dve, "dve")

        def group_norm(dve, k):
            if k == 3:
                dve.wait_ge(S["x2_done"], 16)
            elif k >= 1:
                dve.wait_ge(S["x_done"], 4 * k)
            for b in range(B):
                for g in range(32):
                    last = nc.vector.bn_stats(sb[:, ST + (b * 32 + g) * 6:ST + (b * 32 + g) * 6 + 6],
                                              at(XR + b * 4096 + 4 * g, [[128, 32], [1, 4]]))
            link(last, dve, "dve")
            whole_round(dve, "dve", 64)
            if k == 0:
                dve.wait_ge(S["lines_stored"], 16)
            if k == 2:
                dve.wait_ge(S["bias_loaded"], 16)
                link(nc.vector.tensor_copy(bank[7][:, 192:256], sb[:, BI:BI + 64]), dve, "dve")
                for b in range(B):
                    img, pad = [[128, 32], [4, 32], [1, 4]], [[NP_, 32], [4, 32], [1, 4]]
                    grp, o = [[0, 32], [1, 32], [0, 4]], 32 * NP_ * b + 3
                    link(nc.vector.tensor_tensor(at_part(x_whole, o, pad), at(XR + b * 4096, img), pat(7, MEAN + b * 32, grp), sub), dve, "dve")
                    link(nc.vector.tensor_tensor(at_part(x_whole, o, pad), at_part(x_whole, o, pad), pat(7, RSTD + b * 32, grp), mult), dve, "dve")
                    row = [[NP_, 8], [1, 128]]
                    for q in range(4):
                        eight = at_part(x_whole, o + 8 * NP_ * q, row)
                        nc.vector.tensor_tensor(eight, eight, pat(7, 192 + b * 32 + 8 * q, [[1, 8], [0, 128]]), add).then_inc(S["xp2_raw"], 1)
                return
            for b in range(B):
                img = [[128, 32], [4, 32], [1, 4]]
                grp = [[0, 32], [1, 32], [0, 4]]
                link(nc.vector.tensor_tensor(at(XA + b * 4096, img), at(XR + b * 4096, img), pat(7, MEAN + b * 32, grp), sub), dve, "dve")
                last = nc.vector.tensor_tensor(at(XA + b * 4096, img), at(XA + b * 4096, img), pat(7, RSTD + b * 32, grp), mult)
                if b == 0:
                    link(last, dve, "dve")
            last.then_inc(S["gn_ready"], 1)
            dve.wait_ge(S["gn_ready"], min(k + 1, 3))

        def image_stats(dve, src, n0, n1, st=ST):
            for j, n in enumerate(range(n0, n1)):
                last = nc.vector.bn_stats(sb[:, st + 6 * j:st + 6 * j + 6], sb[:, src + n * 128:src + n * 128 + 128])
            link(last, dve, "dve")

        def scale_images(src, dst, n0, n1, s_at, c_at):
            for n in range(n0, n1):
                last = nc.vector.tensor_scalar(sb[:, dst + n * 128:dst + n * 128 + 128], sb[:, src + n * 128:src + n * 128 + 128],
                                               sb[:, s_at + n - n0:s_at + n - n0 + 1], sb[:, c_at + n - n0:c_at + n - n0 + 1], mult, add)
            return last

        NKP = 17
        NU = NIMG // 4
        UPS = [(a, b) for a in range(2) for b in range(2)]

        STEPS = 45

        def round_at(i):
            out = []
            if (i - 7) % 4 == 0 and 0 <= (i - 7) // 4 < 8:
                out.append(("first", (i - 7) // 4))
            if (i - 12) % 4 == 0 and 4 <= (i - 12) // 4 < 8:
                out.append(("second", (i - 12) // 4))
            return out

        def applied_at(i):
            out = []
            if 0 <= i - 8 < 32:
                out.append(("first", (i - 8) // 4, (i - 8) % 4))
            if 16 <= i - 13 < 32:
                out.append(("second", (i - 13) // 4, (i - 13) % 4))
            return out

        @block.sync
        def _(sp):
            sp.dma_start(sb[0:1, TP2:TP2 + 288], io["taps"]).then_inc(S["taps_loaded"], 16)
            for q in range(4):
                sp.dma_start(at(XR + q * 2048, [[128, 16], [1, 128]]), io["x"][16 * q:16 * q + 16].rearrange("n h w -> h n w")).then_inc(S["x_loaded"], 16)
            sp.dma_start(cst(0, NCONST), io["cst"]).then_inc(S["consts_loaded"], 16)
            sp.dma_start(sb[:, PR:PR + 2 * PROW], bass.AP(tensor=io["prow"].tensor, offset=io["prow"].offset, ap=[[0, 128], [1, 2 * PROW]])).then_inc(S["consts_loaded"], 16)
            sp.dma_start(sb[:, VP:VP + 4], io["vsps"]).then_inc(S["consts_loaded"], 16)
            sp.dma_start(at(WM, [[132, 2], [66, 2], [1, 66]]), io["wm"].rearrange("l j p c -> p l j c")).then_inc(S["consts_loaded"], 16)
            sp.dma_start(sb[0:96, V0 + 16384:V0 + 16384 + 1024], io["sel"]).then_inc(S["consts_loaded"], 16)
            sp.wait_ge(S["lines_made"], 1)
            sp.dma_start(scratch_ln.ap().rearrange("(p n) -> p n", p=1), sb[0:1, LN:LN + NLINE * 256]).then_inc(S["lines_stored"], 16)
            for L in range(NL):
                if L:
                    sp.wait_ge(S["x_done"], 4 * L)
                sp.dma_start(sb[:, QK:QK + 2176], io["qk"][L]).then_inc(S["weights_loaded"], 16)
                sp.dma_start(sb[:, QKF:QKF + 128], io["qkf"][L]).then_inc(S["weights_loaded"], 16)
                sp.dma_start(sb[:, PW:PW + 2 * NQ], io["pw"][L]).then_inc(S["weights_loaded"], 16)
                sp.dma_start(sb[:, VW:VW + 2 * NQ], io["vw"][L]).then_inc(S["weights_loaded"], 16)
                sp.dma_start(sb[0:32, VF:VF + 128], io["vf"][L]).then_inc(S["weights_loaded"], 16)
                for i, ready in enumerate(("hi_ready", "mid_ready", "lo_ready")):
                    sp.wait_ge(S[ready], L + 1)
                    for g in range(4):
                        w = min(KQ, KX - KQ * g) * KY // 2
                        sp.dma_start(at(BP + g * (NQ // 2), [[KX * KY // 2, 3], [1, w]], 32 * i, 32 * i + 32),
                                     at(PARTS[i], [[NQ // 2, 3], [1, w]], 32 * g, 32 * g + 32)).then_inc(S["parts_moved"], 16)
                sp.wait_ge(S["xn_ready"], 4 * (L + 1))
                sp.dma_start(scratch_xn.ap().rearrange("n h w -> h n w"), at(FF, [[128, 64], [1, 128]])).then_inc(S["xn_stored"], 16)
                sp.wait_ge(S["xb_ready"], 13 * (L + 1))
                sp.dma_start(scratch_xb.ap().rearrange("n f x y -> n (f x y)"), sb[0:64, XB:XB + 6336]).then_inc(S["xb_stored"], 16)
                sp.wait_ge(S["z_used"], KC * (L + 1))
                sp.wait_ge(S["xn_stored"], 16 * (L + 1))
                for half in range(2):
                    sp.dma_start(at(XT, [[64, 128], [1, 64]], 64 * half, 64 * half + 64), scratch_xn.ap()[:, :, 64 * half:64 * half + 64]).then_inc(S["xt_loaded"], 16)
                sp.wait_ge(S["xb_stored"], 16 * (L + 1))
                for kp in range(NKP):
                    k = L * NKP + kp
                    if k >= 2:
                        sp.wait_ge(S["bx_ready"], 8 * (k - 1))
                    nk = 2 if kp < NKP - 1 else 1
                    for b in range(B):
                        src = bass.AP(tensor=scratch_xb, offset=b * 32 * 6336 + kp * 2 * KY,
                                      ap=[[0, 4], [6336, 32], [KX * KY, 3], [1, nk * KY]])
                        sp.dma_start(at(XC + 768 * (k % 2) + 384 * b, [[nk * KY, 3], [1, nk * KY]]), src).then_inc(S[f"xc_loaded{k % 2}"], 16)
            sp.wait_ge(S["x_done"], 8)
            sp.dma_start(sb[:, FLIP:FLIP + 128], io["cst3"][:, K_FLIP:K_FLIP + 128]).then_inc(S["flip_loaded"], 16)
            sp.wait_ge(S["lines_stored"], 16)
            sp.dma_start(at(MAT, [[128, NLINE], [1, 128]]), bass.AP(tensor=scratch_ln, offset=0, ap=[[1, 128], [256, NLINE], [1, 128]])).then_inc(S["mats_loaded"], 16)
            sp.dma_start(sb[:, BI:BI + 64], bass.AP(tensor=io["bias"].tensor, offset=0, ap=[[0, 128], [1, 64]])).then_inc(S["bias_loaded"], 16)
            w = (io["w3r"], io["w3i"])

            def load_chunk(c, k):
                for part in range(2):
                    for a in range(2):
                        src = bass.AP(tensor=w[part].tensor, offset=a * 64 * 65 + c * 260, ap=[[32 * 8320, 32], [8320, 32], [1, 260]])
                        lo = 64 * part + 32 * a
                        sp.dma_start(at(WB[k], [[260, 32], [1, 260]], lo, lo + 32), src).then_inc(S[f"w_loaded{k}"], 16)

            sp.wait_ge(S["dn_psum"], 16)
            sp.dma_start(sb[:, CK:CK + NCONST3], io["cst3"]).then_inc(S["k_loaded"], 16)
            sp.wait_ge(S["x2_done"], 16)
            sp.dma_start(scratch_x.ap().rearrange("n h w -> h n w"), at(XR, [[128, 64], [1, 128]])).then_inc(S["x2_stored"], 16)
            sp.wait_ge(S["x2_stored"], 16)
            sp.wait_ge(S["gn_ready"], 3)
            sp.wait_ge(S["g3_psum"], 1)
            load_chunk(0, 0)
            sp.wait_ge(S["g3_psum"], 32)
            load_chunk(1, 1)
            with sp.Fori(1, 8) as it:
                for k in range(2):
                    sp.wait_ge(S["y3_psum"], 10 * it + 5 * k - 5)
                    load_chunk(2 * it + k, k)
            for u in range(NU):
                if u == 0:
                    sp.wait_ge(S["ty_psum"], 33)
                if u >= 4:
                    sp.wait_ge(S["o_ready"], u - 3)
                sp.dma_start(at(XO + 512 * (u % 4), [[128, 4], [1, 128]]), scratch_x.ap()[4 * u:4 * u + 4].rearrange("n h w -> h n w")).then_inc(S[f"xo_loaded{u % 4}"], 16)
                if u >= 2:
                    sp.wait_ge(S["o_ready"], u - 1)
                    sp.dma_start(io["out"][4 * u - 8:4 * u - 4].rearrange("n h w -> h n w"), at(OO + 512 * (u % 2), [[128, 4], [1, 128]])).then_inc(S[f"o_stored{u % 2}"], 16)
            for u in (NU, NU + 1):
                sp.wait_ge(S["o_ready"], u - 1)
                sp.dma_start(io["out"][4 * u - 8:4 * u - 4].rearrange("n h w -> h n w"), at(OO + 512 * (u % 2), [[128, 4], [1, 128]])).then_inc(S[f"o_stored{u % 2}"], 16)
            for e in range(2):
                sp.wait_ge(S[f"o_stored{e}"], 16 * NU // 2)

        @block.gpsimd
        def _(gp):
            def tt(o, a, b_, op):
                link(nc.gpsimd.tensor_tensor(o, a, b_, op), gp, "pool")

            def ts(o, a, s1, s2, o1, o2=ALU.bypass):
                link(nc.gpsimd.tensor_scalar(o, a, s1, s2, o1, o2) if s2 is not None else nc.gpsimd.tensor_scalar(o, a, s1, None, o1), gp, "pool")

            gp.wait_ge(S["taps_loaded"], 16)
            one = lambda off, dims: at(off, dims, 0, 1)
            nc.gpsimd.memset(sb[0:1, CS:CS + 168], 0.0)
            link(nc.gpsimd.memset(sb[0:1, LN:LN + NLINE * 256], 0.0), gp, "pool")
            f, d = TP2, TP2 + 144
            nc.gpsimd.tensor_copy(one(CS, [[7, 12], [6, 2]]), one(f, [[12, 12], [11, 2]]))
            nc.gpsimd.tensor_tensor(one(CS + 1, [[7, 12], [1, 5]]), one(f + 1, [[12, 12], [2, 5]]), one(f + 2, [[12, 12], [2, 5]]), add)
            link(nc.gpsimd.tensor_tensor(one(CS + 84 + 1, [[7, 12], [1, 6]]), one(f, [[12, 12], [2, 6]]), one(f + 1, [[12, 12], [2, 6]]), add), gp, "pool")
            for b in range(2):
                ln, cs = LN + 7 * 256 * b, CS + 84 * b
                nc.gpsimd.tensor_copy(one(ln + 124, [[256, 7], [6, 2]]), one(cs + 77, [[1, 7], [-77, 2]]))
                nc.gpsimd.tensor_tensor(one(ln + 129, [[256, 7], [-1, 5]]), one(cs + 7, [[1, 7], [14, 5]]), one(cs + 14, [[1, 7], [14, 5]]), add)
                ln += 14 * 256
                nc.gpsimd.tensor_tensor(one(ln + 129, [[256, 7], [-1, 6]]), one(cs, [[1, 7], [14, 6]]), one(cs + 7, [[1, 7], [14, 6]]), add)
            ln = LN + 28 * 256
            nc.gpsimd.tensor_scalar(one(ln + 129, [[256, 12], [-1, 6]]), one(d + 12, [[1, 12], [24, 6]]), GAIN, None, mult)
            nc.gpsimd.tensor_scalar(one(ln + 12 * 256 + 130, [[256, 12], [-1, 6]]), one(d, [[1, 12], [24, 6]]), GAIN, None, mult).then_inc(S["lines_made"], 1)
            gp.wait_ge(S["consts_loaded"], 80)
            for L in range(NL):
                gp.wait_ge(S["weights_loaded"], 80 * (L + 1))
                q, k = QK, QK + 1088
                for j in range(4):
                    o = QK + 544 * j
                    tt(sb[:, o:o + 32], sb[:, o:o + 32], sb[:, QKF + 32 * j:QKF + 32 * j + 32], add if j % 2 == 0 else sub)
                    ts(sb[:, o:o + 32], sb[:, o:o + 32], 0.5, None, mult)
                for o, p in ((q, P_QS), (k, P_KS)):
                    kh = [[32, KC], [1, 32]]
                    tt(at(o, kh), at(o, kh), at(PR + L * PROW + p, [[0, KC], [1, 32]]), add)
                n = KC * 32
                fa = [[96, KC], [1, 32]]
                kh = [[32, KC], [1, 32]]
                qr, qi, kr, ki = q, q + n, k, k + n
                tt(sb[:, QT:QT + n], sb[:, qr:qr + n], sb[:, kr:kr + n], mult)
                tt(sb[:, QT + n:QT + 2 * n], sb[:, qi:qi + n], sb[:, ki:ki + n], mult)
                tt(at(AF + 32, fa), at(QT, kh), at(QT + n, kh), add)
                tt(sb[:, QT:QT + n], sb[:, qr:qr + n], sb[:, ki:ki + n], mult)
                tt(sb[:, QT + n:QT + 2 * n], sb[:, qi:qi + n], sb[:, kr:kr + n], mult)
                tt(at(AF + 64, fa), at(QT, kh), at(QT + n, kh), sub)
                ts(at(AF + 96 + 32, [[96, KC - 1], [1, 64]]), at(AF + 96 + 32, [[96, KC - 1], [1, 64]]), 128.0, None, mult)
                ts(sb[:, AF + 32:AF + 96], sb[:, AF + 32:AF + 96], cst(C_MASK, 1), 64.0, mult, mult)
                nc.gpsimd.tensor_tensor(at(AF, fa), at(AF + 32, fa), at(AF + 64, fa), add).then_inc(S["a_form"], 1)
                n = NQ
                w_v, w_p = sb[:, VP + 2 * L:VP + 2 * L + 1], sb[:, VP + 2 * L + 1:VP + 2 * L + 2]
                for j, op in ((0, add), (1, sub)):
                    o = VW + n * j
                    tt(sb[0:32, o:o + 64], sb[0:32, o:o + 64], sb[0:32, VF + 64 * j:VF + 64 * j + 64], op)
                    ts(sb[0:32, o:o + 64], sb[0:32, o:o + 64], 0.5, None, mult)
                vr, vi, pr, pi = VW, VW + n, PW, PW + n
                tmp, fr, fi = BF, BF + n, BF + 2 * n
                col = lambda o: sb[:, o:o + n]
                ts(col(fr), col(pr), w_v, None, mult)
                ts(col(fi), col(pi), w_v, None, mult)
                for o, a, c, op in ((fr, vr, pr, add), (fr, vi, pi, sub), (fi, vr, pi, add), (fi, vi, pr, add)):
                    tt(col(tmp), col(a), col(c), mult)
                    tt(col(o), col(o), col(tmp), op)
                for o, a in ((fr, vr), (fi, vi)):
                    ts(col(tmp), col(a), w_p, None, mult)
                    tt(col(o), col(o), col(tmp), add)
                nc.gpsimd.tensor_tensor(col(BF), col(fr), col(fi), add).then_inc(S["b_form"], 1)
                gp.wait_ge(S["b_form"], L + 1)
                f = sb[:, BF:BF + 3 * n]
                part = lambda i: sb[:, PARTS[i]:PARTS[i] + 3 * n // 2].bitcast(bf16)
                gp.wait_ge(S["hi_ready"], L + 1)
                nc.gpsimd.tensor_tensor(f, f, part(0), sub).then_inc(S["r1_ready"], 1)
                gp.wait_ge(S["mid_ready"], L + 1)
                nc.gpsimd.tensor_tensor(f, f, part(1), sub).then_inc(S["r2_ready"], 1)
                gp.wait_ge(S["xb_psum"], 13 * (L + 1))
                gp.wait_ge(S["x2_psum"], 8 * (L + 1))
                nc.gpsimd.memset(sb[:, TX:TX + 5312], 0.0)
                nc.gpsimd.memset(sb[:, MT:MT + 128], 0.0)
                nc.gpsimd.memset(sb[0:64, MB:MB + 64], 0.0).then_inc(S["zero_t"], 1)
                for kp in range(NKP):
                    n = 128 if kp < NKP - 1 else 64
                    for c in range(8):
                        k = (L * NKP + kp) * 8 + c
                        form = lambda f: at(BX + 768 * (k % 4) + f * n, [[3 * n, 2], [1, n]])
                        gp.wait_ge(S["bx_ready"], k + 1)
                        if c % 4 == 0:
                            nc.gpsimd.tensor_tensor(form(2), form(0), form(2), sub)
                        nc.gpsimd.tensor_tensor(form(1), form(0), form(1), add).then_inc(S["comb_ready"], 1)
                for i in range(1, STEPS):
                    if i <= 32:
                        k = L * 32 + i - 1
                        b_ = k % 2
                        gp.wait_ge(S["gb_used"], k + 1)
                        if k >= 2:
                            gp.wait_ge(S["zc_psum"], k - 1)
                        nc.gpsimd.tensor_tensor(sb[:, SP + 264 * b_:SP + 264 * b_ + 264], sb[:, T1 + 264 * b_:T1 + 264 * b_ + 264],
                                                sb[:, T2 + 264 * b_:T2 + 264 * b_ + 264], add).then_inc(S["sp_ready"], 1)
                    for kind, gg, q in applied_at(i):
                        if kind == "second":
                            k = 4 * (gg % 4) + q
                            gp.wait_ge(S["out_ready"], 16 * L + k + 1)
                            x, h = XR + 512 * k, HH + 512 * k
                            last = nc.gpsimd.tensor_tensor(sb[:, x:x + 512], sb[:, x:x + 512], sb[:, h:h + 512], add)
                            if q == 3:
                                last.then_inc(S["x_done"], 1)
            gp.wait_ge(S["x_done"], 8)
            link(nc.gpsimd.memset(sb[:, ZERO:ZERO + 384], 0.0), gp, "pool")
            for x, y in zip(X_PARTS[1:], Y_PARTS[1:]):
                nc.gpsimd.tensor_copy(at_part(x, 0, [[NP_, 64], [131, 2], [1, 3]]), at(ZERO, [[6, 64], [3, 2], [1, 3]]))
                last = nc.gpsimd.tensor_copy(at_part(y, 0, [[NP_, 32], [131, 2], [1, 3]]), at(ZERO, [[6, 32], [3, 2], [1, 3]]))
            last.then_inc(S["pads_ready"], 1)

            def low(parts, o, dims):
                whole, high, low_ = (at_part(t, o, dims) for t in parts)
                return nc.gpsimd.tensor_tensor(low_, whole, high, sub)

            gp.wait_ge(S["mats_high"], NLINE // 4)
            low(M_PARTS, 0, [[1, NLINE * 128]]).then_inc(S["mats_ready"], 1)
            for q in range(8):
                gp.wait_ge(S["xp2_high"], q + 1)
                low(X_PARTS, 8 * NP_ * q + 3, [[NP_, 8], [1, 128]]).then_inc(S["xp2_ready"], 1)

            with gp.Fori(0, 8) as it:
                for e in range(2):
                    for ab, (a, b) in enumerate(UPS):
                        gp.wait_ge(S["y_high"], 8 * it + 4 * e + ab + 1)
                        low(Y_PARTS, e * 2 * Y_A + a * Y_A + b * Y_B + 3, [[Y_N, 4], [1, 128]]).then_inc(S["y_ready"], 1)
            gp.wait_ge(S["k_loaded"], 16)
            nc.gpsimd.memset(sb[:, XQ:XQ + 4160], 0.0).then_inc(S["xq_zero"], 1)
            gp.wait_ge(S["xq_zero"], 1)
            gp.wait_ge(S["xm_ready"], 64)

            def spread(c, e, first=False):
                if not first:
                    gp.wait_ge(S["y3_psum"], 5 * c - 5)
                for lo in range(0, 128, 32):
                    a = lo // 32 % 2
                    last = nc.gpsimd.tensor_copy(at(XQ + 2080 * e + 2 * a, [[8, 260], [4, 2], [1, 2]], lo, lo + 32),
                                                 at(XM[0] + 520 * c, [[2, 260], [XM[1] - XM[0], 2], [1, 2]], lo, lo + 32))
                last.then_inc(S["xq_ready"], 1)

            spread(0, 0, True)
            spread(1, 1, True)
            with gp.Fori(1, 8) as it:
                spread(2 * it, 0)
                spread(2 * it + 1, 1)

        @block.scalar
        def _(act):
            act.wait_ge(S["consts_loaded"], 80)
            nc.scalar.activation(sb[0:96, SEL:SEL + 512].bitcast(bf16), sb[0:96, V0 + 16384:V0 + 16384 + 1024], ACT.Copy).then_inc(S["sel_cast"], 1)
            act.wait_ge(S["sel_cast"], 2)
            for L in range(NL):
                whole_round(act, "act", 64)
                whole_round(act, "act", 64)
                act.wait_ge(S["b_form"], L + 1)
                f = sb[:, BF:BF + 3 * NQ]
                part = lambda i: sb[:, PARTS[i]:PARTS[i] + 3 * NQ // 2].bitcast(bf16)
                nc.scalar.activation(part(0), f, ACT.Copy).then_inc(S["hi_ready"], 1)
                act.wait_ge(S["r1_ready"], L + 1)
                nc.scalar.activation(part(1), f, ACT.Copy).then_inc(S["mid_ready"], 1)
                act.wait_ge(S["r2_ready"], L + 1)
                nc.scalar.activation(part(2), f, ACT.Copy).then_inc(S["lo_ready"], 1)
                act.wait_ge(S["parts_moved"], 192 * (L + 1))
                for u in range(NU):
                    k = L * NU + u
                    act.wait_ge(S["g_psum"], k + 1)
                    nc.scalar.activation(sb[:, GG + u * 512:GG + u * 512 + 512], bank[u % 2][:, :], ACT.Copy).then_inc(S["g_ready"], 1)
                for u in range(8):
                    k = L * 8 + u
                    act.wait_ge(S["x2_psum"], k + 1)
                    nc.scalar.activation(sb[:, X2 + u * 400:X2 + u * 400 + 400], bank[2 + u % 2][:, 0:400], ACT.Copy).then_inc(S["x2_ready"], 1)
                for u in range(13):
                    k = L * 13 + u
                    ny = min(5, KY - 5 * u)
                    act.wait_ge(S["xb_psum"], k + 1)
                    nc.scalar.activation(at(XB + 5 * u, [[64, 99], [1, ny]], 0, 64), pat(4 + u % 2, 0, [[1, 99], [99, ny]], 0, 64),
                                         ACT.Copy).then_inc(S["xb_ready"], 1)
                act.wait_ge(S["a_form"], L + 1)
                for j in range(4):
                    n = 96 * min(5, KC - 5 * j)
                    last = nc.scalar.activation(bank[j][:, 0:n], sb[:, AF + 480 * j:AF + 480 * j + n], ACT.Copy)
                last.then_inc(S["a_psum"], 1)
                act.wait_ge(S["exp_in"], L + 1)
                nc.scalar.activation(sb[0:64, SC:SC + 1024], sb[0:64, SC:SC + 1024], ACT.Exp).then_inc(S["exp_ready"], 1)
                def rows_copy(kp):
                    kk = L * NKP + kp
                    act.wait_ge(S["sy_psum"], kk + 1)
                    cols = 2 if kp < NKP - 1 else 1
                    nc.scalar.activation(at(SY + 2 * kp, [[33, 2], [1, cols], [66, 64]]), pat(4 + kk % 2, 0, [[128, 2], [64, cols], [1, 64]]),
                                         ACT.Copy).then_inc(S["sy_ready"], 1)

                for kp in range(NKP):
                    kk = L * NKP + kp
                    cols = 2 if kp < NKP - 1 else 1
                    if kp:
                        rows_copy(kp - 1)
                    act.wait_ge(S["bx_used"], 8 * (kk + 1))
                    if kp == 0:
                        act.wait_ge(S["skip_done"], L + 1)
                    for f, part, scale in ((0, 1, 1.0), (1, 0, 1.0), (2, 1, -1.0)):
                        last = nc.scalar.activation(at(YR + 384 * kp + 64 * f, [[192, cols], [1, 64]], 0, 64),
                                                    pat(3 + 3 * (kk % 2), 64 * cols * part, [[64, cols], [1, 64]], 0, 64), ACT.Copy, scale=scale)
                    last.then_inc(S["acc_used"], 1)
                rows_copy(NKP - 1)
                for u in range(NU):
                    k = L * NU + u
                    act.wait_ge(S["zi_psum"], k + 1)
                    if u >= 2:
                        act.wait_ge(S["p_psum"], k - 1)
                    nc.scalar.activation(sb[0:66, ZC + 512 * (u % 2):ZC + 512 * (u % 2) + 512], bank[4][0:66, :], ACT.Copy).then_inc(S["zi_ready"], 1)
                whole_round(act, "act", 64)
                act.wait_ge(S["att_var"], L + 1)
                nc.scalar.activation(sb[:, DV:DV + 64], sb[:, QQ:QQ + 64], ACT.Sqrt, bias=sb[:, EPSC:EPSC + 1]).then_inc(S["att_std"], 1)
                for i in range(STEPS):
                    k = L * 32 + i
                    if i < 32:
                        o = GR + 768 * (k % 3)
                        bk = (0, 4)[k % 2]
                        act.wait_ge(S["ga_psum"], k + 1)
                        if k >= 3:
                            act.wait_ge(S["gb_psum"], k - 2)
                        nc.scalar.activation(at(o, [[192, 4], [1, 128]]), pat(bk, 0, [[128, 4], [1, 128]]), ACT.Copy)
                        nc.scalar.activation(at(o + 128, [[192, 4], [1, 64]]), pat(bk, 0, [[128, 4], [1, 64]]), ACT.Copy, scale=-1.0).then_inc(S["ga_ready"], 1)
                    if 0 <= i - 2 < 32:
                        k = L * 32 + i - 2
                        act.wait_ge(S["zc_psum"], k + 1)
                        if k >= 2:
                            act.wait_ge(S["h_psum"], k - 1)
                        nc.scalar.activation(sb[0:66, ZM + 512 * (k % 2):ZM + 512 * (k % 2) + 512], bank[(2, 6)[k % 2]][0:66, :], ACT.Copy).then_inc(S["zc_ready"], 1)
                    if 0 <= i - 3 < 32:
                        k = L * 32 + i - 3
                        o = HH + 512 * ((i - 3) % 16)
                        act.wait_ge(S["h_psum"], k + 1)
                        nc.scalar.activation(sb[:, o:o + 512], bank[3][:, :], ACT.Copy).then_inc(S["h_ready"], 1)
                    if round_at(i):
                        act_std(act, 16)
                    if 0 <= i - 9 < 16:
                        o = 512 * (i - 9)
                        act.wait_ge(S["pre_gelu"], L * 16 + i - 8)
                        nc.scalar.activation(sb[:, FF + o:FF + o + 512], sb[:, HH + o:HH + o + 512], ACT.Gelu).then_inc(S["gelu_ready"], 1)

            def copy_up(g, e, first=False):
                for ab in range(5):
                    if ab < 4:
                        act.wait_ge(S["up_psum"], 4 * g + ab + 1)
                        if ab == 0 and not first:
                            act.wait_ge(S["dn_psum"], g - 1)
                        a, b = UPS[ab]
                        nc.scalar.activation(at_part(y_whole, e * 2 * Y_A + a * Y_A + b * Y_B + 3, [[Y_N, 4], [1, 128]]), bank[ab][:, :], ACT.Copy).then_inc(S["up_copied"], 1)
                    if ab >= 1:
                        act.wait_ge(S["y_max"], 4 * g + ab)
                        a, b = UPS[ab - 1]
                        o = e * 2 * Y_A + a * Y_A + b * Y_B + 3
                        nc.scalar.activation(at_part(y_high, o, [[Y_N, 4], [1, 128]]), at_part(y_whole, o, [[Y_N, 4], [1, 128]]), ACT.Copy).then_inc(S["y_high"], 1)

            for u in range(NLINE // 4):
                act.wait_ge(S["flip_psum"], u + 1)
                nc.scalar.activation(m_whole[:, 512 * u:512 * u + 512], bank[u % 2][:, :], ACT.Copy)
                nc.scalar.activation(m_high[:, 512 * u:512 * u + 512], bank[u % 2][:, :], ACT.Copy).then_inc(S["mats_high"], 1)
            whole_round(act, "act", 64)
            for q in range(8):
                act.wait_ge(S["xp2_raw"], q + 1)
                o, eight = 8 * NP_ * q + 3, [[NP_, 8], [1, 128]]
                nc.scalar.activation(at_part(x_high, o, eight), at_part(x_whole, o, eight), ACT.Copy).then_inc(S["xp2_high"], 1)
            act.wait_ge(S["pads_ready"], 1)
            for e in range(2):
                copy_up(e, e, True)
            with act.Fori(1, 8) as it:
                for e in range(2):
                    copy_up(2 * it + e, e)
            whole_round(act, "act", 64)
            for b in range(B):
                for u in range(16):
                    act.wait_ge(S["g3_psum"], 16 * b + u + 1)
                    if u == 0 and b:
                        act.wait_ge(S["xm_psum"], 32)
                    for c in range(2):
                        last = nc.scalar.activation(at(G3 + 2 * u + 64 * c, [[1, 2], [32, 2], [192, 64]]), pat(u % 2, 128 * c, [[256, 2], [64, 2], [1, 64]]), ACT.Copy)
                    last.then_inc(S["g3_ready"], 1)
                for u in range(32):
                    act.wait_ge(S["xm_psum"], 32 * b + u + 1)
                    nc.scalar.activation(at(XM[b] + 520 * (u // 2) + 4 * (u % 2), [[8, 65], [2, 2], [1, 2]]),
                                         pat(2 + u % 2, 0, [[1, 65], [130, 2], [65, 2]]), ACT.Copy).then_inc(S["xm_ready"], 1)

            def keep(c, first=False):
                for g in range(5):
                    n = 16 if g < 4 else 1
                    act.wait_ge(S["t_sum"], 5 * c + g + 1)
                    nc.scalar.activation(at(YM + 16 * 64 * g + 4 * c, [[64, n], [4160, 2], [1, 4]]), at(TT + 128 * g, [[8, n], [4, 2], [1, 4]]),
                                         ACT.Copy).then_inc(S["y3_kept"], 1)

            with act.Fori(0, 16) as it:
                keep(it)
            for u in range(33):
                act.wait_ge(S["ty_psum"], u + 1)
                for j in range(2):
                    b, k0, n = (u // 16, 4 * (u % 16), 4) if u < 32 else (0, 64, 2)
                    step = 1 if u < 32 else 4160
                    last = nc.scalar.activation(at(YT + 4160 * b + k0, [[step, n], [130, 32], [65, 2]], 64 * j, 64 * j + 64),
                                                pat(u % 2, 2 * j, [[128, n], [4, 32], [1, 2]], 0, 64), ACT.Copy)
                last.then_inc(S["ty_ready"], 1)
            for u in range(32):
                act.wait_ge(S["z3_psum"], u + 1)
                if u >= 4:
                    act.wait_ge(S["o_psum"], (u - 4) // 2 + 1)
                nc.scalar.activation(sb[0:65, Z3 + 512 * (u % 4):Z3 + 512 * (u % 4) + 512], bank[u % 4][0:65, :], ACT.Copy).then_inc(S["z3_ready"], 1)

        @block.tensor
        def _(pe):
            mm = nc.tensor.matmul

            pe.wait_ge(S["consts_loaded"], 80)
            pe.wait_ge(S["sel_cast"], 2)
            for L in range(NL):
                whole_round(pe, "pe", 64)
                whole_round(pe, "pe", 64)
                for u in range(NU):
                    k = L * NU + u
                    pe.wait_ge(S["xn_ready"], 4 * L + u // 4 + 1)
                    if u >= 2:
                        pe.wait_ge(S["g_ready"], k - 1)
                    for j in range(4):
                        n = 4 * u + j
                        last = mm(bank[u % 2][:, 128 * j:128 * j + 128], sb[:, FF + 128 * n:FF + 128 * n + 128], cst(C_FA, 128), start=True, stop=True)
                    last.then_inc(S["g_psum"], 1)
                pe.wait_ge(S["g_ready"], NU * (L + 1))
                for u in range(8):
                    k = L * 8 + u
                    if u >= 2:
                        pe.wait_ge(S["x2_ready"], k - 1)
                    for j in range(4):
                        for b in range(B):
                            for ri in range(2):
                                o = GG + (b * 32 + 4 * u + j) * 128 + 64 * ri
                                last = mm(bank[2 + u % 2][64 * b:64 * b + 64, 100 * j:100 * j + 100], sb[:, o:o + 64],
                                          cst((C_X21, C_X22)[ri], 100), start=ri == 0, stop=ri == 1)
                    last.then_inc(S["x2_psum"], 1)
                for u in range(13):
                    k = L * 13 + u
                    if u >= 2:
                        pe.wait_ge(S["xb_ready"], k - 1)
                    for j in range(min(5, KY - 5 * u)):
                        for ri in range(2):
                            last = mm(bank[4 + u % 2][0:64, 99 * j:99 * j + 99], at(GG + 5 * u + j + 64 * ri, [[128, 64]]),
                                      cst((C_XB1, C_XB2)[ri], 99), start=ri == 0, stop=ri == 1)
                    last.then_inc(S["xb_psum"], 1)
                pe.wait_ge(S["x2_ready"], 8 * (L + 1))
                mm(bank[6][:, 0:32], cst(C_SR, 128), at(X2 + 83, [[100, 32]]), start=True, stop=True)
                mm(bank[6][:, 32:64], cst(C_SI, 128), at(X2 + 99, [[100, 32]]), start=True, stop=True).then_inc(S["sym_psum"], 1)
                pe.wait_ge(S["t_ready"], L + 1)
                pe.wait_ge(S["xb_ready"], 13 * (L + 1))
                for j in range(16):
                    for ri in range(2):
                        last = mm(bank[5][0:64, 0:32], sb[:, TG + (2 * j + ri) * 64:TG + (2 * j + ri) * 64 + 64],
                                  at(X2 + 68 + 16 * ri + j, [[100, 32]]), start=j + ri == 0, stop=j + ri == 16)
                last.then_inc(S["gout_psum"], 1)
                for kx in range(KC):
                    k = L * KC + kx
                    pe.wait_ge(S["z_ready"], k + 1)
                    for f in range(3):
                        for j in range(2):
                            o = ZZ + 3072 * (k % 2) + 1024 * f + 512 * j
                            last = mm(bank[(4, 6)[j]][0:64, :], sb[:, TX + (3 * kx + f) * 64:TX + (3 * kx + f) * 64 + 64], sb[:, o:o + 512],
                                      start=kx + f == 0, stop=kx == KC - 1 and f == 2)
                    last.then_inc(S["z_used"], 1)
                pe.wait_ge(S["attn_ready"], L + 1)
                for c in range(8):
                    last = nc.tensor.transpose(bank[2][:, 64 * c:64 * c + 64], sb[0:64, SC + 128 * c:SC + 128 * c + 128], cst(C_ID, 64, 0, 64))
                last.then_inc(S["attnT_psum"], 1)
                pe.wait_ge(S["mix_ready"], L + 1)
                nc.tensor.transpose(bank[6][0:64, 0:64], sb[0:64, MB:MB + 64], cst(C_ID, 64, 0, 64)).then_inc(S["mixT_psum"], 1)
                pe.wait_ge(S["mixT_ready"], L + 1)
                pe.wait_ge(S["xt_loaded"], 32 * (L + 1))
                for u in range(16):
                    k = L * 16 + u
                    if u >= 2:
                        pe.wait_ge(S["skip_used"], k - 1)
                    for j in range(4):
                        last = mm(bank[4 + u % 2][:, 128 * j:128 * j + 128], at(XT + 4 * u + j, [[64, 128]]), sb[:, MT:MT + 128], start=True, stop=True)
                    last.then_inc(S["skip_psum"], 1)
                pe.wait_ge(S["attnT_ready"], L + 1)
                pe.wait_ge(S["parts_moved"], 192 * (L + 1))
                seq = [(kp, c) for kp in range(NKP) for c in range(8)]

                def rep(i):
                    kp, c = seq[i]
                    n = 128 if kp < NKP - 1 else 64
                    k = L * len(seq) + i
                    if i >= 3:
                        pe.wait_ge(S["bx_ready"], k - 2)
                    moving = sb[0:96, BP:BP + 3168].bitcast(bf16)
                    moving = bass.AP(tensor=moving.tensor, offset=moving.offset + 128 * kp, ap=[list(moving.ap[0]), [2112, 3], [1, n]])
                    mm(bank[i % 3][:, 0:3 * n], sb[0:96, SEL:SEL + 512].bitcast(bf16)[:, 128 * c:128 * c + 128], moving, start=True, stop=True).then_inc(S["rep_psum"], 1)

                def to_rows(kp):
                    kk = L * NKP + kp
                    pe.wait_ge(S["acc_used"], kk + 1)
                    if kk >= 2:
                        pe.wait_ge(S["sy_ready"], kk - 1)
                    cols = 2 if kp < NKP - 1 else 1
                    for half in range(2):
                        for j in range(cols):
                            o = YR + 192 * (2 * kp + j) + 64 * half
                            last = nc.tensor.transpose(bank[4 + kk % 2][:, 64 * (2 * half + j):64 * (2 * half + j) + 64], sb[0:64, o:o + 128], cst(C_ID, 64, 0, 64))
                    last.then_inc(S["sy_psum"], 1)

                for i in range(3):
                    rep(i)
                for i, (kp, c) in enumerate(seq):
                    k = L * len(seq) + i
                    n = 128 if kp < NKP - 1 else 64
                    kk = L * NKP + kp
                    if c == 0 and kk >= 2:
                        pe.wait_ge(S["acc_used"], kk - 1)
                    if c == 4 and kp:
                        to_rows(kp - 1)
                    pe.wait_ge(S["comb_ready"], k + 1)
                    if i + 3 < len(seq):
                        rep(i + 3)
                    for b in range(B):
                        o = BX + 768 * (k % 4) + 3 * n * b
                        a = AT + 64 * (2 * c + b)
                        im, re = (bank[3 + 3 * (kk % 2)][32 * b:32 * b + 32, n * f:n * f + n] for f in range(2))
                        if c % 4 == 0:
                            both = bank[3 + 3 * (kk % 2)][32 * b:32 * b + 32, 0:2 * n]
                            last = mm(both, sb[:, a:a + 32], sb[:, o + n:o + 3 * n], start=c == 0, stop=False, skip_group_check=True)
                        else:
                            mm(im, sb[:, a:a + 32], sb[:, o + n:o + 2 * n], start=False, stop=c == 7, skip_group_check=True)
                            mm(re, sb[:, a:a + 32], sb[:, o:o + n], start=False, stop=False, skip_group_check=True)
                            last = mm(re, sb[:, a + 32:a + 64], sb[:, o + 2 * n:o + 3 * n], start=False, stop=c == 7, skip_group_check=True)
                    last.then_inc(S["bx_used"], 1)
                to_rows(NKP - 1)
                pe.wait_ge(S["sy_ready"], NKP * (L + 1))
                for u in range(NU + 1):
                    if u < NU:
                        k = L * NU + u
                        if u >= 1:
                            pe.wait_ge(S["zi_ready"], k)
                        for j in range(4):
                            o = SY + (4 * u + j) * 66
                            last = mm(bank[4][0:66, 128 * j:128 * j + 128], sb[:, o:o + 66], cst(C_E, 128), start=True, stop=True)
                        last.then_inc(S["zi_psum"], 1)
                    if u >= 1:
                        k = L * NU + u - 1
                        pe.wait_ge(S["zi_ready"], k + 1)
                        if u >= 2:
                            pe.wait_ge(S["p_used"], k)
                        for j in range(4):
                            o = ZC + 512 * ((u - 1) % 2) + 128 * j
                            last = mm(bank[5][:, 128 * j:128 * j + 128], sb[0:66, o:o + 128], cst(C_D, 128, 0, 66), start=True, stop=True)
                        last.then_inc(S["p_psum"], 1)
                whole_round(pe, "pe", 64)
                small = L * 12
                for i in range(STEPS):
                    if i < 32:
                        k = L * 32 + i
                        if i < 16:
                            pe.wait_ge(S["an_ready"], 4 * L + i // 4 + 1)
                        else:
                            pe.wait_ge(S["gelu_ready"], 16 * L + i - 15)
                        if k >= 2:
                            pe.wait_ge(S["ga_ready"], k - 1)
                        for j in range(4):
                            o = FF + 512 * (i % 16) + 128 * j
                            last = mm(bank[(0, 4)[k % 2]][:, 128 * j:128 * j + 128], sb[:, o:o + 128], cst(C_FA, 128), start=True, stop=True)
                        last.then_inc(S["ga_psum"], 1)
                    if 0 <= i - 1 < 32:
                        k = L * 32 + i - 1
                        pe.wait_ge(S["ga_ready"], k + 1)
                        if k >= 2:
                            pe.wait_ge(S["gb_used"], k - 1)
                        for j in range(4):
                            o = GR + 768 * (k % 3) + 192 * j
                            dst = bank[(1, 5)[k % 2]][:, 66 * j:66 * j + 66]
                            mm(dst, sb[:, o:o + 128], cst(C_FB1, 66), start=True, stop=False)
                            last = mm(dst, sb[:, o + 64:o + 192], cst(C_FB2, 66), start=False, stop=True)
                        last.then_inc(S["gb_psum"], 1)
                    for kind, gg in round_at(i):
                        if small >= 1:
                            pe.wait_ge(S["stats_used"], small)
                        small += 1
                        pe_mean(pe, 16, MS if kind == "first" else MS + 16)
                    if 0 <= i - 2 < 32:
                        k = L * 32 + i - 2
                        pe.wait_ge(S["sp_ready"], k + 1)
                        if k >= 2:
                            pe.wait_ge(S["zc_ready"], k - 1)
                        for j in range(4):
                            o = SP + 264 * (k % 2) + 66 * j
                            last = mm(bank[(2, 6)[k % 2]][0:66, 128 * j:128 * j + 128], sb[:, o:o + 66], cst(C_E, 128), start=True, stop=True)
                        last.then_inc(S["zc_psum"], 1)
                    if 0 <= i - 3 < 32:
                        k = L * 32 + i - 3
                        pe.wait_ge(S["zc_ready"], k + 1)
                        if k >= 1:
                            pe.wait_ge(S["h_ready"], k)
                        for j in range(4):
                            o = ZM + 512 * (k % 2) + 128 * j
                            last = mm(bank[3][:, 128 * j:128 * j + 128], sb[0:66, o:o + 128], cst(C_D, 128, 0, 66), start=True, stop=True)
                        last.then_inc(S["h_psum"], 1)
                    for r in round_at(i):
                        pe_var(pe, 16)
            def exact(dst, m, images, o, start, stop):
                whole, x_hi, x_lo = (at_part(t, o, [[NP_, 4], [1, 128]]) for t in images)
                mm(dst, m_high[:, 128 * m:128 * m + 128], x_hi, start=start, stop=False)
                mm(dst, m_high[:, 128 * m:128 * m + 128], x_lo, start=False, stop=False)
                return mm(dst, m_low[:, 128 * m:128 * m + 128], x_hi, start=False, stop=stop)

            def up(g, pair, first=False):
                pe.wait_ge(S["xp2_ready"], pair + 1)
                for ab, (a, b) in enumerate(UPS):
                    if not first:
                        pe.wait_ge(S["y_max"], 4 * g + ab - 3)
                    shifts = range(-3 + b, 4)
                    for dq in shifts:
                        last = exact(bank[ab][:, :], (a * 2 + b) * 7 + dq + 3, X_PARTS, 4 * NP_ * g + 3 + dq, dq == shifts[0], dq == 3)
                    last.then_inc(S["up_psum"], 1)

            def down(g, e, first=False):
                pe.wait_ge(S["y_ready"], 4 * g + 4)
                if not first:
                    pe.wait_ge(S["x2_done"], g - 1)
                for a in range(2):
                    for j in range(TAPS):
                        b = (j + 1) % 2
                        dq = (j - 5 - b) // 2
                        last = exact(bank[4 + e][:, :], 28 + 12 * a + j, Y_PARTS, e * 2 * Y_A + a * Y_A + b * Y_B + 3 + dq,
                                     a + j == 0, a == 1 and j == TAPS - 1)
                last.then_inc(S["dn_psum"], 1)

            pe.wait_ge(S["mats_loaded"], 16)
            pe.wait_ge(S["flip_loaded"], 16)
            for u in range(NLINE // 4):
                if u >= 2:
                    pe.wait_ge(S["mats_high"], u - 1)
                mm(bank[u % 2][:, :], sb[:, FLIP:FLIP + 128], sb[:, MAT + 512 * u:MAT + 512 * u + 512], start=True, stop=True).then_inc(S["flip_psum"], 1)
            whole_round(pe, "pe", 64)
            pe.wait_ge(S["mats_ready"], 1)
            pe.wait_ge(S["pads_ready"], 1)
            up(0, 0, True)
            up(1, 0)
            down(0, 0, True)
            up(2, 1)
            down(1, 1, True)
            with pe.Fori(1, 7) as it:
                up(2 * it + 1, it)
                down(2 * it, 0)
                up(2 * it + 2, it + 1)
                down(2 * it + 1, 1)
            up(15, 7)
            down(14, 0)
            down(15, 1)
            ck = lambda col, n, hi=128: sb[0:hi, CK + col:CK + col + n]
            whole_round(pe, "pe", 64)
            pe.wait_ge(S["k_loaded"], 16)
            pe.wait_ge(S["gn_ready"], 3)
            for b in range(B):
                for u in range(16):
                    if 16 * b + u >= 2:
                        pe.wait_ge(S["g3_ready"], 16 * b + u - 1)
                    for j in range(2):
                        n = 32 * b + 2 * u + j
                        last = mm(bank[u % 2][:, 256 * j:256 * j + 256], sb[:, XA + 128 * n:XA + 128 * n + 128], ck(K_FA, 256), start=True, stop=True)
                    last.then_inc(S["g3_psum"], 1)
                pe.wait_ge(S["g3_neg"], b + 1)
                for u in range(32):
                    k = 32 * b + u
                    if k >= 2:
                        pe.wait_ge(S["xm_ready"], k - 1)
                    for j in range(2):
                        o = G3 + 192 * (2 * u + j)
                        for s in range(2):
                            last = mm(bank[2 + u % 2][:, 130 * j:130 * j + 130], sb[:, o + 64 * s:o + 64 * s + 128],
                                      ck(K_FB + (65, 0)[s], 130), start=s == 0, stop=s == 1)
                    last.then_inc(S["xm_psum"], 1)

            COPIES = 3

            def modes_chunk(c, k, first=False):
                pe.wait_ge(S["xq_ready"], c + 1)
                pe.wait_ge(S[f"w_loaded{k}"], 32 * (c - k) + 64)
                for g in range(5):
                    if not first:
                        pe.wait_ge(S["t_sum"], 5 * c + g - 4)
                    for j in range(16 if g < 4 else 1):
                        kx = 16 * g + j
                        n = min(COPIES, 16 - j)
                        last = mm(bank[g][:, 32 * j:32 * (j + n)], at(WB[k] + kx, [[65, 128]]), at(XQ + 2080 * k + 32 * kx, [[0, n], [1, 32]]), start=True, stop=True)
                    last.then_inc(S["y3_psum"], 1)

            pe.wait_ge(S["xm_ready"], 64)
            modes_chunk(0, 0, True)
            modes_chunk(1, 1)
            with pe.Fori(1, 8) as it:
                modes_chunk(2 * it, 0)
                modes_chunk(2 * it + 1, 1)
            pe.wait_ge(S["y3_kept"], 80)
            for u in range(33):
                if u >= 2:
                    pe.wait_ge(S["ty_ready"], u - 1)
                for j in range(4 if u < 32 else 2):
                    o = 4160 * (u // 16) + 64 * (4 * (u % 16) + j) if u < 32 else 4160 * j + 64 * 64
                    last = nc.tensor.transpose(bank[u % 2][0:64, 128 * j:128 * j + 128], sb[:, YM + o:YM + o + 64], ck(K_ID, 128))
                last.then_inc(S["ty_psum"], 1)
            pe.wait_ge(S["ty_ready"], 33)
            for u in range(NU + 1):
                for e in range(2):
                    if u < NU:
                        k = 2 * u + e
                        if k >= 4:
                            pe.wait_ge(S["z3_ready"], k - 3)
                        for j in range(2):
                            o = YT + 130 * (4 * u + 2 * e + j)
                            dst = bank[k % 4][0:65, 256 * j:256 * j + 256]
                            mm(dst, sb[:, o:o + 65], ck(K_E, 256), start=True, stop=False)
                            last = mm(dst, sb[:, o + 65:o + 130], ck(K_E + 256, 256), start=False, stop=True)
                        last.then_inc(S["z3_psum"], 1)
                if u >= 1:
                    pe.wait_ge(S["z3_ready"], 2 * u)
                    if u >= 3:
                        pe.wait_ge(S["o_ready"], u - 2)
                    for j in range(4):
                        o = Z3 + 512 * ((2 * u - 2 + j // 2) % 4) + 256 * (j % 2)
                        dst = bank[4 + u % 2][:, 128 * j:128 * j + 128]
                        mm(dst, sb[0:65, o:o + 128], ck(K_DC, 128, 65), start=True, stop=False)
                        last = mm(dst, sb[0:65, o + 128:o + 256], ck(K_DS, 128, 65), start=False, stop=True)
                    last.then_inc(S["o_psum"], 1)

        @block.vector
        def _(dve):
            v = nc.vector

            def L_(ins):
                link(ins, dve, "dve")

            v.memset(sb[:, EPSC:EPSC + 1], EPS).then_inc(S["sel_cast"], 1)
            dve.wait_ge(S["x_loaded"], 64)
            dve.wait_ge(S["consts_loaded"], 80)
            for L in range(NL):
                group_norm(dve, L)
                image_stats(dve, XA, 0, NIMG)
                whole_round(dve, "dve", 64)
                affine(dve, L, P_G, P_B, 64, S0, C0)
                for g in range(4):
                    scale_images(XA, FF, 16 * g, 16 * g + 16, S0 + 16 * g, C0 + 16 * g).then_inc(S["xn_ready"], 1)
                row = lambda p: sb[:, PR + L * PROW + p:PR + L * PROW + p + 32]
                R = lambda r: sb[:, r:r + 32]
                L_(v.scalar_tensor_tensor(R(R_GO), row(P_QS), 64.0, row(P_KS), mult, mult))
                for r, w00, ws, bs in ((R_Q0, P_Q00, P_QS, P_BQ), (R_K0, P_K00, P_KS, P_BK)):
                    L_(v.tensor_tensor(R(r), row(w00), row(ws), add))
                    L_(v.scalar_tensor_tensor(R(r), R(r), par(L, P_B), row(bs), mult, add))
                L_(v.scalar_tensor_tensor(R(R_CT), R(R_Q0), 64.0, R(R_K0), mult, mult))
                L_(v.tensor_tensor(R(R_SS), row(P_PS), row(P_VS), mult))
                L_(v.tensor_tensor(R(R_TMP), row(P_P00), row(P_PS), add))
                L_(v.tensor_tensor(R(R_TMP), R(R_TMP), row(P_BV), mult))
                L_(v.tensor_reduce(sb[:, D0:D0 + 1], R(R_TMP), AX.X, add))
                L_(v.tensor_tensor(sb[:, D0:D0 + 1], sb[:, D0:D0 + 1], par(L, P_BP), add))
                dve.wait_ge(S["sym_psum"], L + 1)
                L_(v.tensor_copy(at(X2 + 83, [[100, 32], [16, 2]]), pat(6, 0, [[1, 32], [32, 2]])))
                L_(v.tensor_scalar(at(X2 + 51, [[100, 32]]), at(X2 + 51, [[100, 32]]), cst(C_MASK + 1, 1), None, mult))
                L_(v.tensor_tensor(at(X2 + 17, [[100, 32]]), at(X2 + 51, [[100, 32]]), at(X2, [[100, 32]]), sub))
                L_(v.tensor_tensor(at(X2 + 34, [[100, 32]]), at(X2 + 51, [[100, 32]]), at(X2, [[100, 32]]), add))
                dve.wait_ge(S["zero_t"], L + 1)
                for b in range(B):
                    p = dict(lo=64 * b, hi=64 * b + 64)
                    for f, src, scale in ((0, 34, 1.0), (1, 51, 1.0), (2, 0, -1.0)):
                        v.tensor_scalar(at(TX + 64 * f + 32 * b, [[192, KC], [1, 32]], **p), at(X2 + src, [[1, KC], [100, 32]], **p), scale, None, mult)
                    for ri in range(2):
                        v.tensor_scalar(at(TG + 64 * ri + 32 * b, [[128, 15], [1, 32]], **p), at(X2 + 68 + 16 * ri, [[1, 15], [100, 32]], **p), 2.0, None, mult)
                        last = v.tensor_copy(at(TG + 64 * ri + 32 * b + 15 * 128, [[1, 32]], **p), at(X2 + 83 + 16 * ri, [[100, 32]], **p))
                last.then_inc(S["t_ready"], 1)
                dve.wait_ge(S["a_psum"], L + 1)
                dve.wait_ge(S["xb_stored"], 16 * (L + 1))
                for kx in range(KC):
                    k = L * KC + kx
                    if kx >= 2:
                        dve.wait_ge(S["z_used"], k - 1)
                    for f in range(3):
                        last = v.tensor_tensor(at(ZZ + 3072 * (k % 2) + 1024 * f, [[32, 32], [1, 32]]), at(X2 + kx + 17 * f, [[0, 32], [100, 32]]),
                                               pat(kx // 5, 96 * (kx % 5) + 32 * f, [[1, 32], [0, 32]]), mult)
                    last.then_inc(S["z_ready"], 1)
                hs, h0, s0 = [[32, 32], [1, 32]], [[1, 32], [0, 32]], [[0, 32], [1, 32]]
                q = lambda off, dims: at(off, dims, 0, 64)
                dve.wait_ge(S["gout_psum"], L + 1)
                dve.wait_ge(S["z_used"], KC * (L + 1))
                L_(v.tensor_tensor(q(TP, hs), pat(5, 0, s0, 0, 64), q(R_GO, h0), mult))
                L_(v.tensor_tensor(q(TP, hs), q(TP, hs), q(R_CT, h0), add))
                for j in range(2):
                    last = v.tensor_tensor(sb[0:64, SC + 512 * j:SC + 512 * j + 512], bank[(4, 6)[j]][0:64, :], sb[0:64, TP + 512 * j:TP + 512 * j + 512], add)
                L_(last)
                L_(v.tensor_reduce(sb[0:64, DV:DV + 32], q(SC, hs), AX.X, amax))
                v.tensor_tensor(q(SC, hs), q(SC, hs), q(DV, h0), sub).then_inc(S["exp_in"], 1)
                dve.wait_ge(S["exp_ready"], L + 1)
                L_(v.tensor_reduce(sb[0:64, DV:DV + 32], q(SC, hs), AX.X, add))
                L_(v.reciprocal(sb[0:64, DV:DV + 32], sb[0:64, DV:DV + 32]))
                v.tensor_tensor(q(SC, hs), q(SC, hs), q(DV, h0), mult).then_inc(S["attn_ready"], 1)
                dve.wait_ge(S["attn_ready"], L + 1)
                L_(v.tensor_tensor(q(TP, hs), q(SC, hs), q(R_SS, h0), mult))
                for b in range(B):
                    last = v.tensor_reduce(sb[32 * b:32 * b + 32, MB + 32 * b:MB + 32 * b + 32], at(TP, [[1, 32], [32, 32]], 32 * b, 32 * b + 32), AX.X, add)
                last.then_inc(S["mix_ready"], 1)
                dve.wait_ge(S["attnT_psum"], L + 1)
                a2 = [[64, 16], [1, 32]]
                v.tensor_copy(at(AT, a2), pat(2, 0, [[32, 16], [1, 32]]))
                v.tensor_scalar(at(AT + 32, a2), pat(2, 0, [[32, 16], [1, 32]]), -1.0, None, mult).then_inc(S["attnT_ready"], 1)
                dve.wait_ge(S["mixT_psum"], L + 1)
                v.tensor_copy(sb[0:64, MT:MT + 64], bank[6][0:64, 0:64])
                v.tensor_copy(sb[64:128, MT + 64:MT + 128], bank[6][0:64, 0:64]).then_inc(S["mixT_ready"], 1)
                dve.wait_ge(S["xn_stored"], 16 * (L + 1))
                for u in range(16):
                    k = L * 16 + u
                    dve.wait_ge(S["skip_psum"], k + 1)
                    for half in range(2):
                        w = 64 * half + 4 * u
                        last = v.scalar_tensor_tensor(at(FF + w, [[1, 4], [128, 64]]), pat(4 + u % 2, 64 * half, [[128, 4], [1, 64]]), sb[:, D0:D0 + 1],
                                                      at(XA + w, [[1, 4], [128, 64]]), add, add)
                    last.then_inc(S["skip_used"], 1)
                dve.wait_ge(S["skip_used"], 16 * (L + 1))
                v.memset(sb[0:1, R_TMP:R_TMP + 1], 0.0).then_inc(S["skip_done"], 1)
                for kp in range(NKP):
                    n = 128 if kp < NKP - 1 else 64
                    kk = L * NKP + kp
                    dve.wait_ge(S[f"xc_loaded{kk % 2}"], 32 * (kk // 2 + 1))
                    for c in range(8):
                        k = kk * 8 + c
                        dve.wait_ge(S["rep_psum"], k + 1)
                        if k >= 4:
                            dve.wait_ge(S["bx_used"], k - 3)
                        v.tensor_tensor(at(BX + 768 * (k % 4), [[3 * n, 2], [1, 3 * n]]), pat((kp * 8 + c) % 3, 0, [[0, 2], [1, 3 * n]]),
                                        at(XC + 768 * (kk % 2), [[384, 2], [1, 3 * n]]), mult).then_inc(S["bx_ready"], 1)
                for u in range(NU):
                    k = L * NU + u
                    dve.wait_ge(S["p_psum"], k + 1)
                    v.tensor_tensor(sb[:, XA + 512 * u:XA + 512 * u + 512], bank[5][:, :], sb[:, FF + 512 * u:FF + 512 * u + 512], add).then_inc(S["p_used"], 1)
                    dve.wait_ge(S["p_used"], k + 1)
                    for n in range(4 * u, 4 * u + 4):
                        last = v.bn_stats(sb[:, ST + 6 * n:ST + 6 * n + 6], sb[:, XA + 128 * n:XA + 128 * n + 128])
                L_(last)
                whole_round(dve, "dve", 64)
                affine(dve, L, P_G + 1, P_B + 1, 64, S1, C1)
                L_(v.tensor_tensor(sb[:, QQ:QQ + 64], bank[7][:, VAR:VAR + 64], sb[:, S1:S1 + 64], mult))
                v.tensor_tensor(sb[:, QQ:QQ + 64], sb[:, QQ:QQ + 64], sb[:, S1:S1 + 64], mult).then_inc(S["att_var"], 1)
                dve.wait_ge(S["att_std"], L + 1)
                L_(v.reciprocal(sb[:, DV:DV + 64], sb[:, DV:DV + 64]))
                L_(v.tensor_tensor(sb[:, S2:S2 + 64], sb[:, DV:DV + 64], sb[:, S1:S1 + 64], mult))
                L_(v.tensor_scalar(sb[:, S2:S2 + 64], sb[:, S2:S2 + 64], par(L, P_G + 2), None, mult))
                L_(v.tensor_tensor(sb[:, C2:C2 + 64], bank[7][:, MEAN:MEAN + 64], sb[:, S2:S2 + 64], mult))
                L_(v.tensor_scalar(sb[:, C2:C2 + 64], sb[:, C2:C2 + 64], -1.0, par(L, P_B + 2), mult, add))
                wm = lambda j, ri: WM + (2 * L + j) * 66 + 33 * ri
                for j in range(2):
                    v.tensor_scalar(sb[:, WI + 66 * j:WI + 66 * j + 33], sb[:, wm(j, 1):wm(j, 1) + 33], -1.0, None, mult)
                    L_(v.tensor_copy(sb[:, WI + 66 * j + 33:WI + 66 * j + 66], sb[:, wm(j, 1):wm(j, 1) + 33]))
                for g in range(4):
                    scale_images(XA, FF, 16 * g, 16 * g + 16, S2 + 16 * g, C2 + 16 * g).then_inc(S["an_ready"], 1)
                for i in range(STEPS):
                    if 0 <= i - 1 < 32:
                        k = L * 32 + i - 1
                        j = (i - 1) // 16
                        bk = (1, 5)[k % 2]
                        dve.wait_ge(S["gb_psum"], k + 1)
                        if k >= 2:
                            dve.wait_ge(S["sp_ready"], k - 1)
                        out = [[66, 4], [33, 2], [1, 33]]
                        v.tensor_tensor(at(T1 + 264 * (k % 2), out), pat(bk, 0, out), at(wm(j, 0), [[0, 4], [0, 2], [1, 33]]), mult)
                        v.tensor_tensor(at(T2 + 264 * (k % 2), out), pat(bk, 33, [[66, 4], [-33, 2], [1, 33]]),
                                        at(WI + 66 * j, [[0, 4], [33, 2], [1, 33]]), mult).then_inc(S["gb_used"], 1)
                    for kind, gg, q in applied_at(i):
                        j, g = gg // 4, gg % 4
                        o = 2048 * g + 512 * q
                        h, f, a = HH + o, FF + o, XA + o
                        if q == 0:
                            dve_rstd(dve, 16)
                        if kind == "first":
                            if q == 0:
                                affine(dve, L, P_G + 3 + j, P_B + 3 + j, 16, S3, C3, par(L, (P_BM0, P_BM1)[j]))
                                v.memset(sb[0:1, R_TMP:R_TMP + 1], 0.0).then_inc(S["stats_used"], 1)
                            L_(scale_images(h, h, 0, 4, S3 + 4 * q, C3 + 4 * q))
                            last = v.scalar_tensor_tensor(sb[:, h:h + 512], sb[:, f:f + 512], par(L, (P_M0S, P_M1S)[j]), sb[:, h:h + 512], mult, add)
                            if j == 0:
                                last.then_inc(S["pre_gelu"], 1)
                            else:
                                L_(last)
                                image_stats(dve, h, 0, 4, ST + 192 + 96 * (gg % 2) + 24 * q)
                                if q == 3:
                                    dve_sums(dve, 16, ST + 192 + 96 * (gg % 2), MS + 16)
                        else:
                            if q == 0:
                                affine(dve, L, P_G + 5, P_B + 5, 16, S5, C5)
                                v.memset(sb[0:1, R_TMP:R_TMP + 1], 0.0).then_inc(S["stats_used"], 1)
                                L_(v.tensor_tensor(sb[:, C5:C5 + 16], sb[:, C5:C5 + 16], sb[:, C1 + 16 * g:C1 + 16 * g + 16], add))
                            L_(scale_images(h, h, 0, 4, S5 + 4 * q, C5 + 4 * q))
                            for n in range(4):
                                s1 = S1 + 16 * g + 4 * q + n
                                last = v.scalar_tensor_tensor(sb[:, h + 128 * n:h + 128 * n + 128], sb[:, a + 128 * n:a + 128 * n + 128],
                                                              sb[:, s1:s1 + 1], sb[:, h + 128 * n:h + 128 * n + 128], mult, add)
                            last.then_inc(S["out_ready"], 1)
                    for kind, gg in round_at(i):
                        dve_var_in(dve, 16, ST + 96 * (gg % 2) + (192 if kind == "second" else 0))
                    if 0 <= i - 3 < 32:
                        u = i - 3
                        dve.wait_ge(S["h_ready"], L * 32 + u + 1)
                        st = ST + 96 * (u // 4 % 2)
                        for n in range(4):
                            o = HH + 512 * (u % 16) + 128 * n
                            last = v.bn_stats(sb[:, st + 6 * (4 * (u % 4) + n):st + 6 * (4 * (u % 4) + n) + 6], sb[:, o:o + 128])
                        if u % 4 == 3:
                            L_(last)
                            dve_sums(dve, 16, st)

            def sloped(g, e, ab):
                dve.wait_ge(S["up_copied"], 4 * g + ab + 1)
                a, b = UPS[ab]
                y = at_part(y_whole, e * 2 * Y_A + a * Y_A + b * Y_B + 3, [[Y_N, 4], [1, 128]])
                v.scalar_tensor_tensor(y, pat(ab, 0, [[128, 4], [1, 128]]), SLOPE, y, mult, amax).then_inc(S["y_max"], 1)

            def residual(g, e):
                dve.wait_ge(S["dn_psum"], g + 1)
                x = at(XR + 512 * g, [[1, 512]], of=x_columns)
                v.tensor_tensor(x, bank[4 + e][:, :], x, add).then_inc(S["x2_done"], 1)

            group_norm(dve, 2)
            for ab in range(4):
                sloped(0, 0, ab)
            for ab in range(4):
                sloped(1, 1, ab)
            residual(0, 0)
            with dve.Fori(1, 8) as it:
                for ab in range(4):
                    sloped(2 * it, 0, ab)
                residual(2 * it - 1, 1)
                for ab in range(4):
                    sloped(2 * it + 1, 1, ab)
                residual(2 * it, 0)
            residual(15, 1)
            group_norm(dve, 3)
            for b in range(B):
                dve.wait_ge(S["g3_ready"], 16 * b + 16)
                v.tensor_scalar(at(G3 + 128, [[192, 64], [1, 64]]), at(G3, [[192, 64], [1, 64]]), -1.0, None, mult).then_inc(S["g3_neg"], 1)

            def own_rows(c, first=False):
                for g in range(5):
                    n = 16 if g < 4 else 1
                    dve.wait_ge(S["y3_psum"], 5 * c + g + 1)
                    if not first:
                        dve.wait_ge(S["y3_kept"], 5 * c + g - 4)
                    t = at(TT + 128 * g, [[8, n], [1, 8]])
                    row = lambda e: sb[:, CK + K_ROW + e:CK + K_ROW + e + 1]
                    col = lambda e: pat(g, 8 * e, [[32, n], [1, 8]])
                    v.tensor_scalar(t, col(0), row(0), None, mult).then_inc(S["t_part"], 1)
                    dve.wait_ge(S["t_part"], 15 * c + 3 * g + 1)
                    v.scalar_tensor_tensor(t, col(1), row(1), t, mult, add).then_inc(S["t_part"], 1)
                    dve.wait_ge(S["t_part"], 15 * c + 3 * g + 2)
                    v.scalar_tensor_tensor(t, col(2), row(2), t, mult, add).then_inc(S["t_part"], 1)
                    dve.wait_ge(S["t_part"], 15 * c + 3 * g + 3)
                    v.scalar_tensor_tensor(t, col(3), row(3), t, mult, add).then_inc(S["t_sum"], 1)

            own_rows(0, True)
            with dve.Fori(1, 16) as it:
                own_rows(it)
            for u in range(NU):
                dve.wait_ge(S["o_psum"], u + 1)
                dve.wait_ge(S[f"xo_loaded{u % 4}"], 16 * (u // 4 + 1))
                if u >= 2:
                    dve.wait_ge(S[f"o_stored{u % 2}"], 16 * (u // 2))
                v.tensor_tensor(sb[:, OO + 512 * (u % 2):OO + 512 * (u % 2) + 512], bank[4 + (u + 1) % 2][:, :], sb[:, XO + 512 * (u % 4):XO + 512 * (u % 4) + 512], add).then_inc(S["o_ready"], 1)


def kernel(**inputs):
    import concourse.bacc as _bacc
    from concourse.bass_utils import run_bass_kernel_spmd as _run

    a = {k: np.asarray(v) for k, v in inputs.items()}
    f32 = np.float32
    zero, one = np.zeros(32, f32), np.ones(1, f32)

    def modes(w, columns):
        out = np.zeros((w.shape[0], KY, columns, 2), f32)
        r = w.shape[1] // 2
        out[:, :r, :w.shape[2]], out[:, KY - r:, :w.shape[2]] = w[:, :r], w[:, r:]
        return out

    def flipped(w):
        return w[:, -np.arange(KY) % KY, 0]

    def quarters(w):
        out = np.zeros((NH, 2, 4 * KQ, KY), f32)
        out[:, :, :w.shape[2]] = w.transpose(0, 3, 2, 1)
        return out.reshape(NH, 2, 4, -1).transpose(2, 0, 1, 3).reshape(4 * NH, -1)

    l0 = lambda n: a["L0_conv_" + n]
    l1 = lambda n: a["L1_conv_" + n]
    join = lambda w: np.concatenate([w[0], w[1]], axis=-3)
    layers = [
        dict(q=join(l0("wQ"))[0], k=join(l0("wK"))[0], v=join(l0("wV"))[0], p=join(l0("wP"))[:, 0], m=(join(l0("wM0"))[0], join(l0("wM1"))[0]),
             g=l0("norm_g"), b=l0("norm_b"), one=(l0("wM0s")[0], l0("wM1s")[0], l0("bM0s"), l0("bM1s"), l0("bPs")),
             rows=(l0("bQs"), l0("bKs"), l0("wQs")[:, 0], l0("wKs")[:, 0], l0("wPs")[0], l0("bVs"), l0("wVs")[:, 0])),
        dict(q=l1("Qcw")[0], k=l1("Kcw")[0], v=l1("Vcw")[0], p=l1("Pcw")[:, 0], m=(l1("m0cw")[0], l1("m1cw")[0]),
             g=np.concatenate([l1("norm1_w"), l1("attn_w"), l1("norm2_w"), one, one, l1("mon_w")]),
             b=np.concatenate([l1("norm1_b"), l1("attn_b"), l1("norm2_b"), zero[:2], l1("mon_b")]),
             one=(l1("m0sw")[0], l1("m1sw")[0], zero[:1], zero[:1], zero[:1]),
             rows=(zero, zero, l1("Qsw")[:, 0], l1("Ksw")[:, 0], l1("Psw")[0], zero, l1("Vsw")[:, 0])),
    ]
    prow, vsps, qk, qkf, pw, vw, vf, wm = ([] for _ in range(8))
    for y in layers:
        q, k, v, p = modes(y["q"], KC), modes(y["k"], KC), modes(y["v"], KC), modes(y["p"], KX)
        prow.append(np.concatenate([y["g"], y["b"], *y["one"], zero[:15], *y["rows"], q[:, 0, 0, 0], k[:, 0, 0, 0], p[:, 0, 0, 0]]))
        vsps += [y["rows"][6], y["rows"][4]]
        both = lambda w: np.concatenate([w, w])
        qk.append(both(np.concatenate([w.transpose(1, 3, 2, 0).reshape(KY, -1) for w in (q, k)], axis=1)))
        qkf.append(both(np.concatenate([flipped(w).transpose(1, 2, 0).reshape(KY, -1) for w in (q, k)], axis=1)))
        pw.append(quarters(p))
        vw.append(quarters(v))
        vf.append(flipped(v).transpose(0, 2, 1).reshape(NH, -1))
        wm.append(np.stack([both(modes(w, KX)[0].transpose(0, 2, 1).reshape(KY, -1)) for w in y["m"]]))
    cst, cst3, sel = shape_constants()
    arrays = {"x": a["x"].reshape(NIMG, H, W), "cst": cst, "cst3": cst3, "w3r": a["L3_conv_weight_real"], "w3i": a["L3_conv_weight_imag"],
              "bias": np.tile(a["L2_conv_bias"].reshape(1, T), (1, B)), "taps": np.concatenate([a["L2_conv_up_filter"].reshape(1, -1), a["L2_conv_dn_filter"].reshape(1, -1)], axis=1),
              "sel": sel, "prow": np.stack(prow), "vsps": np.tile(np.stack(vsps, axis=1), (4, 1)), "qk": np.stack(qk),
              "qkf": np.stack(qkf), "pw": np.stack(pw), "vw": np.stack(vw), "vf": np.stack(vf), "wm": np.stack(wm)}
    arrays = {k: np.ascontiguousarray(v) for k, v in arrays.items()}
    nc = _bacc.Bacc("TRN2", target_bir_lowering=False, num_devices=1)
    io = {k: nc.dram_tensor("in_" + k, v.shape, mybir.dt.from_np(v.dtype), kind="ExternalInput").ap() for k, v in arrays.items()}
    io["out"] = nc.dram_tensor("out_0", (NIMG, H, W), mybir.dt.float32, kind="ExternalOutput").ap()
    build(nc, io)
    r = _run(nc, [{"in_" + k: v for k, v in arrays.items()}], core_ids=[0])
    return r.results[0]["out_0"].reshape(B, T, H, W)
```
